# Optimizing a Trainium2 kernel written in Bass

```python
import numpy as np
import jax
import jax.numpy as jnp

def _softmax(x, axis=-1):
    return jax.nn.softmax(x, axis=axis)

def _gelu(x):
    return jax.nn.gelu(x, approximate=True)

def _silu(x):
    return jax.nn.silu(x)

def _sigmoid(x):
    return jax.nn.sigmoid(x)

def _layernorm(x, axis=-1, eps=1e-05):
    m = jnp.mean(x, axis=axis, keepdims=True)
    v = jnp.var(x, axis=axis, keepdims=True)
    return (x - m) / jnp.sqrt(v + eps)

def _scatter_add(tgt, idx, src, axis=0):
    return tgt.at[idx].add(src)

def _segment_sum(src, seg, n):
    return jax.ops.segment_sum(src, seg, n)
kernel_name = 'mk_adaln_d2_jaxref_r8_444a40'

def setup_inputs(seed: int=0):
    np.random.seed(seed)
    _w = jnp.asarray

    def _L0_attn_setup():
        import jax, jax.numpy as jnp
        import numpy as np
        FEATS = 128
        HEAD = 16
        HEAD_DIM = FEATS // HEAD
        EPS = 1e-12

        def _l2norm(t):
            n = jnp.sqrt(jnp.sum(t * t, axis=-1, keepdims=True))
            return t / jnp.maximum(n, EPS)
        key = jax.random.key(seed)
        ks = jax.random.split(key, 10)
        s = 0.02
        inp = {'x': jax.random.normal(ks[0], (4, 256, FEATS), dtype=jnp.float32), 'Wq': jax.random.normal(ks[1], (FEATS, FEATS), dtype=jnp.float32) * s, 'bq': jnp.zeros((FEATS,), dtype=jnp.float32), 'Wk': jax.random.normal(ks[2], (FEATS, FEATS), dtype=jnp.float32) * s, 'bk': jnp.zeros((FEATS,), dtype=jnp.float32), 'Wv': jax.random.normal(ks[3], (FEATS, FEATS), dtype=jnp.float32) * s, 'bv': jnp.zeros((FEATS,), dtype=jnp.float32), 'Wo': jax.random.normal(ks[4], (FEATS, FEATS), dtype=jnp.float32) * s, 'bo': jnp.zeros((FEATS,), dtype=jnp.float32), 'm': jnp.full((HEAD,), 0.5, dtype=jnp.float32)}
        return inp
    _L0_attn_in = _L0_attn_setup()

    def _L0_ffn_setup():
        import jax, jax.numpy as jnp
        import numpy as np
        E = 8
        K = 2
        S = 1
        THRESHOLD = 0.7
        NORM_TOPK = True
        H = 128
        F = 128
        B, SEQ = (2, 128)
        key = jax.random.key(seed)
        k1, k2, k3, k4, k5 = jax.random.split(key, 5)
        hidden_states = jax.random.normal(k1, (B, SEQ, H), jnp.float32)
        gate_weight = jax.random.normal(k2, (E, H), jnp.float32) * 0.02
        gate_up_proj = jax.random.normal(k3, (E, 2 * F, H), jnp.float32) * 0.02
        down_proj = jax.random.normal(k4, (E, H, F), jnp.float32) * 0.02
        sim = jax.random.uniform(k5, (E, E), jnp.float32)
        sim = (sim + sim.T) / 2.0
        sim = sim.at[jnp.arange(E), jnp.arange(E)].set(1.0)
        return {'hidden_states': hidden_states, 'gate_weight': gate_weight, 'gate_up_proj': gate_up_proj, 'down_proj': down_proj, 'similarity_matrix': sim}
    _L0_ffn_in = _L0_ffn_setup()
    _L0_c = _w((lambda *s: np.random.randn(*s).astype(np.float32) * 0.05)(4, 128))
    _L0_wmod = _w((lambda *s: np.random.randn(*s).astype(np.float32) * 0.05)(128, 6 * 128) * 128 ** (-0.5))

    def _L1_attn_setup():
        import jax, jax.numpy as jnp
        import numpy as np
        import math
        N_HEADS = 16
        DIM = 128
        B, S = (2, 256)

        def _split_heads(x, n_heads):
            b, s, d = x.shape
            dh = d // n_heads
            return x.reshape(b, s, n_heads, dh).transpose(0, 2, 1, 3)
        key = jax.random.key(seed)
        ks = jax.random.split(key, 9)
        std = 0.02
        inp = {'query': jax.random.normal(ks[0], (B, S, DIM), dtype=jnp.float32), 'mask': jnp.ones((B, S), dtype=jnp.int64), 'q_w': jax.random.normal(ks[1], (DIM, DIM), dtype=jnp.float32) * std, 'q_b': jnp.zeros((DIM,), dtype=jnp.float32), 'k_w': jax.random.normal(ks[2], (DIM, DIM), dtype=jnp.float32) * std, 'k_b': jnp.zeros((DIM,), dtype=jnp.float32), 'v_w': jax.random.normal(ks[3], (DIM, DIM), dtype=jnp.float32) * std, 'v_b': jnp.zeros((DIM,), dtype=jnp.float32), 'out_w': jax.random.normal(ks[4], (DIM, DIM), dtype=jnp.float32) * std, 'out_b': jnp.zeros((DIM,), dtype=jnp.float32)}
        return inp
    _L1_attn_in = _L1_attn_setup()

    def _L1_ffn_setup():
        import jax, jax.numpy as jnp
        import numpy as np
        B, S, D = (4, 256, 128)
        F = 512
        E = 8
        K = 2
        EPS = 1e-09
        key = jax.random.key(seed)
        ks = jax.random.split(key, 6)
        scale = 0.02
        return {'x': jax.random.normal(ks[0], (B, S, D), dtype=jnp.float32), 'Wg': jax.random.normal(ks[1], (D, E), dtype=jnp.float32) * scale, 'W1': jax.random.normal(ks[2], (E, D, F), dtype=jnp.float32) * scale, 'b1': jnp.zeros((E, F), dtype=jnp.float32), 'W2': jax.random.normal(ks[3], (E, F, D), dtype=jnp.float32) * scale, 'b2': jnp.zeros((E, D), dtype=jnp.float32)}
    _L1_ffn_in = _L1_ffn_setup()
    _L1_c = _w((lambda *s: np.random.randn(*s).astype(np.float32) * 0.05)(4, 128))
    _L1_wmod = _w((lambda *s: np.random.randn(*s).astype(np.float32) * 0.05)(128, 6 * 128) * 128 ** (-0.5))
    _d = {'L0_attn_x': _L0_attn_in['x'], 'L0_attn_Wq': _L0_attn_in['Wq'], 'L0_attn_bq': _L0_attn_in['bq'], 'L0_attn_Wk': _L0_attn_in['Wk'], 'L0_attn_bk': _L0_attn_in['bk'], 'L0_attn_Wv': _L0_attn_in['Wv'], 'L0_attn_bv': _L0_attn_in['bv'], 'L0_attn_Wo': _L0_attn_in['Wo'], 'L0_attn_bo': _L0_attn_in['bo'], 'L0_attn_m': _L0_attn_in['m'], 'L0_ffn_gate_weight': _L0_ffn_in['gate_weight'], 'L0_ffn_gate_up_proj': _L0_ffn_in['gate_up_proj'], 'L0_ffn_down_proj': _L0_ffn_in['down_proj'], 'L0_ffn_similarity_matrix': _L0_ffn_in['similarity_matrix'], 'L0_c': _L0_c, 'L0_wmod': _L0_wmod, 'L1_attn_mask': _L1_attn_in['mask'], 'L1_attn_q_w': _L1_attn_in['q_w'], 'L1_attn_q_b': _L1_attn_in['q_b'], 'L1_attn_k_w': _L1_attn_in['k_w'], 'L1_attn_k_b': _L1_attn_in['k_b'], 'L1_attn_v_w': _L1_attn_in['v_w'], 'L1_attn_v_b': _L1_attn_in['v_b'], 'L1_attn_out_w': _L1_attn_in['out_w'], 'L1_attn_out_b': _L1_attn_in['out_b'], 'L1_ffn_Wg': _L1_ffn_in['Wg'], 'L1_ffn_W1': _L1_ffn_in['W1'], 'L1_ffn_b1': _L1_ffn_in['b1'], 'L1_ffn_W2': _L1_ffn_in['W2'], 'L1_ffn_b2': _L1_ffn_in['b2'], 'L1_c': _L1_c, 'L1_wmod': _L1_wmod}
    _x0 = _d['L0_attn_x']
    _d['L0_attn_x'] = jax.random.normal(jax.random.fold_in(jax.random.key(seed), 1), (4, 1024, 128), dtype=_x0.dtype)
    del _x0
    return _d

def reference(L0_attn_x, L0_attn_Wq, L0_attn_bq, L0_attn_Wk, L0_attn_bk, L0_attn_Wv, L0_attn_bv, L0_attn_Wo, L0_attn_bo, L0_attn_m, L0_ffn_gate_weight, L0_ffn_gate_up_proj, L0_ffn_down_proj, L0_ffn_similarity_matrix, L0_c, L0_wmod, L1_attn_mask, L1_attn_q_w, L1_attn_q_b, L1_attn_k_w, L1_attn_k_b, L1_attn_v_w, L1_attn_v_b, L1_attn_out_w, L1_attn_out_b, L1_ffn_Wg, L1_ffn_W1, L1_ffn_b1, L1_ffn_W2, L1_ffn_b2, L1_c, L1_wmod):

    def _L0_attn_ref(x, Wq, bq, Wk, bk, Wv, bv, Wo, bo, m):
        import jax, jax.numpy as jnp
        import numpy as np
        FEATS = 128
        HEAD = 16
        HEAD_DIM = FEATS // HEAD
        EPS = 1e-12

        def _l2norm(t):
            n = jnp.sqrt(jnp.sum(t * t, axis=-1, keepdims=True))
            return t / jnp.maximum(n, EPS)
        b, n, f = x.shape

        def proj(W, bias):
            y = x @ W + bias
            return y.reshape(b, n, HEAD, HEAD_DIM).transpose(0, 2, 1, 3)
        q = _l2norm(proj(Wq, bq))
        k = _l2norm(proj(Wk, bk))
        v = proj(Wv, bv)
        sim = jnp.einsum('bhid,bhjd->bhij', q, k)
        sigma_m = jax.nn.sigmoid(m).reshape(1, HEAD, 1, 1)
        scaling = jnp.asarray(n, dtype=x.dtype) ** sigma_m
        attn = sim / scaling
        out = jnp.einsum('bhij,bhjd->bhid', attn, v)
        out = out.transpose(0, 2, 1, 3).reshape(b, n, f)
        return out @ Wo + bo

    def _L0_ffn_ref(hidden_states, gate_weight, gate_up_proj, down_proj, similarity_matrix):
        import jax, jax.numpy as jnp
        import numpy as np
        E = 8
        K = 2
        S = 1
        THRESHOLD = 0.7
        NORM_TOPK = True
        H = 128
        F = 128
        B, SEQ = (2, 128)
        b, s, h = hidden_states.shape
        x = hidden_states.reshape(-1, h)
        N = x.shape[0]
        logits = x @ gate_weight.T
        probs = jax.nn.softmax(logits.astype(jnp.float32), axis=-1)
        top_w, top_i = jax.lax.top_k(probs, K)
        if NORM_TOPK:
            top_w = top_w / jnp.clip(jnp.sum(top_w, -1, keepdims=True), 1e-12)
        primary_mask = jnp.zeros((E,), bool).at[top_i[:, :S].reshape(-1)].set(True)
        sim = jnp.where(primary_mask[None, :], similarity_matrix.astype(jnp.float32), -jnp.inf)
        best_j = jnp.argmax(sim, axis=-1)
        best_sim = jnp.max(sim, axis=-1)
        ids = jnp.arange(E)
        expert_map = jnp.where(~primary_mask & (best_sim >= THRESHOLD), best_j, ids)
        rerouted = expert_map[top_i]
        rows = jnp.arange(N)[:, None]
        dense = jnp.zeros((N, E), top_w.dtype).at[rows, rerouted].add(top_w)
        fw, fi = jax.lax.top_k(dense, K)
        combine = jnp.zeros((N, E), fw.dtype).at[rows, fi].add(jnp.where(fw > 0, fw, 0.0))
        gu = jnp.einsum('nh,efh->enf', x, gate_up_proj)
        g, u = jnp.split(gu, 2, axis=-1)
        hmid = jax.nn.silu(g) * u
        y = jnp.einsum('enf,ehf->enh', hmid, down_proj)
        out = jnp.einsum('ne,enh->nh', combine, y)
        return out.reshape(b, s, h)

    def _L1_attn_ref(query, mask, q_w, q_b, k_w, k_b, v_w, v_b, out_w, out_b):
        import jax, jax.numpy as jnp
        import numpy as np
        import math
        N_HEADS = 16
        DIM = 128
        B, S = (2, 256)

        def _split_heads(x, n_heads):
            b, s, d = x.shape
            dh = d // n_heads
            return x.reshape(b, s, n_heads, dh).transpose(0, 2, 1, 3)
        b, s, d = query.shape
        h = N_HEADS
        dh = d // h
        scale = math.sqrt(dh)
        q = _split_heads(query @ q_w.T + q_b, h) / scale
        k = _split_heads(query @ k_w.T + k_b, h)
        v = _split_heads(query @ v_w.T + v_b, h)
        scores = jnp.einsum('bhqd,bhkd->bhqk', q, k)
        attn = jax.nn.softmax(scores.astype(jnp.float32), axis=-1).astype(query.dtype)
        ctx = jnp.einsum('bhqk,bhkd->bhqd', attn, v)
        ctx = ctx.transpose(0, 2, 1, 3).reshape(b, s, d)
        out = ctx @ out_w.T + out_b
        return out

    def _L1_ffn_ref(x, Wg, W1, b1, W2, b2):
        import jax, jax.numpy as jnp
        import numpy as np
        B, S, D = (4, 256, 128)
        F = 512
        E = 8
        K = 2
        EPS = 1e-09
        logits = jnp.einsum('bsd,de->bse', x, Wg)
        P = jax.nn.softmax(logits, axis=-1)
        _, topk_idx = jax.lax.top_k(P, K)
        mask = jax.nn.one_hot(topk_idx, E, dtype=x.dtype).sum(-2)
        P_topk = P * mask
        P_norm = P_topk / (P_topk.sum(axis=-1, keepdims=True) + EPS)
        h = jax.nn.gelu(jnp.einsum('bsd,edf->ebsf', x, W1) + b1[:, None, None, :], approximate=False)
        y_e = jnp.einsum('ebsf,efd->ebsd', h, W2) + b2[:, None, None, :]
        y = jnp.einsum('ebsd,bse->bsd', y_e, P_norm)
        return y
    x = L0_attn_x
    mod = (_silu(L0_c) @ L0_wmod).reshape(L0_c.shape[0], 6, 1, -1)
    sa, ca, ga, sb, cb, gb = (mod[:, 0], mod[:, 1], mod[:, 2], mod[:, 3], mod[:, 4], mod[:, 5])
    ga = (2 * (ga >= 0) - 1) * jnp.maximum(jnp.abs(ga), 0.25)
    gb = (2 * (gb >= 0) - 1) * jnp.maximum(jnp.abs(gb), 0.25)
    h = _layernorm(x, axis=-1) * (1 + ca) + sa
    x = x + ga * _L0_attn_ref(h, L0_attn_Wq, L0_attn_bq, L0_attn_Wk, L0_attn_bk, L0_attn_Wv, L0_attn_bv, L0_attn_Wo, L0_attn_bo, L0_attn_m)
    h = _layernorm(x, axis=-1) * (1 + cb) + sb
    x = x + gb * _L0_ffn_ref(h, L0_ffn_gate_weight, L0_ffn_gate_up_proj, L0_ffn_down_proj, L0_ffn_similarity_matrix)
    mod = (_silu(L1_c) @ L1_wmod).reshape(L1_c.shape[0], 6, 1, -1)
    sa, ca, ga, sb, cb, gb = (mod[:, 0], mod[:, 1], mod[:, 2], mod[:, 3], mod[:, 4], mod[:, 5])
    ga = (2 * (ga >= 0) - 1) * jnp.maximum(jnp.abs(ga), 0.25)
    gb = (2 * (gb >= 0) - 1) * jnp.maximum(jnp.abs(gb), 0.25)
    h = _layernorm(x, axis=-1) * (1 + ca) + sa
    x = x + ga * _L1_attn_ref(h, L1_attn_mask, L1_attn_q_w, L1_attn_q_b, L1_attn_k_w, L1_attn_k_b, L1_attn_v_w, L1_attn_v_b, L1_attn_out_w, L1_attn_out_b)
    h = _layernorm(x, axis=-1) * (1 + cb) + sb
    x = x + gb * _L1_ffn_ref(h, L1_ffn_Wg, L1_ffn_W1, L1_ffn_b1, L1_ffn_W2, L1_ffn_b2)
    return x

_drawn_inputs = setup_inputs


def setup_inputs(seed=0):
    import zlib

    import numpy as np

    out = dict(_drawn_inputs(seed))
    spreads = {'L0_attn_bq': (0.0, 0.8),
     'L0_attn_bk': (0.0, 0.72),
     'L0_attn_bv': (0.0, 0.717),
     'L0_attn_bo': (0.0, 0.321),
     'L0_attn_m': (0.5, 0.6),
     'L1_attn_q_b': (0.0, 0.8),
     'L1_attn_k_b': (0.0, 0.8),
     'L1_attn_v_b': (0.0, 0.8),
     'L1_attn_out_b': (0.0, 0.339),
     'L1_ffn_b1': (0.0, 0.8),
     'L1_ffn_b2': (0.0, 0.441)}
    factors = {'L0_attn_Wq': 4.912,
     'L0_attn_Wk': 8.0,
     'L0_attn_Wv': 8.0,
     'L0_attn_Wo': 4.419,
     'L0_ffn_gate_weight': 8.0,
     'L0_ffn_gate_up_proj': 8.0,
     'L0_ffn_down_proj': 8.0,
     'L1_attn_q_w': 8.0,
     'L1_attn_k_w': 8.0,
     'L1_attn_v_w': 8.0,
     'L1_attn_out_w': 8.0,
     'L1_ffn_Wg': 3.047,
     'L1_ffn_W1': 6.013,
     'L1_ffn_W2': 5.427}
    for name, (base, spread) in spreads.items():
        noise = np.random.default_rng([zlib.crc32(name.encode()), seed]).standard_normal(out[name].shape)
        drawn = base * np.exp(spread * noise) if base else spread * noise
        out[name] = jnp.asarray(drawn.astype(out[name].dtype))
    for name, factor in factors.items():
        out[name] = (out[name] * factor).astype(out[name].dtype)
    return out
```

```python
import math
from contextlib import ExitStack

import concourse.bass as bass
from concourse import mybir

ALU = mybir.AluOpType
ACT = mybir.ActivationFunctionType
AX_X = mybir.AxisListType.X
F32 = mybir.dt.float32
BF16 = mybir.dt.bfloat16
U32 = mybir.dt.uint32

P = 128
B, S, D = 4, 1024, 128
H, DH = 16, 8
E = 8
F1 = 512
FC = F1 // P
N = B * S
T = N // P
GT = 4
GN = GT * P
G = T // GT
BG = S // GN
LN_EPS = 1e-5
SIM_MIN = 0.7
NEG = 3.0e38
QUADS = H // 4
TERMS = 6
SLOT = TERMS * DH
Q_PARTS = (0, 0, 0, 1, 1, 2)
K_PARTS = (0, 1, 2, 0, 1, 0)
SROWS = SLOT + 3
KT = S // P
HQ = GN // 2
HALVES = B * QUADS * 2
CYCLE = QUADS * 2
TOPS = GT * 4 * 2
ds = bass.ds


class Chain:

    def __init__(self, eng, sem, base=0):
        self.eng, self.sem, self.base, self.n = eng, sem, base, 0

    def add(self, ins):
        ins.then_inc(self.sem, 1)
        self.n += 1

    def wait(self):
        self.eng.wait_ge(self.sem, self.base + self.n)

    def link(self, ins):
        self.add(ins)
        self.wait()


def wait_pos(eng, sem, value):
    if not (isinstance(value, int) and value <= 0):
        eng.wait_ge(sem, value)


class Kernel:

    def __init__(self, nc, ctx, ins, out):
        self.nc, self.ctx, self.ins, self.out = nc, ctx, ins, out
        self.X = self.sb("X", [P, T, D])
        self.HT = self.sb("HT", [P, N])
        self.MV = self.sb("MV", [P, T, 2])
        self.bstats = self.sb("bstats", [P, GT, 6])
        self.std = self.sb("std", [P, T])
        self.rstd = self.sb("rstd", [P, T])
        self.nmr = self.sb("nmr", [P, T])
        self.xn = self.sb("xn", [P, 2, GN])
        self.hT = self.sb("hT", [P, 2, GN])
        self.mv4 = self.sb("mv4", [P, GT, 2])
        self.kvmask = self.sb("kvmask", [P, P])
        self.mark = self.sb("mark", [P, 1])
        self.gated = self.sb("gated", [P, GT, D])
        self.ident = self.sb("ident", [P, P])
        self.identb = self.sb("identb", [P, P], BF16)
        self.ones = self.sb("ones", [P, P])
        self.rank = self.sb("rank", [P, E])
        self.eye8 = self.sb("eye8", [P, E, E])
        self.modv = self.sb("modv", [P, 2, 4, B])
        self.gate_row = self.sb("gate_row", [P, 2, B, 2, D])
        self.wts = self.sb("wts", [P, T, E])

    def sb(self, name, shape, dt=F32):
        return self.ctx.enter_context(self.nc.sbuf_tensor(name, shape, dt))

    def sem(self, name):
        return self.ctx.enter_context(self.nc.semaphore(name))

    def sems(self, tag, names):
        return [self.sem(f"{tag}_{n}") for n in names.split()]

    def stats(self, chain, tile0, x=None):
        nc = self.nc
        for t in range(GT):
            chain.add(nc.vector.bn_stats(self.bstats[:, t, :], self.X[:, tile0 + t, :] if x is None else x[:, t, :]))
        chain.wait()
        if x is not None:
            nc.vector.memset(self.mark[:], 0.0)
        for t in range(GT):
            chain.add(nc.vector.bn_aggr(self.MV[:, tile0 + t, :] if x is None else self.mv4[:, t, :], self.bstats[:, t, :]))
        if x is not None:
            chain.wait()
            chain.link(nc.vector.tensor_scalar(self.MV[:, ds(tile0, GT), :], self.mv4[:], 1.0, None, ALU.mult))

    def norm_dve(self, dve, chain, s_var, s_std):
        nc = self.nc
        nc.vector.tensor_scalar(self.std[:], self.MV[:, :, 1], LN_EPS, None, ALU.add).then_inc(s_var, 1)
        dve.wait_ge(s_std, 1)
        chain.link(nc.vector.reciprocal(self.rstd[:], self.std[:]))
        chain.link(nc.vector.scalar_tensor_tensor(out=self.nmr[:], in0=self.MV[:, :, 0], scalar=-1.0, in1=self.rstd[:],
                                                  op0=ALU.mult, op1=ALU.mult))

    def norm_act(self, act, s_var, s_std):
        act.wait_ge(s_var, 1)
        self.nc.scalar.activation(self.std[:], self.std[:], ACT.Sqrt).then_inc(s_std, 1)

    def normalise(self, tile, t, slot):
        return self.nc.vector.tensor_scalar(self.xn[:, slot, t * P:(t + 1) * P], self.X[:, tile, :], self.rstd[:, tile:tile + 1],
                                            self.nmr[:, tile:tile + 1], ALU.mult, ALU.add)

    def transpose_group(self, dst, slot):
        for t in range(GT):
            last = self.nc.tensor.transpose(dst[:, t * P:(t + 1) * P], self.xn[:, slot, t * P:(t + 1) * P], self.ident[:])
        return last

    def modulate(self, dst, src, layer, which, b):
        return self.nc.scalar.activation(dst, src, ACT.Identity, scale=self.modv[:, layer, 2 * which + 1, ds(b, 1)],
                                         bias=self.modv[:, layer, 2 * which, ds(b, 1)])

    def gate(self, y, layer, which, b):
        g = self.gate_row[:, layer, ds(b, 1), which, :].broadcast_to([P, GT, D])
        return self.nc.vector.tensor_tensor(self.gated[:], y, g, ALU.mult)

    def add_gated(self, tile0):
        x = self.X[:, ds(tile0, GT), :]
        return self.nc.vector.tensor_tensor(x, x, self.gated[:], ALU.add)


def psum(nc, stack, name, n, cols=512):
    return [stack.enter_context(nc.psum_tensor(f"{name}{i}", [P, cols], F32)) for i in range(n)]


def row_of(ap, n):
    return bass.AP(ap.tensor, 0, [[0, P], [1, n]])


def phase_setup(k, bufs):
    nc, ins = k.nc, k.ins
    s_load, s_chain, s_silu, s_spread, s_sig, s_mod, s_zero = k.sems("set", "load chain silu spread sig mod zero")
    Q, K, Vs, zero_rows = bufs
    with ExitStack() as ph:
        def tmp(name, shape):
            return ph.enter_context(nc.sbuf_tensor(name, shape, F32))
        wmod = [tmp(f"wmod{i}", [P, 6 * D]) for i in range(2)]
        cT, cs, cspread = tmp("cT", [P, 2, B]), tmp("cs", [P, 2, B]), tmp("cspread", [P, 2 * B, P])
        headmask, m_col, m_sig, sign, size = tmp("headmask", [P, P]), tmp("m_col", [P, 1]), tmp("m_sig", [P, 2]), tmp("sign", [P, 512]), tmp("size", [P, 512])
        p_col = psum(nc, ph, "p_col", 1)[0]
        p_row = psum(nc, ph, "p_row", 4)
        consts = ins["consts"]
        loads = [(cT[:, 0, :], ins["L0_cT"]), (cT[:, 1, :], ins["L1_cT"]),
                 (wmod[0][:], ins["L0_wmod"]), (wmod[1][:], ins["L1_wmod"]),
                 (k.ident[:], consts[:, 0:P]), (headmask[:], consts[:, P:2 * P]), (k.rank[:], consts[:, 2 * P:2 * P + E]),
                 (k.eye8[:], consts[:, 2 * P + E:2 * P + E + E * E].rearrange("p (i j) -> p i j", i=E)),
                 (m_col[:], bass.AP(ins["L0_attn_m"].tensor, 0, [[1, H], [0, DH], [1, 1]]))]
        xv = ins["L0_attn_x"].rearrange("b (t p) d -> p (b t) d", p=P)
        loads += [(k.X[:, g * GT:(g + 1) * GT, :], xv[:, g * GT:(g + 1) * GT, :]) for g in range(G)]
        with nc.Block() as block:
            @block.sync
            def _(sp):
                for dst, src in loads:
                    sp.dma_start(dst, src).then_inc(s_load, 16)

            @block.gpsimd
            def _(pool):
                chain = Chain(pool, s_zero)
                chain.link(nc.gpsimd.memset(K[:].bitcast(U32), 0))
                chain.link(nc.gpsimd.memset(Q[:].bitcast(U32), 0))
                chain.link(nc.gpsimd.memset(zero_rows[:].bitcast(U32), 0))
                chain.link(nc.gpsimd.memset(Vs[:], 1.0))
                for par in range(2):
                    chain.link(nc.gpsimd.memset(K[64 * par + 32:64 * par + 64, :, :, par, :], -1.0))

            @block.scalar
            def _(act):
                act.wait_ge(s_load, 16 * len(loads))
                nc.scalar.activation(m_sig[:, 0:1], m_col[:], ACT.Sigmoid).then_inc(s_sig, 1)
                nc.scalar.activation(cs[:], cT[:], ACT.Silu).then_inc(s_silu, 1)
                act.wait_ge(s_sig, 1)
                nc.scalar.activation(m_sig[:, 1:2], m_sig[:, 0:1], ACT.Exp, scale=-math.log(S)).then_inc(s_sig, 1)

            @block.tensor
            def _(pe):
                pe.wait_ge(s_silu, 1)
                for layer in range(2):
                    for i, j in enumerate((0, 1, 3, 4)):
                        at = (layer * 4 + i) * B
                        nc.tensor.matmul(p_col[:, at:at + B], wmod[layer][:, j * D:(j + 1) * D], cs[:, layer, :], start=True, stop=True)
                pe.wait_ge(s_spread, 1)
                for layer in range(2):
                    for b in range(B):
                        for i, j in enumerate((2, 5)):
                            at = (b % 2) * 2 * D + i * D
                            last = nc.tensor.matmul(p_row[layer * 2 + b // 2][:, at:at + D], cspread[:, layer * B + b, :],
                                                    wmod[layer][:, j * D:(j + 1) * D], start=True, stop=True)
                last.then_inc(s_mod, 1)

            @block.vector
            def _(dve):
                chain = Chain(dve, s_chain)
                chain.add(nc.vector.memset(k.ones[:], 1.0))
                dve.wait_ge(s_load, 16 * len(loads))
                chain.add(nc.vector.tensor_copy(k.identb[:], k.ident[:]))
                dve.wait_ge(s_silu, 1)
                nc.vector.tensor_copy(cspread[:], cs[:].rearrange("p l b -> p (l b)").unsqueeze(2).broadcast_to([P, 2 * B, P])).then_inc(s_spread, 1)
                for g in range(G):
                    chain.wait()
                    k.stats(chain, g * GT)
                dve.wait_ge(s_sig, 2)
                chain.add(nc.vector.tensor_scalar(k.kvmask[:], headmask[:], m_sig[:, 1:2], None, ALU.mult))
                dve.wait_ge(s_mod, 1)
                chain.link(nc.vector.tensor_copy(k.modv[:].rearrange("p l k b -> p (l k b)"), p_col[:, 0:2 * 4 * B]))
                for layer in range(2):
                    for i in (1, 3):
                        chain.add(nc.vector.tensor_scalar(k.modv[:, layer, i, :], k.modv[:, layer, i, :], 1.0, None, ALU.add))
                for i in range(4):
                    row = k.gate_row[:, i // 2, (i % 2) * 2:(i % 2) * 2 + 2, :, :].rearrange("p b k d -> p (b k d)")
                    chain.link(nc.vector.tensor_copy(row, p_row[i][:, :]))
                    chain.link(nc.vector.tensor_scalar(sign[:], row, 0.0, 2.0, ALU.is_ge, ALU.mult))
                    chain.link(nc.vector.scalar_tensor_tensor(out=size[:], in0=row, scalar=-1.0, in1=row, op0=ALU.mult, op1=ALU.max))
                    chain.link(nc.vector.tensor_scalar(size[:], size[:], 0.25, None, ALU.max))
                    chain.link(nc.vector.scalar_tensor_tensor(out=row, in0=sign[:], scalar=-1.0, in1=size[:], op0=ALU.add, op1=ALU.mult))


def phase_linear_attention(k):
    nc, ins = k.nc, k.ins
    s_w, s_var, s_std, s_chain, s_xn, s_xT, s_hT, s_qkv, s_biased, s_sq, s_sum, s_root, s_unit = k.sems(
        "la", "w var std chain xn xT hT qkv biased sq sum root unit")
    s_kv, s_kvT, s_g, s_gm, s_qT, s_qTs, s_o, s_gated = k.sems("la2", "kv kvT g gm qT qTs o gated")
    with ExitStack() as ph:
        def tmp(name, shape):
            return ph.enter_context(nc.sbuf_tensor(name, shape, F32))
        w_qkv, b_qkv, w_o, b_o = tmp("w_qkv", [P, 3 * D]), tmp("b_qkv", [P, 3 * D]), tmp("w_o", [P, D]), tmp("b_o", [1, D])
        qkv = tmp("qkv", [P, BG, GT, 3 * D])
        sq, norm, inv = tmp("sq", [P, GT, 2 * D]), tmp("norm", [P, GT * 2 * H]), tmp("inv", [P, GT * 2 * H])
        qT, kvT, kvo = tmp("qT", [P, S]), tmp("kvT", [P, P]), tmp("kvo", [P, P])
        p_x = psum(nc, ph, "p_x", 1)[0]
        p_qkv = psum(nc, ph, "p_qkv", 3)
        p_kv, p_kvo, p_qT, p_o = (psum(nc, ph, n, 1)[0] for n in ("p_kv", "p_kvo", "p_qT", "p_o"))
        loads = [(w_qkv[:, i * D:(i + 1) * D], ins[f"L0_attn_W{n}"]) for i, n in enumerate("qkv")]
        loads += [(b_qkv[:, i * D:(i + 1) * D], row_of(ins[f"L0_attn_b{n}"], D)) for i, n in enumerate("qkv")]
        loads += [(w_o[:], ins["L0_attn_Wo"]), (b_o[:], ins["L0_attn_bo"].unsqueeze(0))]
        with nc.Block() as block:
            @block.sync
            def _(sp):
                for dst, src in loads:
                    sp.dma_start(dst, src).then_inc(s_w, 16)

            @block.scalar
            def _(act):
                k.norm_act(act, s_var, s_std)
                for b in range(B):
                    for j in range(BG):
                        g = b * BG + j
                        act.wait_ge(s_xT, g + 1)
                        k.modulate(k.hT[:, j, :], p_x[:, :], 0, 0, b).then_inc(s_hT, 1)
                        act.wait_ge(s_biased, (g + 1) * GT)
                        nc.scalar.activation(sq[:], qkv[:, j, :, 0:2 * D], ACT.Square).then_inc(s_sq, 1)
                        act.wait_ge(s_sum, g + 1)
                        nc.scalar.activation(norm[:], norm[:], ACT.Sqrt).then_inc(s_root, 1)
                        act.wait_ge(s_qT, g + 1)
                        nc.scalar.activation(qT[:, j * GN:(j + 1) * GN], p_qT[:, :], ACT.Copy).then_inc(s_qTs, 1)

            @block.tensor
            def _(pe):
                pe.wait_ge(s_w, 16 * len(loads))
                for b in range(B):
                    for j in range(BG):
                        g = b * BG + j
                        pe.wait_ge(s_xn, g + 1)
                        k.transpose_group(p_x, j).then_inc(s_xT, 1)
                        pe.wait_ge(s_hT, g + 1)
                        for t in range(GT):
                            if t == 3:
                                pe.wait_ge(s_biased, g * GT + 1)
                            nc.tensor.matmul(p_qkv[t % 3][:, 0:3 * D], k.hT[:, j, t * P:(t + 1) * P], w_qkv[:],
                                             start=True, stop=True).then_inc(s_qkv, 1)
                        pe.wait_ge(s_unit, g + 1)
                        for t in range(GT):
                            last = nc.tensor.matmul(p_kv[:, 0:P], qkv[:, j, t, 2 * D:3 * D], qkv[:, j, t, D:2 * D],
                                                    start=(j == 0 and t == 0), stop=(j == BG - 1 and t == GT - 1))
                        last.then_inc(s_kv, 1)
                        for t in range(GT):
                            last = nc.tensor.transpose(p_qT[:, t * P:(t + 1) * P], qkv[:, j, t, 0:D], k.ident[:])
                        last.then_inc(s_qT, 1)
                    pe.wait_ge(s_kvT, b + 1)
                    nc.tensor.matmul(p_kvo[:, 0:D], kvT[:], w_o[:], start=True, stop=True).then_inc(s_g, 1)
                    pe.wait_ge(s_gm, b + 1)
                    for j in range(BG):
                        g = b * BG + j
                        pe.wait_ge(s_qTs, g + 1)
                        if j:
                            pe.wait_ge(s_gated, g)
                        for t in range(GT):
                            o = p_o[:, t * D:(t + 1) * D]
                            nc.tensor.matmul(o, k.ones[0:1, :], b_o[:], start=True, stop=False)
                            last = nc.tensor.matmul(o, qT[:, (j * GT + t) * P:(j * GT + t + 1) * P], kvo[:], start=False, stop=True)
                        last.then_inc(s_o, 1)

            @block.vector
            def _(dve):
                chain = Chain(dve, s_chain)
                k.norm_dve(dve, chain, s_var, s_std)
                before, steps = chain.n, BG * (2 + 1 + 2 * GT)
                dve.wait_ge(s_w, 16 * len(loads))
                for b in range(B):
                    chain = Chain(dve, s_chain, before + b * steps)
                    for j in range(BG):
                        g = b * BG + j
                        for t in range(GT):
                            last = k.normalise(g * GT + t, t, j)
                        last.then_inc(s_xn, 1)
                        for t in range(GT):
                            dve.wait_ge(s_qkv, g * GT + t + 1)
                            nc.vector.tensor_tensor(qkv[:, j, t, :], p_qkv[t % 3][:, 0:3 * D], b_qkv[:], ALU.add).then_inc(s_biased, 1)
                        dve.wait_ge(s_sq, g + 1)
                        nc.vector.tensor_reduce(norm[:], sq[:].rearrange("p t (h d) -> p (t h) d", d=DH), AX_X, ALU.add).then_inc(s_sum, 1)
                        dve.wait_ge(s_root, g + 1)
                        chain.link(nc.vector.tensor_scalar(inv[:], norm[:], 1e-12, None, ALU.max))
                        chain.link(nc.vector.reciprocal(inv[:], inv[:]))
                        qk = qkv[:, j, :, 0:2 * D].rearrange("p t (h d) -> p t h d", d=DH)
                        iv = inv[:].rearrange("p (t h) -> p t h", t=GT).unsqueeze(3).broadcast_to([P, GT, 2 * H, DH])
                        nc.vector.tensor_tensor(qk, qk, iv, ALU.mult).then_inc(s_unit, 1)
                    dve.wait_ge(s_kv, (b + 1) * BG)
                    nc.vector.tensor_tensor(kvT[:], p_kv[:, 0:P], k.kvmask[:], ALU.mult).then_inc(s_kvT, 1)
                    dve.wait_ge(s_g, b + 1)
                    nc.vector.tensor_copy(kvo[:], p_kvo[:, 0:D]).then_inc(s_gm, 1)
                    for j in range(BG):
                        g = b * BG + j
                        dve.wait_ge(s_o, g + 1)
                        k.gate(p_o[:, :].rearrange("p (t d) -> p t d", t=GT), 0, 0, b).then_inc(s_gated, 1)
                        dve.wait_ge(s_gated, g + 1)
                        chain.link(k.add_gated(g * GT))
                        k.stats(chain, g * GT)
                        chain.wait()
                    assert chain.n == steps, chain.n


def top_two(k, dve, chain, act_sems, scr, guard):
    nc = k.nc
    s_shift, s_exp = act_sems
    p, first, second, cand, v1, v2, r = (scr[n] for n in ("p", "first", "second", "cand", "v1", "v2", "r"))

    def wide(v):
        return v[:].unsqueeze(2).broadcast_to([P, T, E])

    rank = k.rank[:].unsqueeze(1).broadcast_to([P, T, E])
    chain.link(nc.vector.tensor_reduce(v1[:], p[:], AX_X, ALU.max))
    nc.vector.tensor_tensor(p[:], p[:], wide(v1), ALU.subtract).then_inc(s_shift, 1)
    dve.wait_ge(s_exp, 1)
    chain.link(nc.vector.tensor_reduce(v1[:], p[:], AX_X, ALU.add))
    chain.link(nc.vector.reciprocal(v1[:], v1[:]))
    chain.link(nc.vector.tensor_tensor(p[:], p[:], wide(v1), ALU.mult))
    for v, mask in ((v1, first), (v2, second)):
        chain.link(nc.vector.tensor_reduce(v[:], p[:], AX_X, ALU.max))
        chain.link(nc.vector.tensor_tensor(cand[:], p[:], wide(v), ALU.is_equal))
        chain.link(nc.vector.tensor_tensor(cand[:], cand[:], rank, ALU.mult))
        chain.link(nc.vector.tensor_reduce(r[:], cand[:], AX_X, ALU.max))
        chain.link(nc.vector.tensor_tensor(mask[:], wide(r), rank, ALU.is_equal))
        if v is v1:
            chain.link(nc.vector.scalar_tensor_tensor(out=p[:], in0=mask[:], scalar=-4.0, in1=p[:], op0=ALU.mult, op1=ALU.add))
    chain.link(nc.vector.tensor_tensor(r[:], v1[:], v2[:], ALU.add))
    chain.link(nc.vector.tensor_scalar(r[:], r[:], guard[1], None, guard[0]))
    chain.link(nc.vector.reciprocal(r[:], r[:]))
    chain.link(nc.vector.tensor_tensor(v1[:], v1[:], r[:], ALU.mult))
    chain.link(nc.vector.tensor_tensor(v2[:], v2[:], r[:], ALU.mult))
    chain.link(nc.vector.tensor_tensor(cand[:], first[:], wide(v1), ALU.mult))
    chain.link(nc.vector.tensor_tensor(k.wts[:], second[:], wide(v2), ALU.mult))
    chain.link(nc.vector.tensor_tensor(k.wts[:], k.wts[:], cand[:], ALU.add))


def phase_gating(k, layer, w_name, guard, loads):
    nc, ins = k.nc, k.ins
    tag = f"g{layer}"
    s_w, s_var, s_std, s_chain, s_xn, s_xT, s_hT, s_logit, s_shift, s_exp, s_prim = k.sems(
        tag, "w var std chain xn xT hT logit shift exp prim")
    with ExitStack() as ph:
        def tmp(name, shape):
            return ph.enter_context(nc.sbuf_tensor(f"{tag}_{name}", shape, F32))
        w_gate = tmp("w_gate", [P, E])
        scr = {n: tmp(n, [P, T, E]) for n in ("p", "first", "second", "cand")}
        scr |= {n: tmp(n, [P, T]) for n in ("v1", "v2", "r")}
        p_x = psum(nc, ph, f"{tag}_px", 2)
        p_l = psum(nc, ph, f"{tag}_pl", 1)[0]
        p_c = psum(nc, ph, f"{tag}_pc", 1)[0]
        mine = [(w_gate[:], ins[w_name])]
        if layer == 0:
            sim = tmp("sim", [P, E, E])
            used, prim, best, move = tmp("used", [P, E]), tmp("prim", [P, E]), tmp("best", [P, E]), tmp("move", [P, E])
            eq, far = tmp("eq", [P, E, E]), tmp("far", [P, E])
            route, routeT = tmp("route", [P, E, E]), tmp("routeT", [P, E, E])
            spread = tmp("spread", [P, T, E, E])
            mine.append((sim[:], bass.AP(ins["L0_ffn_similarity_matrix"].tensor, 0, [[0, P], [E, E], [1, E]])))
        with nc.Block() as block:
            @block.sync
            def _(sp):
                for dst, src in mine:
                    sp.dma_start(dst, src).then_inc(s_w, 16)
                for dst, src, s in loads:
                    sp.dma_start(dst, src).then_inc(s, 16)

            @block.scalar
            def _(act):
                k.norm_act(act, s_var, s_std)
                for g in range(G):
                    act.wait_ge(s_xT, g + 1)
                    k.modulate(k.HT[:, g * GN:(g + 1) * GN], p_x[g % 2][:, :], layer, 1, g // BG).then_inc(s_hT, 1)
                act.wait_ge(s_shift, 1)
                nc.scalar.activation(scr["p"][:], scr["p"][:], ACT.Exp).then_inc(s_exp, 1)

            @block.tensor
            def _(pe):
                pe.wait_ge(s_w, 16 * len(mine))

                def logits(g):
                    pe.wait_ge(s_hT, g + 1)
                    for t in range(g * GT, (g + 1) * GT):
                        last = nc.tensor.matmul(p_l[:, t * E:(t + 1) * E], k.HT[:, t * P:(t + 1) * P], w_gate[:], start=True, stop=True)
                    last.then_inc(s_logit, 1)

                for g in range(G):
                    pe.wait_ge(s_xn, g + 1)
                    wait_pos(pe, s_hT, g - 1)
                    k.transpose_group(p_x[g % 2], g % 2).then_inc(s_xT, 1)
                    if g:
                        logits(g - 1)
                logits(G - 1)
                if layer == 0:
                    pe.wait_ge(s_prim, 1)
                    nc.tensor.matmul(p_c[:, 0:E], k.ones[:], used[:], start=True, stop=True).then_inc(s_prim, 1)

            @block.vector
            def _(dve):
                chain = Chain(dve, s_chain)
                k.norm_dve(dve, chain, s_var, s_std)
                for g in range(G):
                    wait_pos(dve, s_xT, g - 1)
                    for t in range(GT):
                        last = k.normalise(g * GT + t, t, g % 2)
                    last.then_inc(s_xn, 1)
                dve.wait_ge(s_logit, G)
                chain.link(nc.vector.tensor_copy(scr["p"][:], p_l[:, 0:T * E].rearrange("p (t e) -> p t e", e=E)))
                top_two(k, dve, chain, (s_shift, s_exp), scr, guard)
                if layer:
                    return
                chain.wait()
                nc.vector.tensor_reduce(used[:], scr["first"][:].rearrange("p t e -> p e t"), AX_X, ALU.max).then_inc(s_prim, 1)
                dve.wait_ge(s_prim, 2)
                chain.link(nc.vector.tensor_scalar(prim[:], p_c[:, 0:E], 0.5, None, ALU.is_gt))
                chain.link(nc.vector.tensor_scalar(far[:], prim[:], -1.0, NEG, ALU.add, ALU.mult))
                dve.wait_ge(s_w, 16 * len(mine))
                columns = prim[:].unsqueeze(1).broadcast_to([P, E, E])
                chain.link(nc.vector.tensor_tensor(sim[:], sim[:], columns, ALU.mult))
                chain.link(nc.vector.tensor_tensor(sim[:], sim[:], far[:].unsqueeze(1).broadcast_to([P, E, E]), ALU.add))
                chain.link(nc.vector.tensor_reduce(best[:], sim[:], AX_X, ALU.max))
                rank = k.rank[:].unsqueeze(1).broadcast_to([P, E, E])
                chain.link(nc.vector.tensor_tensor(eq[:], sim[:], best[:].unsqueeze(2).broadcast_to([P, E, E]), ALU.is_equal))
                chain.link(nc.vector.tensor_tensor(eq[:], eq[:], rank, ALU.mult))
                chain.link(nc.vector.tensor_reduce(far[:], eq[:], AX_X, ALU.max))
                chain.link(nc.vector.tensor_tensor(route[:], far[:].unsqueeze(2).broadcast_to([P, E, E]), rank, ALU.is_equal))
                chain.link(nc.vector.tensor_scalar(move[:], best[:], SIM_MIN, None, ALU.is_ge))
                chain.link(nc.vector.tensor_scalar(prim[:], prim[:], -1.0, 1.0, ALU.mult, ALU.add))
                chain.link(nc.vector.tensor_tensor(move[:], move[:], prim[:], ALU.mult))
                chain.link(nc.vector.tensor_tensor(route[:], route[:], k.eye8[:], ALU.subtract))
                chain.link(nc.vector.tensor_tensor(route[:], route[:], move[:].unsqueeze(2).broadcast_to([P, E, E]), ALU.mult))
                chain.link(nc.vector.tensor_tensor(route[:], route[:], k.eye8[:], ALU.add))
                chain.link(nc.vector.tensor_copy(routeT[:], route[:].rearrange("p i j -> p j i")))
                chain.link(nc.vector.tensor_tensor(spread[:], k.wts[:].unsqueeze(2).broadcast_to([P, T, E, E]),
                                                   routeT[:].unsqueeze(1).broadcast_to([P, T, E, E]), ALU.mult))
                chain.link(nc.vector.tensor_reduce(k.wts[:], spread[:], AX_X, ALU.add))


def phase_experts0(k, w_gu, w_down, s_weights):
    nc = k.nc
    s_chain, s_gu, s_silu, s_mid, s_y, s_acc = k.sems("x0", "chain gu silu mid y acc")
    with ExitStack() as ph:
        def tmp(name, shape):
            return ph.enter_context(nc.sbuf_tensor(name, shape, F32))
        gate_s, mid, acc = tmp("gate_s", [P, 2, GN]), tmp("mid", [P, 2, GN]), tmp("acc0", [P, GT, D])
        p_g, p_u, p_y = psum(nc, ph, "p_g", 2), psum(nc, ph, "p_u", 2), psum(nc, ph, "p_y", 2)
        with nc.Block() as block:
            @block.scalar
            def _(act):
                with act.Fori(0, B) as b:
                    for j in range(BG):
                        for e in range(E):
                            n = (b * BG + j) * E + e
                            act.wait_ge(s_gu, n + 1)
                            nc.scalar.activation(gate_s[:, e % 2, :], p_g[e % 2][:, :], ACT.Silu).then_inc(s_silu, 1)

            @block.tensor
            def _(pe):
                def project(g, e):
                    rhs = k.HT[:, ds(g * GN, GN)]
                    nc.tensor.matmul(p_g[e % 2][:, :], w_gu[:, e, 0:P], rhs, start=True, stop=True)
                    nc.tensor.matmul(p_u[e % 2][:, :], w_gu[:, e, P:2 * P], rhs, start=True, stop=True).then_inc(s_gu, 1)

                def down(g, e):
                    n = g * E + e
                    pe.wait_ge(s_mid, n + 1)
                    pe.wait_ge(s_acc, n + 1)
                    for t in range(GT):
                        last = nc.tensor.matmul(p_y[e % 2][:, t * D:(t + 1) * D], mid[:, e % 2, t * P:(t + 1) * P], w_down[:, e, :],
                                                start=True, stop=True)
                    last.then_inc(s_y, 1)

                pe.wait_ge(s_weights, 32)
                with pe.Fori(0, B) as b:
                    for j in range(BG):
                        g = b * BG + j
                        project(g, 0)
                        for e in range(1, E):
                            project(g, e)
                            down(g, e - 1)
                        down(g, E - 1)

            @block.vector
            def _(dve):
                def middle(g, e):
                    dve.wait_ge(s_silu, g * E + e + 1)
                    nc.vector.tensor_tensor(mid[:, e % 2, :], gate_s[:, e % 2, :], p_u[e % 2][:, :], ALU.mult).then_inc(s_mid, 1)

                def accumulate(g, e):
                    n = g * E + e
                    dve.wait_ge(s_y, n + 1)
                    dve.wait_ge(s_acc, n + 2)
                    for t in range(GT):
                        w, y = k.wts[:, ds(g * GT + t, 1), e], p_y[e % 2][:, t * D:(t + 1) * D]
                        if e == 0:
                            last = nc.vector.tensor_scalar(acc[:, t, :], y, w, None, ALU.mult)
                        else:
                            last = nc.vector.scalar_tensor_tensor(out=acc[:, t, :], in0=y, scalar=w, in1=acc[:, t, :],
                                                                  op0=ALU.mult, op1=ALU.add)
                    last.then_inc(s_acc, 1)

                nc.vector.memset(k.gated[:, 0, 0:1], 0.0).then_inc(s_acc, 2)
                steps = BG * (4 + 2 * GT)
                with dve.Fori(0, B) as b:
                    chain = Chain(dve, s_chain, b * steps)
                    for j in range(BG):
                        g = b * BG + j
                        middle(g, 0)
                        for e in range(1, E):
                            middle(g, e)
                            accumulate(g, e - 1)
                        accumulate(g, E - 1)
                        dve.wait_ge(s_acc, (g + 1) * E + 2)
                        chain.link(k.gate(acc[:], 0, 1, b))
                        chain.link(k.add_gated(g * GT))
                        chain.link(nc.vector.tensor_scalar(acc[:], k.X[:, ds(g * GT, GT), :], 1.0, None, ALU.mult))
                        k.stats(chain, g * GT, acc)
                    assert chain.n == steps, chain.n


def phase_qkv(k, V, q_dram, k_dram):
    nc, ins = k.nc, k.ins
    s_w, s_var, s_std, s_chain, s_xn, s_xT, s_hT, s_proj, s_sb, s_v, s_vs, s_split, s_store = k.sems(
        "qkv", "w var std chain xn xT hT proj sb v vs split store")
    with ExitStack() as ph:
        def tmp(name, shape, dt=F32):
            return ph.enter_context(nc.sbuf_tensor(name, shape, dt))
        w = {n: tmp(f"w_{n}", [P, D]) for n in "qkv"}
        bias = tmp("bias_qk", [P, 2])
        b_v = tmp("b_v", [P, D])
        full = tmp("full", [P, 2, 2, GN])
        part = tmp("part", [P, 2, 2, 3, GN], BF16)
        p_x = psum(nc, ph, "q_px", 2)
        p_q, p_k, p_v = psum(nc, ph, "p_q", 2), psum(nc, ph, "p_k", 2), psum(nc, ph, "p_v", 2)
        loads = [(w[n][:], ins[f"L1_attn_{n}_wT"]) for n in "qkv"]
        loads += [(bias[:, i:i + 1], ins[f"L1_attn_{n}_b"].unsqueeze(1)) for i, n in enumerate("qk")]
        loads += [(b_v[:], row_of(ins["L1_attn_v_b"], D))]
        scale = 1.0 / math.sqrt(DH)
        stores = 2 * TERMS * 16
        FREE = 2 * 2
        with nc.Block() as block:
            @block.sync
            def _(sp):
                for dst, src in loads:
                    sp.dma_start(dst, src).then_inc(s_w, 16)
                for b in range(B):
                    for j in range(BG):
                        g = b * BG + j
                        for i, (dram, order) in enumerate(((q_dram, Q_PARTS), (k_dram, K_PARTS))):
                            sp.wait_ge(s_split, FREE + 2 * g + i + 1)
                            for t, part_of in enumerate(order):
                                sp.dma_start(dram[t][:, ds(g * GN, GN)], part[:, j, i, part_of, :]).then_inc(s_store, 16)
                        sp.wait_ge(s_store, stores * (g + 3))

            @block.scalar
            def _(act):
                k.norm_act(act, s_var, s_std)
                act.wait_ge(s_w, 16 * len(loads))
                act.wait_ge(s_chain, 3)
                for b in range(B):
                    for j in range(BG):
                        g = b * BG + j
                        act.wait_ge(s_xT, g + 1)
                        k.modulate(k.hT[:, j, :], p_x[j][:, :], 1, 0, b).then_inc(s_hT, 1)
                        for i, (p, sc) in enumerate(((p_q, scale), (p_k, 1.0))):
                            act.wait_ge(s_proj, 2 * g + i + 1)
                            act.wait_ge(s_split, 2 * g + i + 1)
                            nc.scalar.activation(full[:, j, i, :], p[j][:, :], ACT.Identity, scale=sc, bias=bias[:, i:i + 1]).then_inc(s_sb, 1)

            @block.tensor
            def _(pe):
                pe.wait_ge(s_w, 16 * len(loads))
                for b in range(B):
                    for j in range(BG):
                        g = b * BG + j
                        pe.wait_ge(s_xn, g + 1)
                        k.transpose_group(p_x[j], j).then_inc(s_xT, 1)
                        pe.wait_ge(s_hT, g + 1)
                        for p, n in ((p_q, "q"), (p_k, "k")):
                            nc.tensor.matmul(p[j][:, :], w[n][:], k.hT[:, j, :], start=True, stop=True).then_inc(s_proj, 1)
                        pe.wait_ge(s_vs, g + 1)
                        for t in range(GT):
                            last = nc.tensor.matmul(p_v[j][:, t * D:(t + 1) * D], k.hT[:, j, t * P:(t + 1) * P], w["v"][:], start=True, stop=True)
                        last.then_inc(s_v, 1)

            @block.vector
            def _(dve):
                chain = Chain(dve, s_chain)
                k.norm_dve(dve, chain, s_var, s_std)
                dve.wait_ge(s_w, 16 * len(loads))
                chain.link(nc.vector.tensor_scalar(bias[:, 0:1], bias[:, 0:1], scale, None, ALU.mult))
                nc.vector.memset(k.gated[:, 0, 0:1], 0.0).then_inc(s_vs, 2)
                nc.vector.memset(k.gated[:, 0, 1:2], 0.0).then_inc(s_split, FREE)
                nc.vector.memset(k.gated[:, 0, 2:3], 0.0).then_inc(s_store, 2 * stores)
                before, steps = chain.n, BG * 2 * 3
                for b in range(B):
                    chain = Chain(dve, s_chain, before + b * steps)
                    for j in range(BG):
                        g = b * BG + j
                        for t in range(GT):
                            last = k.normalise(g * GT + t, t, j)
                        last.then_inc(s_xn, 1)
                        for i in range(2):
                            dve.wait_ge(s_sb, 2 * g + i + 1)
                            if i == 0:
                                dve.wait_ge(s_store, stores * (g + 1))
                            x, hi, mid, lo = full[:, j, i, :], part[:, j, i, 0, :], part[:, j, i, 1, :], part[:, j, i, 2, :]
                            chain.link(nc.vector.tensor_copy(hi, x))
                            chain.link(nc.vector.tensor_tensor(x, x, hi, ALU.subtract))
                            chain.link(nc.vector.tensor_copy(mid, x))
                            nc.vector.tensor_tensor(lo, x, mid, ALU.subtract).then_inc(s_split, 1)
                        dve.wait_ge(s_v, g + 1)
                        nc.vector.tensor_tensor(V[:, ds(g * GT, GT), :], p_v[j][:, :].rearrange("p (t d) -> p t d", t=GT),
                                                b_v[:].unsqueeze(1).broadcast_to([P, GT, D]), ALU.add).then_inc(s_vs, 1)
                    assert chain.n == steps, chain.n


def base_batch(base, c):
    return base + c // CYCLE


def run(eng, step):
    step(0, 0, False)
    with eng.Fori(0, B - 1) as base:
        for c in range(1, CYCLE + 1):
            step(base, c, False)
    for c in range(1, CYCLE):
        step(B - 1, c, True)


def phase_attention(k, V, C, q_dram, k_dram, bufs):
    nc = k.nc
    s_top, s_max, s_mparts, s_mT, s_mrows, s_mdma, s_qk, s_exp, s_v, s_pv, s_o, s_oT, s_c, s_chain, s_recip = k.sems(
        "at", "top max mparts mT mrows mdma qk exp v pv o oT c chain recip")
    s_slot = k.sems("at_slot", "0 1 2 3")
    Q, K, Vs, zero_rows = bufs
    with ExitStack() as ph:
        def tmp(name, shape, dt=F32):
            return ph.enter_context(nc.sbuf_tensor(name, shape, dt))
        prob = tmp("prob", [P, 2, 4, GN])
        halfmax, top, rest = tmp("halfmax", [P, 2, TOPS]), tmp("top", [P, GT * 4]), tmp("rest", [P, GT * 4])
        mparts = tmp("mparts", [P, 2, GT, 12], BF16)
        mrows = tmp("mrows", [12, 2, GN], BF16)
        o_sb, recip = tmp("o_sb", [P, GN]), tmp("recip", [P, GT * 4])
        p_s = psum(nc, ph, "p_s", 2, 1024)
        p_m = psum(nc, ph, "p_m", 2)
        p_out = psum(nc, ph, "p_out", 1)[0]
        p_t = psum(nc, ph, "p_t", 1)[0]
        p_tb = p_t[:, :].bitcast(BF16)

        def quad(c):
            return (c % CYCLE) // 2

        with nc.Block() as block:
            @block.sync
            def _(sp):
                def fill(token0, c):
                    q = quad(c)
                    for par in range(2):
                        rows = slice(64 * par, 64 * par + SLOT)
                        for pair in range(2):
                            h = 4 * q + 2 * pair + par
                            sp.dma_start(Q[rows, q, pair, :], q_dram[:, h * DH:(h + 1) * DH, ds(token0, S)]).then_inc(s_slot[q], 16)
                            sp.dma_start(K[rows, q, pair, par, :], k_dram[:, h * DH:(h + 1) * DH, ds(token0, S)]).then_inc(s_slot[q], 16)
                        sp.dma_start(Q[64 * par + SLOT:64 * par + SROWS, q, :, :], zero_rows[:]).then_inc(s_slot[q], 16)

                def max_rows(base, c):
                    q, half = quad(c), c % 2
                    sp.wait_ge(s_mrows, base * CYCLE + c + 1)
                    for par in range(2):
                        for pair in range(2):
                            at = (par * 2 + pair) * 3
                            sp.dma_start(Q[64 * par + SLOT:64 * par + SROWS, q, pair, half * GN:(half + 1) * GN],
                                         mrows[at:at + 3, c % 2, :]).then_inc(s_mdma, 16)

                def step(base, c, last):
                    j = base * CYCLE + c
                    if c % 2 == 0 and (not last or c + 4 < CYCLE):
                        token0 = sp.snap(base_batch(base, c + 4) * S) if not isinstance(base, int) else base_batch(base, c + 4) * S
                        sp.wait_ge(s_qk, 2 * KT * j + 1)
                        fill(token0, c + 4)
                    if not last or c + 1 < CYCLE:
                        max_rows(base, c + 1)

                fill(0, 0)
                fill(0, 2)
                max_rows(0, 0)
                run(sp, step)
                sp.wait_ge(s_mdma, 64 * HALVES)

            @block.gpsimd
            def _(pool):
                def values(base, c):
                    b, q = base_batch(base, c), quad(c)
                    for h in range(4):
                        at = (4 * q + h) * DH
                        last = nc.gpsimd.tensor_copy(Vs[:, q % 2, :, h, 0:DH], V[:, ds(b * KT, KT), at:at + DH])
                    last.then_inc(s_v, 1)

                def step(base, c, last):
                    j = base * CYCLE + c
                    if c % 2 == 0 and (not last or c + 2 < CYCLE):
                        wait_pos(pool, s_pv, KT * j)
                        values(base, c + 2)

                values(0, 0)
                run(pool, step)

            @block.tensor
            def _(pe):
                def tops(base, c, n, first=0):
                    x = TOPS * (base * CYCLE + c) + n
                    q, half = quad(c), c % 2
                    tile, h, kh = n // 8, n // 2 % 4, n % 2
                    pair, par = h // 2, h % 2
                    at = half * GN + tile * P
                    if n == 0 and half == 0:
                        pe.wait_ge(s_slot[q], 160 * (base_batch(base, c) + 1))
                    wait_pos(pe, s_max, x - 1)
                    nc.tensor.matmul(p_m[n % 2][:, :], Q[:, q, pair, at:at + P], K[:, q, pair, par, kh * GN:(kh + 1) * GN],
                                     start=True, stop=True).then_inc(s_top, 1)

                def scores(base, c, kt, pair):
                    u = (base * CYCLE + c) * KT + kt
                    q, half = quad(c), c % 2
                    wait_pos(pe, s_exp, 2 * u + pair - 1)
                    for par in range(2):
                        last = nc.tensor.matmul(p_s[pair][:, par * GN:(par + 1) * GN], K[:, q, pair, par, kt * P:(kt + 1) * P],
                                                Q[:, q, pair, half * GN:(half + 1) * GN], start=True, stop=True)
                    last.then_inc(s_qk, 1)

                def weigh(base, c, kt, part):
                    u = (base * CYCLE + c) * KT + kt
                    if part == 0:
                        pe.wait_ge(s_exp, 2 * u + 2)
                    if kt == 0 and part == 0:
                        if c % 2 == 0:
                            pe.wait_ge(s_v, base * QUADS + c // 2 + 1)
                        wait_pos(pe, s_o, base * CYCLE + c)
                    for h in range(4):
                        last = nc.tensor.matmul(p_out[32 * h:32 * h + 32, part * HQ:(part + 1) * HQ], Vs[:, quad(c) % 2, kt, h, :],
                                                prob[:, kt % 2, h, part * HQ:(part + 1) * HQ], start=(kt == 0 and part == 0),
                                                stop=(kt == KT - 1), skip_group_check=True)
                    if part:
                        last.then_inc(s_pv, 1)

                def turn_max(base, c):
                    j = base * CYCLE + c
                    pe.wait_ge(s_mparts, j + 1)
                    wait_pos(pe, s_c, j - 2)
                    for t in range(GT):
                        last = nc.tensor.transpose(p_tb[0:12, t * P:(t + 1) * P], mparts[:, c % 2, t, :], k.identb[:])
                    last.then_inc(s_mT, 1)

                def turn_out(base, c, turned):
                    j = base * CYCLE + c
                    pe.wait_ge(s_o, j + 1)
                    pe.wait_ge(s_mrows, turned)
                    wait_pos(pe, s_c, j)
                    for t in range(GT):
                        last = nc.tensor.transpose(p_t[:, t * P:(t + 1) * P], o_sb[:, t * P:(t + 1) * P], k.ident[:])
                    last.then_inc(s_oT, 1)

                def step(base, c, last):
                    ahead = not last or c + 2 < CYCLE
                    pe.wait_ge(s_mdma, 64 * (base * CYCLE + c + 1))
                    for kt in range(KT):
                        for i in range(4):
                            if i < 2:
                                scores(base, c, kt, i)
                            elif kt or c:
                                weigh(base, c if kt else c - 1, (kt - 1) % KT, i - 2)
                            if ahead:
                                tops(base, c + 2, 4 * kt + i)
                        if kt == 1 and (not last or c + 1 < CYCLE):
                            turn_max(base, c + 1)
                        if kt == 3 and c:
                            turn_out(base, c - 1, base * CYCLE + c + 2 if not last or c + 1 < CYCLE else HALVES)

                for c in range(2):
                    for n in range(TOPS):
                        tops(0, c, n)
                    if c == 0:
                        turn_max(0, 0)
                run(pe, step)
                weigh(B - 1, CYCLE - 1, KT - 1, 0)
                weigh(B - 1, CYCLE - 1, KT - 1, 1)
                turn_out(B - 1, CYCLE - 1, HALVES)

            @block.scalar
            def _(act):
                def rows_out(base, c):
                    j = base * CYCLE + c
                    act.wait_ge(s_mT, j + 1)
                    wait_pos(act, s_mdma, 64 * (j - 1))
                    nc.scalar.activation(mrows[:, c % 2, :], p_tb[0:12, 0:GN], ACT.Copy).then_inc(s_mrows, 1)

                def evacuate(base, c):
                    j = base * CYCLE + c
                    act.wait_ge(s_pv, KT * (j + 1))
                    wait_pos(act, s_oT, j)
                    nc.scalar.activation(o_sb[:], p_out[:, :], ACT.Copy).then_inc(s_o, 1)

                def step(base, c, last):
                    for kt in range(KT):
                        u = (base * CYCLE + c) * KT + kt
                        if kt == 1 and c:
                            evacuate(base, c - 1)
                        wait_pos(act, s_pv, u - 1)
                        for pair in range(2):
                            act.wait_ge(s_qk, 2 * u + pair + 1)
                            nc.scalar.activation(prob[:, kt % 2, 2 * pair:2 * pair + 2, :],
                                                 p_s[pair][:, :].rearrange("p (h n) -> p h n", h=2), ACT.Exp).then_inc(s_exp, 1)
                        if kt == 2 and (not last or c + 1 < CYCLE):
                            rows_out(base, c + 1)

                rows_out(0, 0)
                run(act, step)
                evacuate(B - 1, CYCLE - 1)

            @block.vector
            def _(dve):
                steps = 4
                def tops(base, c, n):
                    x = TOPS * (base * CYCLE + c) + n
                    dve.wait_ge(s_top, x + 1)
                    nc.vector.tensor_reduce(halfmax[:, c % 2, n:n + 1], p_m[n % 2][:, :], AX_X, ALU.max).then_inc(s_max, 1)

                def parts(base, c):
                    j = base * CYCLE + c
                    dve.wait_ge(s_max, TOPS * (j + 1))
                    wait_pos(dve, s_mT, j - 1)
                    chain = Chain(dve, s_chain, j * steps)
                    chain.link(nc.vector.tensor_reduce(top[:], halfmax[:, c % 2, :].rearrange("p (n k) -> p n k", k=2), AX_X, ALU.max))
                    view = mparts[:, c % 2, :, :].rearrange("p t (par pair part) -> p t pair par part", par=2, pair=2)

                    def heads(x):
                        return x[:].rearrange("p (t pair par) -> p t pair par", t=GT, pair=2)
                    chain.link(nc.vector.tensor_copy(view[:, :, :, :, 0], heads(top)))
                    chain.link(nc.vector.tensor_tensor(heads(rest), heads(top), view[:, :, :, :, 0], ALU.subtract))
                    chain.link(nc.vector.tensor_copy(view[:, :, :, :, 1], heads(rest)))
                    nc.vector.tensor_tensor(view[:, :, :, :, 2], heads(rest), view[:, :, :, :, 1], ALU.subtract).then_inc(s_mparts, 1)

                def normalise(base, c):
                    j = base * CYCLE + c
                    dve.wait_ge(s_oT, j + 1)
                    o = p_t[:, :].rearrange("p (t h r) -> p t h r", t=GT, h=4)
                    nc.vector.reciprocal(recip[:].rearrange("p (t h) -> p t h", t=GT), o[:, :, :, DH]).then_inc(s_recip, 1)
                    dve.wait_ge(s_recip, j + 1)
                    tile0 = base_batch(base, c) * KT + (c % 2) * GT
                    at = quad(c) * 4 * DH
                    dst = C[:, ds(tile0, GT), at:at + 4 * DH].rearrange("p t (h d) -> p t h d", h=4)
                    nc.vector.tensor_tensor(dst, o[:, :, :, 0:DH],
                                            recip[:].rearrange("p (t h) -> p t h", t=GT).unsqueeze(3).broadcast_to([P, GT, 4, DH]),
                                            ALU.mult).then_inc(s_c, 1)

                def step(base, c, last):
                    if not last or c + 1 < CYCLE:
                        parts(base, c + 1)
                    for kt in range(KT):
                        if not last or c + 2 < CYCLE:
                            for n in range(4):
                                tops(base, c + 2, 4 * kt + n)
                        if kt == 5 and c:
                            normalise(base, c - 1)

                for c in range(2):
                    for n in range(TOPS):
                        tops(0, c, n)
                    if c == 0:
                        parts(0, 0)
                run(dve, step)
                normalise(B - 1, CYCLE - 1)


def phase_project(k, C):
    nc, ins = k.nc, k.ins
    s_w, s_chain, s_cT, s_cTs, s_o, s_gated = k.sems("pr", "w chain cT cTs o gated")
    with ExitStack() as ph:
        def tmp(name, shape):
            return ph.enter_context(nc.sbuf_tensor(name, shape, F32))
        w_o, b_o = tmp("w_o1", [P, D]), tmp("b_o1", [1, D])
        p_c, p_o = psum(nc, ph, "p_c", 2), psum(nc, ph, "p_o1", 2)
        with nc.Block() as block:
            @block.sync
            def _(sp):
                sp.dma_start(w_o[:], ins["L1_attn_out_wT"]).then_inc(s_w, 16)
                sp.dma_start(b_o[:], ins["L1_attn_out_b"].unsqueeze(0)).then_inc(s_w, 16)

            @block.scalar
            def _(act):
                for g in range(G):
                    act.wait_ge(s_cT, g + 1)
                    wait_pos(act, s_o, g - 1)
                    nc.scalar.activation(k.hT[:, g % 2, :], p_c[g % 2][:, :], ACT.Copy).then_inc(s_cTs, 1)

            @block.tensor
            def _(pe):
                def turn(g):
                    wait_pos(pe, s_cTs, g - 1)
                    for t in range(GT):
                        last = nc.tensor.transpose(p_c[g % 2][:, t * P:(t + 1) * P], C[:, g * GT + t, :], k.ident[:])
                    last.then_inc(s_cT, 1)

                def project(g):
                    pe.wait_ge(s_cTs, g + 1)
                    wait_pos(pe, s_gated, g - 1)
                    for t in range(GT):
                        o = p_o[g % 2][:, t * D:(t + 1) * D]
                        nc.tensor.matmul(o, k.ones[0:1, :], b_o[:], start=True, stop=False)
                        last = nc.tensor.matmul(o, k.hT[:, g % 2, t * P:(t + 1) * P], w_o[:], start=False, stop=True)
                    last.then_inc(s_o, 1)

                pe.wait_ge(s_w, 32)
                turn(0)
                for g in range(1, G):
                    turn(g)
                    project(g - 1)
                project(G - 1)

            @block.vector
            def _(dve):
                chain = Chain(dve, s_chain)
                for g in range(G):
                    dve.wait_ge(s_o, g + 1)
                    k.gate(p_o[g % 2][:, :].rearrange("p (t d) -> p t d", t=GT), 1, 0, g // BG).then_inc(s_gated, 1)
                    dve.wait_ge(s_gated, g + 1)
                    chain.link(k.add_gated(g * GT))
                    k.stats(chain, g * GT)
                    chain.wait()


def phase_experts1(k, w1, b1, w2, b2, s_weights):
    nc = k.nc
    s_chain, s_up, s_gelu, s_y, s_acc, s_res, s_out = k.sems("x1", "chain up gelu y acc res out")
    out_v = k.out.rearrange("b (t p) d -> p (b t) d", p=P)
    with ExitStack() as ph:
        def tmp(name, shape):
            return ph.enter_context(nc.sbuf_tensor(name, shape, F32))
        hid, acc = tmp("hid", [P, 2, FC, GN]), tmp("acc1", [P, GT, D])
        p_h, p_y = psum(nc, ph, "p_h", 4), psum(nc, ph, "p_y1", 2)
        with nc.Block() as block:
            @block.sync
            def _(sp):
                with sp.Fori(0, G) as g:
                    sp.wait_ge(s_res, g + 1)
                    sp.dma_start(out_v[:, ds(g * GT, GT), :], k.X[:, ds(g * GT, GT), :]).then_inc(s_out, 16)
                sp.wait_ge(s_out, 16 * G)

            @block.scalar
            def _(act):
                with act.Fori(0, B) as b:
                    for j in range(BG):
                        for e in range(E):
                            n = (b * BG + j) * E + e
                            act.wait_ge(s_y, n + 1)
                            for c in range(FC):
                                act.wait_ge(s_up, n * FC + c + 1)
                                nc.scalar.activation(hid[:, e % 2, c, :], p_h[c][:, :], ACT.Gelu, bias=b1[:, e, c:c + 1]).then_inc(s_gelu, 1)

            @block.tensor
            def _(pe):
                def up(g, e):
                    n = g * E + e
                    rhs = k.HT[:, ds(g * GN, GN)]
                    for c in range(FC):
                        pe.wait_ge(s_gelu, n * FC + c + 1)
                        nc.tensor.matmul(p_h[c][:, :], w1[:, e, c * P:(c + 1) * P], rhs, start=True, stop=True).then_inc(s_up, 1)

                def down(g, e):
                    n = g * E + e
                    pe.wait_ge(s_gelu, (n + 2) * FC)
                    pe.wait_ge(s_acc, n + 1)
                    for t in range(GT):
                        for c in range(FC):
                            last = nc.tensor.matmul(p_y[e % 2][:, t * D:(t + 1) * D], hid[:, e % 2, c, t * P:(t + 1) * P], w2[:, e, c, :],
                                                    start=(c == 0), stop=(c == FC - 1))
                    last.then_inc(s_y, 1)

                pe.wait_ge(s_weights, 64)
                with pe.Fori(0, B) as b:
                    for j in range(BG):
                        g = b * BG + j
                        up(g, 0)
                        for e in range(1, E):
                            up(g, e)
                            down(g, e - 1)
                        down(g, E - 1)

            @block.vector
            def _(dve):
                nc.vector.memset(k.gated[:, 0, 0:1], 0.0).then_inc(s_acc, 2)
                nc.vector.memset(k.gated[:, 0, 1:2], 0.0).then_inc(s_y, 2)
                nc.vector.memset(k.gated[:, 0, 2:3], 0.0).then_inc(s_gelu, FC)
                dve.wait_ge(s_weights, 64)
                steps = BG * (E + 1)
                with dve.Fori(0, B) as b:
                    chain = Chain(dve, s_chain, b * steps)
                    for j in range(BG):
                        g = b * BG + j
                        for e in range(E):
                            for t in range(GT):
                                w = k.wts[:, ds(g * GT + t, 1), e]
                                if e == 0:
                                    last = nc.vector.tensor_scalar(acc[:, t, :], b2[:, e, :], w, None, ALU.mult)
                                else:
                                    last = nc.vector.scalar_tensor_tensor(out=acc[:, t, :], in0=b2[:, e, :], scalar=w, in1=acc[:, t, :],
                                                                          op0=ALU.mult, op1=ALU.add)
                            chain.link(last)
                        for e in range(E):
                            n = g * E + e
                            dve.wait_ge(s_y, n + 3)
                            if e:
                                dve.wait_ge(s_acc, n + 2)
                            for t in range(GT):
                                last = nc.vector.scalar_tensor_tensor(out=acc[:, t, :], in0=p_y[e % 2][:, t * D:(t + 1) * D],
                                                                      scalar=k.wts[:, ds(g * GT + t, 1), e], in1=acc[:, t, :],
                                                                      op0=ALU.mult, op1=ALU.add)
                            last.then_inc(s_acc, 1)
                        dve.wait_ge(s_acc, (g + 1) * E + 2)
                        chain.link(k.gate(acc[:], 1, 1, b))
                        k.add_gated(g * GT).then_inc(s_res, 1)
                        dve.wait_ge(s_res, g + 1)
                    assert chain.n == steps, chain.n


def build(nc, ins, out):
    with ExitStack() as ctx:
        k = Kernel(nc, ctx, ins, out)
        q_dram = nc.dram_tensor("q_parts", [TERMS, P, N], BF16).ap()
        k_dram = nc.dram_tensor("k_parts", [TERMS, P, N], BF16).ap()
        s_w0, s_w1 = k.sem("weights0"), k.sem("weights1")

        def tensor(stack, name, shape, dt=F32):
            return stack.enter_context(nc.sbuf_tensor(name, shape, dt))

        with ExitStack() as attn:
            bufs = (tensor(attn, "Q", [P, QUADS, 2, S], BF16),
                    tensor(attn, "K", [P, QUADS, 2, 2, S], BF16),
                    tensor(attn, "Vs", [P, 2, KT, 4, 32]),
                    tensor(attn, "zero_rows", [3, 2, S], BF16))
            V = tensor(attn, "V", [P, T, D])
            phase_setup(k, bufs)
            phase_linear_attention(k)
            with ExitStack() as mixture:
                w_gu, w_down = tensor(mixture, "w_gu", [P, E, 2 * P]), tensor(mixture, "w_down", [P, E, D])
                phase_gating(k, 0, "L0_ffn_gate_wT", (ALU.max, 1e-12),
                             [(w_gu[:], ins["L0_ffn_gu"], s_w0), (w_down[:], ins["L0_ffn_down"], s_w0)])
                phase_experts0(k, w_gu, w_down, s_w0)
            phase_qkv(k, V, q_dram, k_dram)
            C = k.HT[:].rearrange("p (t d) -> p t d", d=D)
            phase_attention(k, V, C, q_dram, k_dram, bufs)
        w1, b1 = k.sb("w1", [P, E, F1]), k.sb("b1", [P, E, FC])
        w2, b2 = k.sb("w2", [P, E, FC, D]), k.sb("b2", [P, E, D])
        phase_project(k, C)
        phase_gating(k, 1, "L1_ffn_Wg", (ALU.add, 1e-9), [
            (w1[:], ins["L1_ffn_W1"].rearrange("e d f -> d e f"), s_w1), (b1[:], ins["L1_ffn_b1"], s_w1),
            (w2[:], ins["L1_ffn_W2"].rearrange("e (c f) d -> f e c d", f=P), s_w1),
            (b2[:], bass.AP(ins["L1_ffn_b2"].tensor, 0, [[0, P], [D, E], [1, D]]), s_w1)])
        phase_experts1(k, w1, b1, w2, b2, s_w1)


def kernel(**inputs):
    import numpy as np
    import concourse.bacc as bacc
    from concourse.bass_utils import run_bass_kernel_spmd

    a = {n: np.asarray(v) for n, v in inputs.items()}
    consts = np.concatenate([np.eye(P), np.kron(np.eye(H), np.ones((DH, DH))), np.tile(np.arange(E, 0, -1), (P, 1)),
                             np.tile(np.eye(E).reshape(1, -1), (P, 1))], axis=1).astype(np.float32)
    same = ["L0_attn_x", "L0_attn_Wq", "L0_attn_Wk", "L0_attn_Wv", "L0_attn_Wo", "L0_attn_bq", "L0_attn_bk", "L0_attn_bv", "L0_attn_bo",
            "L0_attn_m", "L0_ffn_similarity_matrix", "L0_wmod", "L1_attn_q_b", "L1_attn_k_b", "L1_attn_v_b", "L1_attn_out_b",
            "L1_ffn_Wg", "L1_ffn_W1", "L1_ffn_W2", "L1_ffn_b2", "L1_wmod"]
    laid = {n: a[n] for n in same} | {"consts": consts}
    laid |= {f"L1_attn_{n}_wT": a[f"L1_attn_{n}_w"].T for n in ("q", "k", "v", "out")}
    laid |= {f"L{i}_cT": a[f"L{i}_c"].T for i in range(2)}
    laid["L0_ffn_gate_wT"] = a["L0_ffn_gate_weight"].T
    laid["L0_ffn_gu"] = a["L0_ffn_gate_up_proj"].transpose(2, 0, 1)
    laid["L0_ffn_down"] = a["L0_ffn_down_proj"].transpose(2, 0, 1)
    laid["L1_ffn_b1"] = a["L1_ffn_b1"].reshape(E, FC, P).transpose(2, 0, 1)

    nc = bacc.Bacc("TRN2", target_bir_lowering=False, num_devices=1)
    arrays, aps = {}, {}
    for n, v in laid.items():
        arrays[f"in_{n}"] = np.ascontiguousarray(v)
        aps[n] = nc.dram_tensor(f"in_{n}", arrays[f"in_{n}"].shape, F32, kind="ExternalInput").ap()
    out = nc.dram_tensor("out", [B, S, D], F32, kind="ExternalOutput").ap()
    build(nc, aps, out)
    r = run_bass_kernel_spmd(nc, [arrays], core_ids=[0])
    return r.results[0]["out"]
```

```python
import math
from contextlib import ExitStack

import concourse.bass as bass
from concourse import mybir

ALU = mybir.AluOpType
ACT = mybir.ActivationFunctionType
AX_X = mybir.AxisListType.X
F32 = mybir.dt.float32
BF16 = mybir.dt.bfloat16
F32R = mybir.dt.float32r
U32 = mybir.dt.uint32

P = 128
B, S, D = 4, 1024, 128
H, DH = 16, 8
E = 8
F1 = 512
FC = F1 // P
N = B * S
T = N // P
GT = 4
GN = GT * P
G = T // GT
BG = S // GN
LN_EPS = 1e-5
SIM_MIN = 0.7
NEG = 3.0e38
QUADS = H // 4
TERMS = 6
SLOT = TERMS * DH
Q_PARTS = (0, 0, 0, 1, 1, 2)
K_PARTS = (0, 1, 2, 0, 1, 0)
SROWS = SLOT + 3
KT = S // P
HQ = GN // 2
HALVES = B * QUADS * 2
CYCLE = QUADS * 2
TOPS = GT * 4 * 2
ds = bass.ds


class Chain:

    def __init__(self, eng, sem, base=0):
        self.eng, self.sem, self.base, self.n = eng, sem, base, 0

    def add(self, ins):
        ins.then_inc(self.sem, 1)
        self.n += 1

    def wait(self):
        self.eng.wait_ge(self.sem, self.base + self.n)

    def link(self, ins):
        self.add(ins)
        self.wait()


def wait_pos(eng, sem, value):
    if not (isinstance(value, int) and value <= 0):
        eng.wait_ge(sem, value)


class Kernel:

    def __init__(self, nc, ctx, ins, out):
        self.nc, self.ctx, self.ins, self.out = nc, ctx, ins, out
        self.X = self.sb("X", [P, T, D])
        self.HT = self.sb("HT", [P, N])
        self.MV = self.sb("MV", [P, T, 2])
        self.bstats = self.sb("bstats", [P, GT, 6])
        self.std = self.sb("std", [P, T])
        self.rstd = self.sb("rstd", [P, T])
        self.nmr = self.sb("nmr", [P, T])
        self.xn = self.sb("xn", [P, 2, GN])
        self.hT = self.sb("hT", [P, 2, GN])
        self.mv4 = self.sb("mv4", [P, GT, 2])
        self.kvmask = self.sb("kvmask", [P, P])
        self.mark = self.sb("mark", [P, 1])
        self.gated = self.sb("gated", [P, 2, GT, D])
        self.ident = self.sb("ident", [P, P])
        self.identb = self.sb("identb", [P, P], BF16)
        self.ones = self.sb("ones", [P, P])
        self.rank = self.sb("rank", [P, E])
        self.eye8 = self.sb("eye8", [P, E, E])
        self.pick = self.sb("pick", [2 * E, E, P], F32R)
        self.WT = self.sb("WT", [2 * E, N], F32R)
        self.modv = self.sb("modv", [P, 2, 4, B])
        self.gate_row = self.sb("gate_row", [P, 2, B, 2, D])
        self.wts = self.sb("wts", [P, T, E])

    def sb(self, name, shape, dt=F32):
        return self.ctx.enter_context(self.nc.sbuf_tensor(name, shape, dt))

    def sem(self, name):
        return self.ctx.enter_context(self.nc.semaphore(name))

    def sems(self, tag, names):
        return [self.sem(f"{tag}_{n}") for n in names.split()]

    def stats(self, chain, tile0, loop=False):
        nc = self.nc
        if loop:
            nc.vector.memset(self.mark[:], 0.0)
        for t in range(GT):
            chain.add(nc.vector.bn_stats(self.bstats[:, t, :], self.X[:, tile0 + t, :] if not loop else
                                         self.X[:, ds(tile0 + t, 1), :].rearrange("p o d -> p (o d)")))
        chain.wait()
        if loop:
            nc.vector.memset(self.mark[:], 0.0)
        for t in range(GT):
            chain.add(nc.vector.bn_aggr(self.mv4[:, t, :] if loop else self.MV[:, tile0 + t, :], self.bstats[:, t, :]))
        if loop:
            chain.wait()
            chain.link(nc.vector.tensor_scalar(self.MV[:, ds(tile0, GT), :], self.mv4[:], 1.0, None, ALU.mult))

    def norm_dve(self, dve, chain, s_var, s_std):
        nc = self.nc
        nc.vector.tensor_scalar(self.std[:], self.MV[:, :, 1], LN_EPS, None, ALU.add).then_inc(s_var, 1)
        dve.wait_ge(s_std, 1)
        chain.link(nc.vector.reciprocal(self.rstd[:], self.std[:]))
        chain.link(nc.vector.scalar_tensor_tensor(out=self.nmr[:], in0=self.MV[:, :, 0], scalar=-1.0, in1=self.rstd[:],
                                                  op0=ALU.mult, op1=ALU.mult))

    def norm_act(self, act, s_var, s_std):
        act.wait_ge(s_var, 1)
        self.nc.scalar.activation(self.std[:], self.std[:], ACT.Sqrt).then_inc(s_std, 1)

    def normalise(self, tile, t, slot):
        return self.nc.vector.tensor_scalar(self.xn[:, slot, t * P:(t + 1) * P], self.X[:, tile, :], self.rstd[:, tile:tile + 1],
                                            self.nmr[:, tile:tile + 1], ALU.mult, ALU.add)

    def normalise_act(self, tile, t, slot):
        return self.nc.scalar.activation(self.xn[:, slot, t * P:(t + 1) * P], self.X[:, tile, :], ACT.Identity,
                                         scale=self.rstd[:, tile:tile + 1], bias=self.nmr[:, tile:tile + 1])

    def transpose_group(self, dst, slot):
        for t in range(GT):
            last = self.nc.tensor.transpose(dst[:, t * P:(t + 1) * P], self.xn[:, slot, t * P:(t + 1) * P], self.ident[:])
        return last

    def modulate(self, dst, src, layer, which, b):
        return self.nc.scalar.activation(dst, src, ACT.Identity, scale=self.modv[:, layer, 2 * which + 1, ds(b, 1)],
                                         bias=self.modv[:, layer, 2 * which, ds(b, 1)])

    def gate(self, y, layer, which, b, slot=0):
        g = self.gate_row[:, layer, ds(b, 1), which, :].broadcast_to([P, GT, D])
        return self.nc.vector.tensor_tensor(self.gated[:, slot], y, g, ALU.mult)

    def add_gated(self, tile0, slot=0, eng=None):
        x = self.X[:, ds(tile0, GT), :]
        return (eng or self.nc.vector).tensor_tensor(x, x, self.gated[:, slot], ALU.add)


def psum(nc, stack, name, n, cols=512):
    return [stack.enter_context(nc.psum_tensor(f"{name}{i}", [P, cols], F32)) for i in range(n)]


def row_of(ap, n):
    return bass.AP(ap.tensor, 0, [[0, P], [1, n]])


def phase_setup(k, bufs):
    nc, ins = k.nc, k.ins
    s_load, s_chain, s_silu, s_spread, s_sig, s_mod, s_zero = k.sems("set", "load chain silu spread sig mod zero")
    Q, K, Vs, zero_rows = bufs
    with ExitStack() as ph:
        def tmp(name, shape):
            return ph.enter_context(nc.sbuf_tensor(name, shape, F32))
        wmod = [tmp(f"wmod{i}", [P, 6 * D]) for i in range(2)]
        cT, cs, cspread = tmp("cT", [P, 2, B]), tmp("cs", [P, 2, B]), tmp("cspread", [P, 2 * B, P])
        headmask, m_col, m_sig, sign, size = tmp("headmask", [P, P]), tmp("m_col", [P, 1]), tmp("m_sig", [P, 2]), tmp("sign", [P, 512]), tmp("size", [P, 512])
        p_col = psum(nc, ph, "p_col", 1)[0]
        p_row = psum(nc, ph, "p_row", 4)
        consts = ins["consts"]
        loads = [(cT[:, 0, :], ins["L0_cT"]), (cT[:, 1, :], ins["L1_cT"]),
                 (wmod[0][:], ins["L0_wmod"]), (wmod[1][:], ins["L1_wmod"]),
                 (k.ident[:], consts[:, 0:P]), (headmask[:], consts[:, P:2 * P]), (k.rank[:], consts[:, 2 * P:2 * P + E]),
                 (k.eye8[:], consts[:, 2 * P + E:2 * P + E + E * E].rearrange("p (i j) -> p i j", i=E)),
                 (m_col[:], bass.AP(ins["L0_attn_m"].tensor, 0, [[1, H], [0, DH], [1, 1]]))]
        xv = ins["L0_attn_x"].rearrange("b (t p) d -> p (b t) d", p=P)
        loads += [(k.X[:, g * GT:(g + 1) * GT, :], xv[:, g * GT:(g + 1) * GT, :]) for g in range(G)]
        with nc.Block() as block:
            @block.sync
            def _(sp):
                for dst, src in loads:
                    sp.dma_start(dst, src).then_inc(s_load, 16)

            @block.gpsimd
            def _(pool):
                chain = Chain(pool, s_zero)
                chain.link(nc.gpsimd.memset(K[:].bitcast(U32), 0))
                chain.link(nc.gpsimd.memset(Q[:].bitcast(U32), 0))
                chain.link(nc.gpsimd.memset(zero_rows[:].bitcast(U32), 0))
                chain.link(nc.gpsimd.memset(Vs[:], 1.0))
                for par in range(2):
                    chain.link(nc.gpsimd.memset(K[64 * par + 32:64 * par + 64, :, :, par, :], -1.0))

            @block.scalar
            def _(act):
                act.wait_ge(s_load, 16 * len(loads))
                nc.scalar.activation(m_sig[:, 0:1], m_col[:], ACT.Sigmoid).then_inc(s_sig, 1)
                nc.scalar.activation(cs[:], cT[:], ACT.Silu).then_inc(s_silu, 1)
                act.wait_ge(s_sig, 1)
                nc.scalar.activation(m_sig[:, 1:2], m_sig[:, 0:1], ACT.Exp, scale=-math.log(S)).then_inc(s_sig, 1)

            @block.tensor
            def _(pe):
                pe.wait_ge(s_silu, 1)
                for layer in range(2):
                    for i, j in enumerate((0, 1, 3, 4)):
                        at = (layer * 4 + i) * B
                        nc.tensor.matmul(p_col[:, at:at + B], wmod[layer][:, j * D:(j + 1) * D], cs[:, layer, :], start=True, stop=True)
                pe.wait_ge(s_spread, 1)
                for layer in range(2):
                    for b in range(B):
                        for i, j in enumerate((2, 5)):
                            at = (b % 2) * 2 * D + i * D
                            last = nc.tensor.matmul(p_row[layer * 2 + b // 2][:, at:at + D], cspread[:, layer * B + b, :],
                                                    wmod[layer][:, j * D:(j + 1) * D], start=True, stop=True)
                last.then_inc(s_mod, 1)

            @block.vector
            def _(dve):
                chain = Chain(dve, s_chain)
                chain.add(nc.vector.memset(k.ones[:], 1.0))
                dve.wait_ge(s_load, 16 * len(loads))
                chain.add(nc.vector.tensor_copy(k.identb[:], k.ident[:]))
                ones_at = [k.ident[0:2 * E, i * E:(i + 1) * E].unsqueeze(2).broadcast_to([2 * E, E, P]) for i in range(2)]
                chain.add(nc.vector.tensor_tensor(k.pick[:], ones_at[0], ones_at[1], ALU.add))
                dve.wait_ge(s_silu, 1)
                nc.vector.tensor_copy(cspread[:], cs[:].rearrange("p l b -> p (l b)").unsqueeze(2).broadcast_to([P, 2 * B, P])).then_inc(s_spread, 1)
                for g in range(G):
                    chain.wait()
                    k.stats(chain, g * GT)
                dve.wait_ge(s_sig, 2)
                chain.add(nc.vector.tensor_scalar(k.kvmask[:], headmask[:], m_sig[:, 1:2], None, ALU.mult))
                dve.wait_ge(s_mod, 1)
                chain.link(nc.vector.tensor_copy(k.modv[:].rearrange("p l k b -> p (l k b)"), p_col[:, 0:2 * 4 * B]))
                for layer in range(2):
                    for i in (1, 3):
                        chain.add(nc.vector.tensor_scalar(k.modv[:, layer, i, :], k.modv[:, layer, i, :], 1.0, None, ALU.add))
                for i in range(4):
                    row = k.gate_row[:, i // 2, (i % 2) * 2:(i % 2) * 2 + 2, :, :].rearrange("p b k d -> p (b k d)")
                    chain.link(nc.vector.tensor_copy(row, p_row[i][:, :]))
                    chain.link(nc.vector.tensor_scalar(sign[:], row, 0.0, 2.0, ALU.is_ge, ALU.mult))
                    chain.link(nc.vector.scalar_tensor_tensor(out=size[:], in0=row, scalar=-1.0, in1=row, op0=ALU.mult, op1=ALU.max))
                    chain.link(nc.vector.tensor_scalar(size[:], size[:], 0.25, None, ALU.max))
                    chain.link(nc.vector.scalar_tensor_tensor(out=row, in0=sign[:], scalar=-1.0, in1=size[:], op0=ALU.add, op1=ALU.mult))


def phase_linear_attention(k):
    nc, ins = k.nc, k.ins
    s_w, s_var, s_std, s_chain, s_xn, s_xT, s_hT, s_qkv, s_biased, s_sq, s_sum, s_root, s_unit = k.sems(
        "la", "w var std chain xn xT hT qkv biased sq sum root unit")
    s_kv, s_kvT, s_g, s_gm, s_qT, s_qTs, s_o, s_gated, s_x = k.sems("la2", "kv kvT g gm qT qTs o gated x")
    RING = 3
    with ExitStack() as ph:
        def tmp(name, shape):
            return ph.enter_context(nc.sbuf_tensor(name, shape, F32))
        w_qkv, b_qkv, w_o, b_o = tmp("w_qkv", [P, 3 * D]), tmp("b_qkv", [P, 3 * D]), tmp("w_o", [P, D]), tmp("b_o", [1, D])
        qkv = tmp("qkv", [P, RING, GT, 3 * D])
        sq, norm, inv = tmp("sq", [P, 2, GT, 2 * D]), tmp("norm", [P, 2, GT * 2 * H]), tmp("inv", [P, GT * 2 * H])
        qT, kvT, kvo = tmp("qT", [P, GT, GN]), tmp("kvT", [P, P]), tmp("kvo", [P, P])
        p_x = psum(nc, ph, "p_x", 1)[0]
        p_qkv = psum(nc, ph, "p_qkv", 3)
        p_kv, p_kvo, p_qT, p_o = (psum(nc, ph, n, 1)[0] for n in ("p_kv", "p_kvo", "p_qT", "p_o"))
        loads = [(w_qkv[:, i * D:(i + 1) * D], ins[f"L0_attn_W{n}"]) for i, n in enumerate("qkv")]
        loads += [(b_qkv[:, i * D:(i + 1) * D], row_of(ins[f"L0_attn_b{n}"], D)) for i, n in enumerate("qkv")]
        loads += [(w_o[:], ins["L0_attn_Wo"]), (b_o[:], ins["L0_attn_bo"].unsqueeze(0))]
        with nc.Block() as block:
            @block.sync
            def _(sp):
                for dst, src in loads:
                    sp.dma_start(dst, src).then_inc(s_w, 16)

            @block.scalar
            def _(act):
                def norm_group(g):
                    wait_pos(act, s_xT, g - 1)
                    for t in range(GT):
                        last = k.normalise_act(g * GT + t, t, g % 2)
                    last.then_inc(s_xn, 1)

                def modulate(g):
                    act.wait_ge(s_xT, g + 1)
                    wait_pos(act, s_qkv, (g - 1) * GT)
                    k.modulate(k.hT[:, g % 2, :], p_x[:, :], 0, 0, g // BG).then_inc(s_hT, 1)

                def queries(g):
                    act.wait_ge(s_qT, g + 1)
                    wait_pos(act, s_o, g - GT + 1)
                    nc.scalar.activation(qT[:, g % GT, :], p_qT[:, :], ACT.Copy).then_inc(s_qTs, 1)

                k.norm_act(act, s_var, s_std)
                act.wait_ge(s_chain, 2)
                norm_group(0)
                modulate(0)
                norm_group(1)
                for i in range(G + 1):
                    if i + 1 < G:
                        modulate(i + 1)
                    if i + 2 < G:
                        norm_group(i + 2)
                    if i >= 2:
                        queries(i - 2)
                    if i >= 1:
                        act.wait_ge(s_sum, i)
                        nc.scalar.activation(norm[:, (i - 1) % 2, :], norm[:, (i - 1) % 2, :], ACT.Sqrt).then_inc(s_root, 1)
                    if i < G:
                        act.wait_ge(s_biased, (i + 1) * GT)
                        wait_pos(act, s_sum, i - 1)
                        nc.scalar.activation(sq[:, i % 2], qkv[:, i % RING, :, 0:2 * D], ACT.Square).then_inc(s_sq, 1)
                queries(G - 1)

            @block.tensor
            def _(pe):
                def turn(g):
                    pe.wait_ge(s_xn, g + 1)
                    wait_pos(pe, s_hT, g)
                    k.transpose_group(p_x, g % 2).then_inc(s_xT, 1)

                def project(g):
                    pe.wait_ge(s_hT, g + 1)
                    for t in range(GT):
                        n = g * GT + t
                        wait_pos(pe, s_biased, n - 2)
                        nc.tensor.matmul(p_qkv[n % 3][:, 0:3 * D], k.hT[:, g % 2, t * P:(t + 1) * P], w_qkv[:],
                                         start=True, stop=True).then_inc(s_qkv, 1)

                def keys_values(g):
                    pe.wait_ge(s_unit, g + 1)
                    if g % BG == 0:
                        wait_pos(pe, s_kvT, g // BG)
                    for t in range(GT):
                        last = nc.tensor.matmul(p_kv[:, 0:P], qkv[:, g % RING, t, 2 * D:3 * D], qkv[:, g % RING, t, D:2 * D],
                                                start=(g % BG == 0 and t == 0), stop=(g % BG == BG - 1 and t == GT - 1))
                    last.then_inc(s_kv, 1)
                    wait_pos(pe, s_qTs, g)
                    for t in range(GT):
                        last = nc.tensor.transpose(p_qT[:, t * P:(t + 1) * P], qkv[:, g % RING, t, 0:D], k.ident[:])
                    last.then_inc(s_qT, 1)

                def fold_projection(b):
                    pe.wait_ge(s_kvT, b + 1)
                    wait_pos(pe, s_gm, b)
                    nc.tensor.matmul(p_kvo[:, 0:D], kvT[:], w_o[:], start=True, stop=True).then_inc(s_g, 1)

                def output(g):
                    pe.wait_ge(s_gm, g // BG + 1)
                    pe.wait_ge(s_qTs, g + 1)
                    wait_pos(pe, s_gated, g)
                    for t in range(GT):
                        o = p_o[:, t * D:(t + 1) * D]
                        nc.tensor.matmul(o, k.ones[0:1, :], b_o[:], start=True, stop=False)
                        last = nc.tensor.matmul(o, qT[:, g % GT, t * P:(t + 1) * P], kvo[:], start=False, stop=True)
                    last.then_inc(s_o, 1)

                pe.wait_ge(s_w, 16 * len(loads))
                turn(0)
                for i in range(G + 3):
                    if i + 1 < G:
                        turn(i + 1)
                    if i < G:
                        project(i)
                    if i >= 3 and i % BG == 1:
                        fold_projection((i - 3) // BG)
                    if 1 <= i <= G:
                        keys_values(i - 1)
                    if 3 <= i:
                        output(i - 3)

            @block.gpsimd
            def _(pool):
                for g in range(G):
                    pool.wait_ge(s_gated, g + 1)
                    k.add_gated(g * GT, g % 2, nc.gpsimd).then_inc(s_x, 1)

            @block.vector
            def _(dve):
                chain = Chain(dve, s_chain)
                k.norm_dve(dve, chain, s_var, s_std)
                dve.wait_ge(s_w, 16 * len(loads))
                for i in range(G + 4):
                    if 1 <= i <= G:
                        dve.wait_ge(s_sq, i)
                        nc.vector.tensor_reduce(norm[:, (i - 1) % 2, :], sq[:, (i - 1) % 2].rearrange("p t (h d) -> p (t h) d", d=DH),
                                                AX_X, ALU.add).then_inc(s_sum, 1)
                    if i >= 3 and i % BG == 1 and i < G + 3:
                        b = (i - 3) // BG
                        dve.wait_ge(s_kv, (b + 1) * BG)
                        wait_pos(dve, s_g, b)
                        nc.vector.tensor_tensor(kvT[:], p_kv[:, 0:P], k.kvmask[:], ALU.mult).then_inc(s_kvT, 1)
                    if i < G:
                        wait_pos(dve, s_qT, i - RING + 1)
                        for t in range(GT):
                            n = i * GT + t
                            dve.wait_ge(s_qkv, n + 1)
                            nc.vector.tensor_tensor(qkv[:, i % RING, t, :], p_qkv[n % 3][:, 0:3 * D], b_qkv[:], ALU.add).then_inc(s_biased, 1)
                    if i >= 3 and i % BG == 1 and i < G + 3:
                        dve.wait_ge(s_g, b + 1)
                        wait_pos(dve, s_o, b * BG)
                        nc.vector.tensor_copy(kvo[:], p_kvo[:, 0:D]).then_inc(s_gm, 1)
                    if 1 <= i <= G:
                        dve.wait_ge(s_root, i)
                        chain.link(nc.vector.tensor_scalar(inv[:], norm[:, (i - 1) % 2, :], 1e-12, None, ALU.max))
                        chain.link(nc.vector.reciprocal(inv[:], inv[:]))
                        qk = qkv[:, (i - 1) % RING, :, 0:2 * D].rearrange("p t (h d) -> p t h d", d=DH)
                        iv = inv[:].rearrange("p (t h) -> p t h", t=GT).unsqueeze(3).broadcast_to([P, GT, 2 * H, DH])
                        nc.vector.tensor_tensor(qk, qk, iv, ALU.mult).then_inc(s_unit, 1)
                    if 3 <= i < G + 3:
                        g = i - 3
                        dve.wait_ge(s_o, g + 1)
                        wait_pos(dve, s_x, g - 1)
                        k.gate(p_o[:, :].rearrange("p (t d) -> p t d", t=GT), 0, 0, g // BG, g % 2).then_inc(s_gated, 1)
                    if i >= 4:
                        dve.wait_ge(s_x, i - 3)
                        k.stats(chain, (i - 4) * GT)
                        chain.wait()


def top_two(k, dve, chain, act_sems, scr, guard):
    nc = k.nc
    s_shift, s_exp = act_sems
    p, first, second, cand, v1, v2, r = (scr[n] for n in ("p", "first", "second", "cand", "v1", "v2", "r"))

    def wide(v):
        return v[:].unsqueeze(2).broadcast_to([P, T, E])

    rank = k.rank[:].unsqueeze(1).broadcast_to([P, T, E])
    chain.link(nc.vector.tensor_reduce(v1[:], p[:], AX_X, ALU.max))
    nc.vector.tensor_tensor(p[:], p[:], wide(v1), ALU.subtract).then_inc(s_shift, 1)
    dve.wait_ge(s_exp, 1)
    chain.link(nc.vector.tensor_reduce(v1[:], p[:], AX_X, ALU.add))
    chain.link(nc.vector.reciprocal(v1[:], v1[:]))
    chain.link(nc.vector.tensor_tensor(p[:], p[:], wide(v1), ALU.mult))
    for v, mask in ((v1, first), (v2, second)):
        chain.link(nc.vector.tensor_reduce(v[:], p[:], AX_X, ALU.max))
        chain.link(nc.vector.tensor_tensor(cand[:], p[:], wide(v), ALU.is_equal))
        chain.link(nc.vector.tensor_tensor(cand[:], cand[:], rank, ALU.mult))
        chain.link(nc.vector.tensor_reduce(r[:], cand[:], AX_X, ALU.max))
        chain.link(nc.vector.tensor_tensor(mask[:], wide(r), rank, ALU.is_equal))
        if v is v1:
            chain.link(nc.vector.scalar_tensor_tensor(out=p[:], in0=mask[:], scalar=-4.0, in1=p[:], op0=ALU.mult, op1=ALU.add))
    chain.link(nc.vector.tensor_tensor(r[:], v1[:], v2[:], ALU.add))
    chain.link(nc.vector.tensor_scalar(r[:], r[:], guard[1], None, guard[0]))
    chain.link(nc.vector.reciprocal(r[:], r[:]))
    chain.link(nc.vector.tensor_tensor(v1[:], v1[:], r[:], ALU.mult))
    chain.link(nc.vector.tensor_tensor(v2[:], v2[:], r[:], ALU.mult))
    chain.link(nc.vector.tensor_tensor(cand[:], first[:], wide(v1), ALU.mult))
    chain.link(nc.vector.tensor_tensor(k.wts[:], second[:], wide(v2), ALU.mult))
    chain.link(nc.vector.tensor_tensor(k.wts[:], k.wts[:], cand[:], ALU.add))


def phase_gating(k, layer, w_name, guard, loads, splits):
    nc, ins = k.nc, k.ins
    tag = f"g{layer}"
    s_w, s_var, s_std, s_chain, s_xn, s_xT, s_hT, s_logit, s_shift, s_exp, s_prim = k.sems(
        tag, "w var std chain xn xT hT logit shift exp prim")
    s_high, s_low, s_parts, s_wT, s_wTs = k.sems(tag + "b", "high low parts wT wTs")
    with ExitStack() as ph:
        def tmp(name, shape):
            return ph.enter_context(nc.sbuf_tensor(f"{tag}_{name}", shape, F32))
        w_gate = tmp("w_gate", [P, E])
        scr = {n: tmp(n, [P, T, E]) for n in ("p", "first", "second", "cand")}
        scr |= {n: tmp(n, [P, T]) for n in ("v1", "v2", "r")}
        p_x = psum(nc, ph, f"{tag}_px", 2)
        p_l = psum(nc, ph, f"{tag}_pl", 1)[0]
        p_c = psum(nc, ph, f"{tag}_pc", 1)[0]
        p_w = psum(nc, ph, f"{tag}_pw", 2)
        parts = tmp("parts", [P, T, 2 * E])
        mine = [(w_gate[:], ins[w_name])]
        if layer == 0:
            sim = tmp("sim", [P, E, E])
            used, prim, best, move = tmp("used", [P, E]), tmp("prim", [P, E]), tmp("best", [P, E]), tmp("move", [P, E])
            eq, far = tmp("eq", [P, E, E]), tmp("far", [P, E])
            route, routeT = tmp("route", [P, E, E]), tmp("routeT", [P, E, E])
            spread = tmp("spread", [P, T, E, E])
            mine.append((sim[:], bass.AP(ins["L0_ffn_similarity_matrix"].tensor, 0, [[0, P], [E, E], [1, E]])))
        with nc.Block() as block:
            @block.sync
            def _(sp):
                for dst, src in mine:
                    sp.dma_start(dst, src).then_inc(s_w, 16)
                for dst, src, s in loads:
                    sp.dma_start(dst, src).then_inc(s, 16)

            @block.scalar
            def _(act):
                k.norm_act(act, s_var, s_std)
                for g in range(G):
                    act.wait_ge(s_xT, g + 1)
                    k.modulate(k.HT[:, g * GN:(g + 1) * GN], p_x[g % 2][:, :], layer, 1, g // BG).then_inc(s_hT, 1)
                    for whole, high, _, s, value in splits[g * len(splits) // G:(g + 1) * len(splits) // G]:
                        act.wait_ge(s, value)
                        nc.scalar.activation(high, whole, ACT.Copy).then_inc(s_high, 1)
                act.wait_ge(s_shift, 1)
                nc.scalar.activation(scr["p"][:], scr["p"][:], ACT.Exp).then_inc(s_exp, 1)
                for g in range(G):
                    act.wait_ge(s_wT, g + 1)
                    nc.scalar.activation(k.WT[:, g * GN:(g + 1) * GN], p_w[g % 2][0:2 * E, :], ACT.Copy).then_inc(s_wTs, 1)

            @block.gpsimd
            def _(pool):
                for i, (whole, high, low, _, _) in enumerate(splits):
                    pool.wait_ge(s_high, i + 1)
                    nc.gpsimd.tensor_tensor(low, whole, high, ALU.subtract).then_inc(s_low, 1)

            @block.tensor
            def _(pe):
                pe.wait_ge(s_w, 16 * len(mine))

                def logits(g):
                    pe.wait_ge(s_hT, g + 1)
                    for t in range(g * GT, (g + 1) * GT):
                        last = nc.tensor.matmul(p_l[:, t * E:(t + 1) * E], k.HT[:, t * P:(t + 1) * P], w_gate[:], start=True, stop=True)
                    last.then_inc(s_logit, 1)

                for g in range(G):
                    pe.wait_ge(s_xn, g + 1)
                    wait_pos(pe, s_hT, g - 1)
                    k.transpose_group(p_x[g % 2], g % 2).then_inc(s_xT, 1)
                    if g:
                        logits(g - 1)
                logits(G - 1)
                if layer == 0:
                    pe.wait_ge(s_prim, 1)
                    nc.tensor.matmul(p_c[:, 0:E], k.ones[:], used[:], start=True, stop=True).then_inc(s_prim, 1)
                pe.wait_ge(s_parts, 2)
                for g in range(G):
                    wait_pos(pe, s_wTs, g - 1)
                    for t in range(GT):
                        last = nc.tensor.transpose(p_w[g % 2][0:2 * E, t * P:(t + 1) * P], parts[:, g * GT + t, :], k.ident[:])
                    last.then_inc(s_wT, 1)

            @block.vector
            def _(dve):
                chain = Chain(dve, s_chain)
                k.norm_dve(dve, chain, s_var, s_std)
                for g in range(G):
                    wait_pos(dve, s_xT, g - 1)
                    for t in range(GT):
                        last = k.normalise(g * GT + t, t, g % 2)
                    last.then_inc(s_xn, 1)
                dve.wait_ge(s_logit, G)
                chain.link(nc.vector.tensor_copy(scr["p"][:], p_l[:, 0:T * E].rearrange("p (t e) -> p t e", e=E)))
                top_two(k, dve, chain, (s_shift, s_exp), scr, guard)

                def split_weights():
                    high = parts[:, :, 0:E].bitcast(F32R)
                    nc.vector.tensor_copy(high, k.wts[:]).then_inc(s_parts, 1)
                    dve.wait_ge(s_parts, 1)
                    nc.vector.tensor_tensor(parts[:, :, E:2 * E], k.wts[:], high, ALU.subtract).then_inc(s_parts, 1)

                if layer:
                    split_weights()
                    return
                chain.wait()
                nc.vector.tensor_reduce(used[:], scr["first"][:].rearrange("p t e -> p e t"), AX_X, ALU.max).then_inc(s_prim, 1)
                dve.wait_ge(s_prim, 2)
                chain.link(nc.vector.tensor_scalar(prim[:], p_c[:, 0:E], 0.5, None, ALU.is_gt))
                chain.link(nc.vector.tensor_scalar(far[:], prim[:], -1.0, NEG, ALU.add, ALU.mult))
                dve.wait_ge(s_w, 16 * len(mine))
                columns = prim[:].unsqueeze(1).broadcast_to([P, E, E])
                chain.link(nc.vector.tensor_tensor(sim[:], sim[:], columns, ALU.mult))
                chain.link(nc.vector.tensor_tensor(sim[:], sim[:], far[:].unsqueeze(1).broadcast_to([P, E, E]), ALU.add))
                chain.link(nc.vector.tensor_reduce(best[:], sim[:], AX_X, ALU.max))
                rank = k.rank[:].unsqueeze(1).broadcast_to([P, E, E])
                chain.link(nc.vector.tensor_tensor(eq[:], sim[:], best[:].unsqueeze(2).broadcast_to([P, E, E]), ALU.is_equal))
                chain.link(nc.vector.tensor_tensor(eq[:], eq[:], rank, ALU.mult))
                chain.link(nc.vector.tensor_reduce(far[:], eq[:], AX_X, ALU.max))
                chain.link(nc.vector.tensor_tensor(route[:], far[:].unsqueeze(2).broadcast_to([P, E, E]), rank, ALU.is_equal))
                chain.link(nc.vector.tensor_scalar(move[:], best[:], SIM_MIN, None, ALU.is_ge))
                chain.link(nc.vector.tensor_scalar(prim[:], prim[:], -1.0, 1.0, ALU.mult, ALU.add))
                chain.link(nc.vector.tensor_tensor(move[:], move[:], prim[:], ALU.mult))
                chain.link(nc.vector.tensor_tensor(route[:], route[:], k.eye8[:], ALU.subtract))
                chain.link(nc.vector.tensor_tensor(route[:], route[:], move[:].unsqueeze(2).broadcast_to([P, E, E]), ALU.mult))
                chain.link(nc.vector.tensor_tensor(route[:], route[:], k.eye8[:], ALU.add))
                chain.link(nc.vector.tensor_copy(routeT[:], route[:].rearrange("p i j -> p j i")))
                chain.link(nc.vector.tensor_tensor(spread[:], k.wts[:].unsqueeze(2).broadcast_to([P, T, E, E]),
                                                   routeT[:].unsqueeze(1).broadcast_to([P, T, E, E]), ALU.mult))
                chain.link(nc.vector.tensor_reduce(k.wts[:], spread[:], AX_X, ALU.add))
                split_weights()


def by_groups(eng, step):
    step(0, 0, False)
    with eng.Fori(0, B - 1) as base:
        for c in range(1, BG + 1):
            step(base, c, False)
    step(B - 1, 1, True)


def product3(nc, out, lhs, rhs, start=True, stop=True):
    (lh, ll), (rh, rl) = lhs, rhs
    nc.tensor.matmul(out, lh, rh, start=start, stop=False)
    nc.tensor.matmul(out, lh, rl, start=False, stop=False)
    return nc.tensor.matmul(out, ll, rh, start=False, stop=stop)


def split_input(k, dve, s_x, x, w_rows, g):
    h = k.HT[:, ds(g * GN, GN)]
    k.nc.vector.tensor_scalar(x[:, 0, :], h, 1.0, None, ALU.mult).then_inc(s_x, 1)
    dve.wait_ge(s_x, 2 * g + 1)
    k.nc.vector.tensor_tensor(x[:, 1, :], h, x[:, 0, :], ALU.subtract)
    k.nc.vector.tensor_scalar(w_rows, k.WT[:, ds(g * GN, GN)], 1.0, None, ALU.mult).then_inc(s_x, 1)


def phase_experts0(k, w_gu, w_down):
    nc = k.nc
    s_chain, s_x, s_gu, s_silu, s_t, s_mid, s_high, s_low, s_y, s_yT, s_turn, s_gated, s_res = k.sems(
        "x0", "chain x gu silu t mid high low y yT turn gated res")
    with ExitStack() as ph:
        def tmp(name, shape, dt=F32):
            return ph.enter_context(nc.sbuf_tensor(name, shape, dt))
        x = tmp("x0_parts", [P, 2, 2, GN], F32R)
        w_rows = tmp("w0_rows", [2 * E, 2, GN], F32R)
        gate_s, mid = tmp("gate_s", [P, 2, GN]), tmp("mid", [P, 2, GN])
        mid_parts = tmp("mid_parts", [P, 2, 2, GN], F32R)
        yT = tmp("yT0", [P, GN])
        p_g, p_u, p_w = psum(nc, ph, "p_g", 2), psum(nc, ph, "p_u", 2), psum(nc, ph, "p_w0", 2)
        p_y, p_t = psum(nc, ph, "p_y0", 1)[0], psum(nc, ph, "p_t0", 1)[0]
        stat_steps = 2 * GT + 1

        def first(g):
            return isinstance(g, int) and g == 0

        with nc.Block() as block:
            @block.scalar
            def _(act):
                def high(n, slot):
                    act.wait_ge(s_mid, n + 1)
                    nc.scalar.activation(mid_parts[:, slot, 0, :], mid[:, slot, :], ACT.Copy).then_inc(s_high, 1)

                def out_of_psum(g):
                    act.wait_ge(s_y, (g + 1) * E)
                    nc.scalar.activation(yT[:], p_y[:, :], ACT.Copy).then_inc(s_yT, 1)

                def step(base, c, last):
                    g = base * BG + c
                    for e in range(E):
                        n = g * E + e
                        act.wait_ge(s_gu, n + 1)
                        wait_pos(act, s_mid, n - 1)
                        nc.scalar.activation(gate_s[:, e % 2, :], p_g[e % 2][:, :], ACT.Silu).then_inc(s_silu, 1)
                        if e or not first(g):
                            high(n - 1, (e + 1) % 2)
                        if e == 1 and not first(g):
                            out_of_psum(g - 1)

                by_groups(act, step)
                act.wait_ge(s_y, G * E - 2)
                high(G * E - 1, 1)
                out_of_psum(G - 1)

            @block.tensor
            def _(pe):
                def project(g, c, e):
                    n = g * E + e
                    wait_pos(pe, s_silu, n - 1)
                    wait_pos(pe, s_mid, n - 1)
                    if e == 0:
                        pe.wait_ge(s_x, 2 * g + 2)
                    xs = (x[:, c % 2, 0, :], x[:, c % 2, 1, :])
                    nc.tensor.matmul(p_w[e % 2][:, :], k.pick[:, e, :], w_rows[:, c % 2, :], start=True, stop=True)
                    for p, at in ((p_g, 0), (p_u, P)):
                        ws = (w_gu[0][:, e, at:at + P], w_gu[1][:, e, at:at + P])
                        last = product3(nc, p[e % 2][:, :], ws, xs)
                    last.then_inc(s_gu, 1)

                def down(g, e):
                    n = g * E + e
                    pe.wait_ge(s_low, n + 1)
                    if e == 0:
                        wait_pos(pe, s_yT, g)
                    ws = (w_down[0][:, e, :], w_down[1][:, e, :])
                    last = product3(nc, p_y[:, :], ws, (mid_parts[:, e % 2, 0, :], mid_parts[:, e % 2, 1, :]), e == 0, e == E - 1)
                    last.then_inc(s_y, 1)

                def turn(g):
                    pe.wait_ge(s_yT, g + 1)
                    for t in range(GT):
                        last = nc.tensor.transpose(p_t[:, t * P:(t + 1) * P], yT[:, t * P:(t + 1) * P], k.ident[:])
                    last.then_inc(s_turn, 1)

                def step(base, c, last):
                    g = base * BG + c
                    for e in range(E):
                        project(g, c, e)
                        if e >= 2:
                            down(g, e - 2)
                        elif not first(g):
                            down(g - 1, E - 2 + e)
                        if e == 3 and not first(g):
                            turn(g - 1)

                by_groups(pe, step)
                down(G - 1, E - 2)
                down(G - 1, E - 1)
                turn(G - 1)

            @block.gpsimd
            def _(pool):
                with pool.Fori(0, G) as g:
                    pool.wait_ge(s_gated, g + 1)
                    k.add_gated(g * GT, 0, nc.gpsimd).then_inc(s_res, 1)

            @block.vector
            def _(dve):
                def low(n, slot):
                    dve.wait_ge(s_high, n + 1)
                    nc.vector.tensor_tensor(mid_parts[:, slot, 1, :], mid[:, slot, :], mid_parts[:, slot, 0, :],
                                            ALU.subtract).then_inc(s_low, 1)

                def gate(g, b):
                    dve.wait_ge(s_turn, g + 1)
                    k.gate(p_t[:, :].rearrange("p (t d) -> p t d", t=GT), 0, 1, b).then_inc(s_gated, 1)

                def stats(g):
                    chain = Chain(dve, s_chain, g * stat_steps)
                    dve.wait_ge(s_res, g + 1)
                    k.stats(chain, g * GT, True)
                    assert chain.n == stat_steps

                def step(base, c, last):
                    g = base * BG + c
                    for e in range(E):
                        n = g * E + e
                        dve.wait_ge(s_silu, n + 1)
                        nc.vector.tensor_tensor(gate_s[:, e % 2, :], gate_s[:, e % 2, :], p_w[e % 2][:, :], ALU.mult).then_inc(s_t, 1)
                        if e or not first(g):
                            low(n - 1, (e + 1) % 2)
                        dve.wait_ge(s_t, n + 1)
                        nc.vector.tensor_tensor(mid[:, e % 2, :], gate_s[:, e % 2, :], p_u[e % 2][:, :], ALU.mult).then_inc(s_mid, 1)
                        if not first(g):
                            if e == 4:
                                gate(g - 1, base + (c - 1) // BG)
                            if e == 6:
                                stats(g - 1)
                        if e == 5 and not last:
                            split_input(k, dve, s_x, x[:, (c + 1) % 2], w_rows[:, (c + 1) % 2, :], g + 1)

                split_input(k, dve, s_x, x[:, 0], w_rows[:, 0, :], 0)
                by_groups(dve, step)
                low(G * E - 1, 1)
                gate(G - 1, B - 1)
                stats(G - 1)
                dve.wait_ge(s_chain, G * stat_steps)


def phase_qkv(k, V, q_dram, k_dram):
    nc, ins = k.nc, k.ins
    s_w, s_var, s_std, s_chain, s_xn, s_xT, s_hT, s_proj, s_full, s_rest, s_v, s_vs, s_split = k.sems(
        "qkv", "w var std chain xn xT hT proj full rest v vs split")
    s_store = k.sems("qkv_store", "0 1")
    with ExitStack() as ph:
        def tmp(name, shape, dt=F32):
            return ph.enter_context(nc.sbuf_tensor(name, shape, dt))
        w = {n: tmp(f"w_{n}", [P, D]) for n in "qkv"}
        bias = tmp("bias_qk", [P, 2])
        b_v = tmp("b_v", [P, D])
        full = tmp("full", [P, 2, 2, GN])
        part = tmp("part", [P, 2, 2, 3, S], BF16)
        p_x = psum(nc, ph, "q_px", 2)
        p_q, p_k, p_v = psum(nc, ph, "p_q", 2), psum(nc, ph, "p_k", 2), psum(nc, ph, "p_v", 2)
        loads = [(w[n][:], ins[f"L1_attn_{n}_wT"]) for n in "qkv"]
        loads += [(bias[:, i:i + 1], ins[f"L1_attn_{n}_b"].unsqueeze(1)) for i, n in enumerate("qk")]
        loads += [(b_v[:], row_of(ins["L1_attn_v_b"], D))]
        scale = 1.0 / math.sqrt(DH)
        stores = 2 * TERMS * 16

        def part_of(g, i, n):
            return part[:, g // BG % 2, i, n, (g % BG) * GN:(g % BG + 1) * GN]

        with nc.Block() as block:
            @block.sync
            def _(sp):
                for dst, src in loads:
                    sp.dma_start(dst, src).then_inc(s_w, 16)
                for b in range(B):
                    for i, (dram, order) in enumerate(((q_dram, Q_PARTS), (k_dram, K_PARTS))):
                        sp.wait_ge(s_split, 2 * ((b + 1) * BG - 1) + i + 1)
                        for t, n in enumerate(order):
                            sp.dma_start(dram[t][:, b * S:(b + 1) * S], part[:, b % 2, i, n, :]).then_inc(s_store[b % 2], 16)
                for slot in range(2):
                    sp.wait_ge(s_store[slot], stores * B // 2)

            @block.scalar
            def _(act):
                def norm_group(g):
                    wait_pos(act, s_xT, g - 1)
                    for t in range(GT):
                        last = k.normalise_act(g * GT + t, t, g % 2)
                    last.then_inc(s_xn, 1)

                def modulate(g):
                    act.wait_ge(s_xT, g + 1)
                    wait_pos(act, s_v, g - 1)
                    k.modulate(k.hT[:, g % 2, :], p_x[g % 2][:, :], 1, 0, g // BG).then_inc(s_hT, 1)

                k.norm_act(act, s_var, s_std)
                act.wait_ge(s_w, 16 * len(loads))
                act.wait_ge(s_chain, 3)
                norm_group(0)
                norm_group(1)
                modulate(0)
                for g in range(G):
                    if g + 1 < G:
                        modulate(g + 1)
                    if g + 2 < G:
                        norm_group(g + 2)
                    for i, (p, sc) in enumerate(((p_q, scale), (p_k, 1.0))):
                        act.wait_ge(s_proj, 2 * g + i + 1)
                        wait_pos(act, s_split, 2 * (g - 2) + i + 1)
                        if g % BG == 0:
                            wait_pos(act, s_store[g // BG % 2], stores * (g // BG // 2))
                        nc.scalar.activation(full[:, g % 2, i, :], p[g % 2][:, :], ACT.Identity, scale=sc, bias=bias[:, i:i + 1])
                        nc.scalar.activation(part_of(g, i, 0), p[g % 2][:, :], ACT.Identity, scale=sc, bias=bias[:, i:i + 1]).then_inc(s_full, 1)

            @block.tensor
            def _(pe):
                def turn(g):
                    pe.wait_ge(s_xn, g + 1)
                    wait_pos(pe, s_hT, g - 1)
                    k.transpose_group(p_x[g % 2], g % 2).then_inc(s_xT, 1)

                pe.wait_ge(s_w, 16 * len(loads))
                turn(0)
                for g in range(G):
                    if g + 1 < G:
                        turn(g + 1)
                    pe.wait_ge(s_hT, g + 1)
                    wait_pos(pe, s_full, 2 * (g - 1))
                    for p, n in ((p_q, "q"), (p_k, "k")):
                        nc.tensor.matmul(p[g % 2][:, :], w[n][:], k.hT[:, g % 2, :], start=True, stop=True).then_inc(s_proj, 1)
                    wait_pos(pe, s_vs, g - 1)
                    for t in range(GT):
                        last = nc.tensor.matmul(p_v[g % 2][:, t * D:(t + 1) * D], k.hT[:, g % 2, t * P:(t + 1) * P], w["v"][:], start=True, stop=True)
                    last.then_inc(s_v, 1)

            @block.vector
            def _(dve):
                chain = Chain(dve, s_chain)
                k.norm_dve(dve, chain, s_var, s_std)
                dve.wait_ge(s_w, 16 * len(loads))
                chain.link(nc.vector.tensor_scalar(bias[:, 0:1], bias[:, 0:1], scale, None, ALU.mult))
                for g in range(G):
                    for i in range(2):
                        dve.wait_ge(s_full, 2 * g + i + 1)
                        x = full[:, g % 2, i, :]
                        nc.vector.tensor_tensor(x, x, part_of(g, i, 0), ALU.subtract).then_inc(s_rest, 1)
                    for i in range(2):
                        dve.wait_ge(s_rest, 2 * g + i + 1)
                        chain.add(nc.vector.tensor_copy(part_of(g, i, 1), full[:, g % 2, i, :]))
                    dve.wait_ge(s_v, g + 1)
                    nc.vector.tensor_tensor(V[:, g * GT:(g + 1) * GT, :], p_v[g % 2][:, :].rearrange("p (t d) -> p t d", t=GT),
                                            b_v[:].unsqueeze(1).broadcast_to([P, GT, D]), ALU.add).then_inc(s_vs, 1)
                    chain.wait()
                    for i in range(2):
                        nc.vector.tensor_tensor(part_of(g, i, 2), full[:, g % 2, i, :], part_of(g, i, 1), ALU.subtract).then_inc(s_split, 1)


def base_batch(base, c):
    return base + c // CYCLE


def run(eng, step):
    step(0, 0, False)
    with eng.Fori(0, B - 1) as base:
        for c in range(1, CYCLE + 1):
            step(base, c, False)
    for c in range(1, CYCLE):
        step(B - 1, c, True)


def phase_attention(k, V, C, q_dram, k_dram, bufs):
    nc = k.nc
    s_top, s_max, s_mparts, s_mT, s_mrows, s_mdma, s_qk, s_exp, s_v, s_pv, s_o, s_oT, s_c, s_chain, s_recip = k.sems(
        "at", "top max mparts mT mrows mdma qk exp v pv o oT c chain recip")
    s_slot = k.sems("at_slot", "0 1 2 3")
    Q, K, Vs, zero_rows = bufs
    with ExitStack() as ph:
        def tmp(name, shape, dt=F32):
            return ph.enter_context(nc.sbuf_tensor(name, shape, dt))
        prob = tmp("prob", [P, 2, 4, GN])
        halfmax, top, rest = tmp("halfmax", [P, 2, TOPS]), tmp("top", [P, GT * 4]), tmp("rest", [P, GT * 4])
        mparts = tmp("mparts", [P, 2, GT, 12], BF16)
        mrows = tmp("mrows", [12, 2, GN], BF16)
        o_sb, recip = tmp("o_sb", [P, GN]), tmp("recip", [P, GT * 4])
        p_s = psum(nc, ph, "p_s", 2, 1024)
        p_m = psum(nc, ph, "p_m", 2)
        p_out = psum(nc, ph, "p_out", 1)[0]
        p_t = psum(nc, ph, "p_t", 1)[0]
        p_tb = p_t[:, :].bitcast(BF16)

        def quad(c):
            return (c % CYCLE) // 2

        with nc.Block() as block:
            @block.sync
            def _(sp):
                def fill(token0, c):
                    q = quad(c)
                    for par in range(2):
                        rows = slice(64 * par, 64 * par + SLOT)
                        for pair in range(2):
                            h = 4 * q + 2 * pair + par
                            sp.dma_start(Q[rows, q, pair, :], q_dram[:, h * DH:(h + 1) * DH, ds(token0, S)]).then_inc(s_slot[q], 16)
                            sp.dma_start(K[rows, q, pair, par, :], k_dram[:, h * DH:(h + 1) * DH, ds(token0, S)]).then_inc(s_slot[q], 16)
                        sp.dma_start(Q[64 * par + SLOT:64 * par + SROWS, q, :, :], zero_rows[:]).then_inc(s_slot[q], 16)

                def max_rows(base, c):
                    q, half = quad(c), c % 2
                    sp.wait_ge(s_mrows, base * CYCLE + c + 1)
                    for par in range(2):
                        for pair in range(2):
                            at = (par * 2 + pair) * 3
                            sp.dma_start(Q[64 * par + SLOT:64 * par + SROWS, q, pair, half * GN:(half + 1) * GN],
                                         mrows[at:at + 3, c % 2, :]).then_inc(s_mdma, 16)

                def step(base, c, last):
                    j = base * CYCLE + c
                    if c % 2 == 0 and (not last or c + 4 < CYCLE):
                        token0 = sp.snap(base_batch(base, c + 4) * S) if not isinstance(base, int) else base_batch(base, c + 4) * S
                        sp.wait_ge(s_qk, 2 * KT * j + 1)
                        fill(token0, c + 4)
                    if not last or c + 1 < CYCLE:
                        max_rows(base, c + 1)

                fill(0, 0)
                fill(0, 2)
                max_rows(0, 0)
                run(sp, step)
                sp.wait_ge(s_mdma, 64 * HALVES)

            @block.gpsimd
            def _(pool):
                def values(base, c):
                    b, q = base_batch(base, c), quad(c)
                    for h in range(4):
                        at = (4 * q + h) * DH
                        last = nc.gpsimd.tensor_copy(Vs[:, q % 2, :, h, 0:DH], V[:, ds(b * KT, KT), at:at + DH])
                    last.then_inc(s_v, 1)

                def step(base, c, last):
                    j = base * CYCLE + c
                    if c % 2 == 0 and (not last or c + 2 < CYCLE):
                        wait_pos(pool, s_pv, KT * j)
                        values(base, c + 2)

                values(0, 0)
                run(pool, step)

            @block.tensor
            def _(pe):
                def tops(base, c, n, first=0):
                    x = TOPS * (base * CYCLE + c) + n
                    q, half = quad(c), c % 2
                    tile, h, kh = n // 8, n // 2 % 4, n % 2
                    pair, par = h // 2, h % 2
                    at = half * GN + tile * P
                    if n == 0 and half == 0:
                        pe.wait_ge(s_slot[q], 160 * (base_batch(base, c) + 1))
                    wait_pos(pe, s_max, x - 1)
                    nc.tensor.matmul(p_m[n % 2][:, :], Q[:, q, pair, at:at + P], K[:, q, pair, par, kh * GN:(kh + 1) * GN],
                                     start=True, stop=True).then_inc(s_top, 1)

                def scores(base, c, kt, pair):
                    u = (base * CYCLE + c) * KT + kt
                    q, half = quad(c), c % 2
                    wait_pos(pe, s_exp, 2 * u + pair - 1)
                    for par in range(2):
                        last = nc.tensor.matmul(p_s[pair][:, par * GN:(par + 1) * GN], K[:, q, pair, par, kt * P:(kt + 1) * P],
                                                Q[:, q, pair, half * GN:(half + 1) * GN], start=True, stop=True)
                    last.then_inc(s_qk, 1)

                def weigh(base, c, kt, part):
                    u = (base * CYCLE + c) * KT + kt
                    if part == 0:
                        pe.wait_ge(s_exp, 2 * u + 2)
                    if kt == 0 and part == 0:
                        if c % 2 == 0:
                            pe.wait_ge(s_v, base * QUADS + c // 2 + 1)
                        wait_pos(pe, s_o, base * CYCLE + c)
                    for h in range(4):
                        last = nc.tensor.matmul(p_out[32 * h:32 * h + 32, part * HQ:(part + 1) * HQ], Vs[:, quad(c) % 2, kt, h, :],
                                                prob[:, kt % 2, h, part * HQ:(part + 1) * HQ], start=(kt == 0 and part == 0),
                                                stop=(kt == KT - 1), skip_group_check=True)
                    if part:
                        last.then_inc(s_pv, 1)

                def turn_max(base, c):
                    j = base * CYCLE + c
                    pe.wait_ge(s_mparts, j + 1)
                    wait_pos(pe, s_c, j - 2)
                    for t in range(GT):
                        last = nc.tensor.transpose(p_tb[0:12, t * P:(t + 1) * P], mparts[:, c % 2, t, :], k.identb[:])
                    last.then_inc(s_mT, 1)

                def turn_out(base, c, turned):
                    j = base * CYCLE + c
                    pe.wait_ge(s_o, j + 1)
                    pe.wait_ge(s_mrows, turned)
                    wait_pos(pe, s_c, j)
                    for t in range(GT):
                        last = nc.tensor.transpose(p_t[:, t * P:(t + 1) * P], o_sb[:, t * P:(t + 1) * P], k.ident[:])
                    last.then_inc(s_oT, 1)

                def step(base, c, last):
                    ahead = not last or c + 2 < CYCLE
                    pe.wait_ge(s_mdma, 64 * (base * CYCLE + c + 1))
                    for kt in range(KT):
                        for i in range(4):
                            if i < 2:
                                scores(base, c, kt, i)
                            elif kt or c:
                                weigh(base, c if kt else c - 1, (kt - 1) % KT, i - 2)
                            if ahead:
                                tops(base, c + 2, 4 * kt + i)
                        if kt == 1 and (not last or c + 1 < CYCLE):
                            turn_max(base, c + 1)
                        if kt == 3 and c:
                            turn_out(base, c - 1, base * CYCLE + c + 2 if not last or c + 1 < CYCLE else HALVES)

                for c in range(2):
                    for n in range(TOPS):
                        tops(0, c, n)
                    if c == 0:
                        turn_max(0, 0)
                run(pe, step)
                weigh(B - 1, CYCLE - 1, KT - 1, 0)
                weigh(B - 1, CYCLE - 1, KT - 1, 1)
                turn_out(B - 1, CYCLE - 1, HALVES)

            @block.scalar
            def _(act):
                def rows_out(base, c):
                    j = base * CYCLE + c
                    act.wait_ge(s_mT, j + 1)
                    wait_pos(act, s_mdma, 64 * (j - 1))
                    nc.scalar.activation(mrows[:, c % 2, :], p_tb[0:12, 0:GN], ACT.Copy).then_inc(s_mrows, 1)

                def evacuate(base, c):
                    j = base * CYCLE + c
                    act.wait_ge(s_pv, KT * (j + 1))
                    wait_pos(act, s_oT, j)
                    nc.scalar.activation(o_sb[:], p_out[:, :], ACT.Copy).then_inc(s_o, 1)

                def step(base, c, last):
                    for kt in range(KT):
                        u = (base * CYCLE + c) * KT + kt
                        if kt == 1 and c:
                            evacuate(base, c - 1)
                        wait_pos(act, s_pv, u - 1)
                        for pair in range(2):
                            act.wait_ge(s_qk, 2 * u + pair + 1)
                            nc.scalar.activation(prob[:, kt % 2, 2 * pair:2 * pair + 2, :],
                                                 p_s[pair][:, :].rearrange("p (h n) -> p h n", h=2), ACT.Exp).then_inc(s_exp, 1)
                        if kt == 2 and (not last or c + 1 < CYCLE):
                            rows_out(base, c + 1)

                rows_out(0, 0)
                run(act, step)
                evacuate(B - 1, CYCLE - 1)

            @block.vector
            def _(dve):
                steps = 4
                def tops(base, c, n):
                    x = TOPS * (base * CYCLE + c) + n
                    dve.wait_ge(s_top, x + 1)
                    nc.vector.tensor_reduce(halfmax[:, c % 2, n:n + 1], p_m[n % 2][:, :], AX_X, ALU.max).then_inc(s_max, 1)

                def parts(base, c):
                    j = base * CYCLE + c
                    dve.wait_ge(s_max, TOPS * (j + 1))
                    wait_pos(dve, s_mT, j - 1)
                    chain = Chain(dve, s_chain, j * steps)
                    chain.link(nc.vector.tensor_reduce(top[:], halfmax[:, c % 2, :].rearrange("p (n k) -> p n k", k=2), AX_X, ALU.max))
                    view = mparts[:, c % 2, :, :].rearrange("p t (par pair part) -> p t pair par part", par=2, pair=2)

                    def heads(x):
                        return x[:].rearrange("p (t pair par) -> p t pair par", t=GT, pair=2)
                    chain.link(nc.vector.tensor_copy(view[:, :, :, :, 0], heads(top)))
                    chain.link(nc.vector.tensor_tensor(heads(rest), heads(top), view[:, :, :, :, 0], ALU.subtract))
                    chain.link(nc.vector.tensor_copy(view[:, :, :, :, 1], heads(rest)))
                    nc.vector.tensor_tensor(view[:, :, :, :, 2], heads(rest), view[:, :, :, :, 1], ALU.subtract).then_inc(s_mparts, 1)

                def normalise(base, c):
                    j = base * CYCLE + c
                    dve.wait_ge(s_oT, j + 1)
                    o = p_t[:, :].rearrange("p (t h r) -> p t h r", t=GT, h=4)
                    nc.vector.reciprocal(recip[:].rearrange("p (t h) -> p t h", t=GT), o[:, :, :, DH]).then_inc(s_recip, 1)
                    dve.wait_ge(s_recip, j + 1)
                    tile0 = base_batch(base, c) * KT + (c % 2) * GT
                    at = quad(c) * 4 * DH
                    dst = C[:, ds(tile0, GT), at:at + 4 * DH].rearrange("p t (h d) -> p t h d", h=4)
                    nc.vector.tensor_tensor(dst, o[:, :, :, 0:DH],
                                            recip[:].rearrange("p (t h) -> p t h", t=GT).unsqueeze(3).broadcast_to([P, GT, 4, DH]),
                                            ALU.mult).then_inc(s_c, 1)

                def step(base, c, last):
                    if not last or c + 1 < CYCLE:
                        parts(base, c + 1)
                    for kt in range(KT):
                        if not last or c + 2 < CYCLE:
                            for n in range(4):
                                tops(base, c + 2, 4 * kt + n)
                        if kt == 5 and c:
                            normalise(base, c - 1)

                for c in range(2):
                    for n in range(TOPS):
                        tops(0, c, n)
                    if c == 0:
                        parts(0, 0)
                run(dve, step)
                normalise(B - 1, CYCLE - 1)


def phase_project(k, C, loads):
    nc, ins = k.nc, k.ins
    s_w, s_chain, s_cT, s_cTs, s_o, s_gated = k.sems("pr", "w chain cT cTs o gated")
    with ExitStack() as ph:
        def tmp(name, shape):
            return ph.enter_context(nc.sbuf_tensor(name, shape, F32))
        w_o, b_o = tmp("w_o1", [P, D]), tmp("b_o1", [1, D])
        p_c, p_o = psum(nc, ph, "p_c", 2), psum(nc, ph, "p_o1", 2)
        with nc.Block() as block:
            @block.sync
            def _(sp):
                sp.dma_start(w_o[:], ins["L1_attn_out_wT"]).then_inc(s_w, 16)
                sp.dma_start(b_o[:], ins["L1_attn_out_b"].unsqueeze(0)).then_inc(s_w, 16)
                for dst, src, s in loads:
                    sp.dma_start(dst, src).then_inc(s, 16)

            @block.scalar
            def _(act):
                for g in range(G):
                    act.wait_ge(s_cT, g + 1)
                    wait_pos(act, s_o, g - 1)
                    nc.scalar.activation(k.hT[:, g % 2, :], p_c[g % 2][:, :], ACT.Copy).then_inc(s_cTs, 1)

            @block.tensor
            def _(pe):
                def turn(g):
                    wait_pos(pe, s_cTs, g - 1)
                    for t in range(GT):
                        last = nc.tensor.transpose(p_c[g % 2][:, t * P:(t + 1) * P], C[:, g * GT + t, :], k.ident[:])
                    last.then_inc(s_cT, 1)

                def project(g):
                    pe.wait_ge(s_cTs, g + 1)
                    wait_pos(pe, s_gated, g - 1)
                    for t in range(GT):
                        o = p_o[g % 2][:, t * D:(t + 1) * D]
                        nc.tensor.matmul(o, k.ones[0:1, :], b_o[:], start=True, stop=False)
                        last = nc.tensor.matmul(o, k.hT[:, g % 2, t * P:(t + 1) * P], w_o[:], start=False, stop=True)
                    last.then_inc(s_o, 1)

                pe.wait_ge(s_w, 32)
                turn(0)
                for g in range(1, G):
                    turn(g)
                    project(g - 1)
                project(G - 1)

            @block.vector
            def _(dve):
                chain = Chain(dve, s_chain)
                for g in range(G):
                    dve.wait_ge(s_o, g + 1)
                    k.gate(p_o[g % 2][:, :].rearrange("p (t d) -> p t d", t=GT), 1, 0, g // BG).then_inc(s_gated, 1)
                    dve.wait_ge(s_gated, g + 1)
                    chain.link(k.add_gated(g * GT))
                    k.stats(chain, g * GT)
                    chain.wait()


def phase_experts1(k, w1, b1, w2, b2):
    nc = k.nc
    s_x, s_w, s_ws, s_up, s_gelu, s_low, s_y, s_mul, s_b, s_acc, s_turn, s_gated, s_res, s_out = k.sems(
        "x1", "x w ws up gelu low y mul b acc turn gated res out")
    out_v = k.out.rearrange("b (t p) d -> p (b t) d", p=P)
    with ExitStack() as ph:
        def tmp(name, shape, dt=F32):
            return ph.enter_context(nc.sbuf_tensor(name, shape, dt))
        x = tmp("x1_parts", [P, 2, 2, GN], F32R)
        w_rows = tmp("w1_rows", [2 * E, 2, GN], F32R)
        hid = tmp("hid", [P, FC, GN])
        hid_parts = tmp("hid_parts", [P, 2, 2, FC, GN], F32R)
        w_rep = tmp("w_rep", [P, 4, GN])
        weighted, acc = k.xn, k.hT
        p_h, p_y = psum(nc, ph, "p_h", 4), psum(nc, ph, "p_y1", 2)
        p_w, p_t = psum(nc, ph, "p_w1", 1)[0], psum(nc, ph, "p_t1", 1)[0]

        def first(g):
            return isinstance(g, int) and g == 0

        with nc.Block() as block:
            @block.sync
            def _(sp):
                with sp.Fori(0, G) as g:
                    sp.wait_ge(s_res, g + 1)
                    sp.dma_start(out_v[:, ds(g * GT, GT), :], k.X[:, ds(g * GT, GT), :]).then_inc(s_out, 16)
                sp.wait_ge(s_out, 16 * G)

            @block.scalar
            def _(act):
                def step(base, c, last):
                    for e in range(E):
                        n = (base * BG + c) * E + e
                        act.wait_ge(s_w, n + 1)
                        wait_pos(act, s_mul, n - 3)
                        nc.scalar.activation(w_rep[:, e % 4, :], p_w[:, :], ACT.Copy).then_inc(s_ws, 1)
                        wait_pos(act, s_y, n - 1)
                        for f in range(FC):
                            act.wait_ge(s_up, n * FC + f + 1)
                            wait_pos(act, s_low, (n - 1) * FC + f + 1)
                            nc.scalar.activation(hid[:, f, :], p_h[f][:, :], ACT.Gelu, bias=b1[:, e, f:f + 1])
                            nc.scalar.activation(hid_parts[:, e % 2, 0, f, :], p_h[f][:, :], ACT.Gelu, bias=b1[:, e, f:f + 1]).then_inc(s_gelu, 1)

                by_groups(act, step)

            @block.tensor
            def _(pe):
                def weight_row(g, c, e):
                    wait_pos(pe, s_ws, g * E + e)
                    nc.tensor.matmul(p_w[:, :], k.pick[:, e, :], w_rows[:, c % 2, :], start=True, stop=True).then_inc(s_w, 1)

                def up(g, c, e):
                    n = g * E + e
                    xs = (x[:, c % 2, 0, :], x[:, c % 2, 1, :])
                    for f in range(FC):
                        wait_pos(pe, s_gelu, (n - 1) * FC + f + 1)
                        cols = slice(f * P, (f + 1) * P)
                        product3(nc, p_h[f][:, :], (w1[0][:, e, cols], w1[1][:, e, cols]), xs).then_inc(s_up, 1)

                def second_biases(c):
                    nc.tensor.matmul(p_t[:, :], b2[0][:], w_rows[:, c % 2, :], start=True, stop=False)
                    nc.tensor.matmul(p_t[:, :], b2[1][0:E, :], w_rows[0:E, c % 2, :], start=False, stop=True).then_inc(s_b, 1)

                def down(n, e):
                    pe.wait_ge(s_low, (n + 1) * FC)
                    wait_pos(pe, s_mul, n - 1)
                    for f in range(FC):
                        hs = (hid_parts[:, e % 2, 0, f, :], hid_parts[:, e % 2, 1, f, :])
                        last = product3(nc, p_y[e % 2][:, :], (w2[0][:, e, f, :], w2[1][:, e, f, :]), hs, f == 0, f == FC - 1)
                    last.then_inc(s_y, 1)

                def turn(g, slot):
                    pe.wait_ge(s_acc, (g + 1) * E)
                    for t in range(GT):
                        last = nc.tensor.transpose(p_t[:, t * P:(t + 1) * P], acc[:, slot, t * P:(t + 1) * P], k.ident[:])
                    last.then_inc(s_turn, 1)

                def step(base, c, last):
                    g = base * BG + c
                    pe.wait_ge(s_x, 2 * g + 2)
                    for e in range(E):
                        weight_row(g, c, e)
                        up(g, c, e)
                        if e == 0:
                            second_biases(c)
                        if e or not first(g):
                            down(g * E + e - 1, (e - 1) % E)
                        if e == 3 and not first(g):
                            pe.wait_ge(s_acc, g * E + 1)
                            turn(g - 1, (c + 1) % 2)

                by_groups(pe, step)
                down(G * E - 1, E - 1)
                turn(G - 1, (G - 1) % 2)

            @block.vector
            def _(dve):
                def low(n, e, f):
                    dve.wait_ge(s_gelu, n * FC + f + 1)
                    nc.vector.tensor_tensor(hid_parts[:, e % 2, 1, f, :], hid[:, f, :], hid_parts[:, e % 2, 0, f, :],
                                            ALU.subtract).then_inc(s_low, 1)

                def weigh(n, e):
                    dve.wait_ge(s_ws, n + 1)
                    dve.wait_ge(s_y, n + 1)
                    wait_pos(dve, s_acc, n - 1)
                    nc.vector.tensor_tensor(weighted[:, e % 2, :], p_y[e % 2][:, :], w_rep[:, e % 4, :], ALU.mult).then_inc(s_mul, 1)

                def accumulate(g, e, acc_slot):
                    n = g * E + e
                    dve.wait_ge(s_mul, n + 1)
                    if e == 0:
                        dve.wait_ge(s_b, g + 1)
                    else:
                        dve.wait_ge(s_acc, n)
                    a = acc[:, acc_slot, :]
                    nc.vector.tensor_tensor(a, weighted[:, e % 2, :], p_t[:, :] if e == 0 else a, ALU.add).then_inc(s_acc, 1)

                def finish(g, b):
                    dve.wait_ge(s_turn, g + 1)
                    k.gate(p_t[:, :].rearrange("p (t d) -> p t d", t=GT), 1, 1, b).then_inc(s_gated, 1)
                    dve.wait_ge(s_gated, g + 1)
                    k.add_gated(g * GT).then_inc(s_res, 1)
                    dve.wait_ge(s_res, g + 1)

                def step(base, c, last):
                    g = base * BG + c
                    for e in range(E):
                        n = g * E + e
                        low(n, e, 0)
                        if e >= 2:
                            accumulate(g, e - 2, c % 2)
                        elif not first(g):
                            accumulate(g - 1, E - 2 + e, (c + 1) % 2)
                        for f in range(1, FC):
                            low(n, e, f)
                        if e or not first(g):
                            weigh(n - 1, (e - 1) % E)
                        if e == 4 and not first(g):
                            finish(g - 1, base + (c - 1) // BG)
                        if e == 5 and not last:
                            split_input(k, dve, s_x, x[:, (c + 1) % 2], w_rows[:, (c + 1) % 2, :], g + 1)

                split_input(k, dve, s_x, x[:, 0], w_rows[:, 0, :], 0)
                by_groups(dve, step)
                accumulate(G - 1, E - 2, (G - 1) % 2)
                weigh(G * E - 1, E - 1)
                accumulate(G - 1, E - 1, (G - 1) % 2)
                finish(G - 1, B - 1)


def build(nc, ins, out):
    with ExitStack() as ctx:
        k = Kernel(nc, ctx, ins, out)
        q_dram = nc.dram_tensor("q_parts", [TERMS, P, N], BF16).ap()
        k_dram = nc.dram_tensor("k_parts", [TERMS, P, N], BF16).ap()
        s_w0, s_w1 = k.sem("weights0"), k.sems("weights1", "up down")

        def tensor(stack, name, shape, dt=F32):
            return stack.enter_context(nc.sbuf_tensor(name, shape, dt))

        with ExitStack() as attn:
            bufs = (tensor(attn, "Q", [P, QUADS, 2, S], BF16),
                    tensor(attn, "K", [P, QUADS, 2, 2, S], BF16),
                    tensor(attn, "Vs", [P, 2, KT, 4, 32]),
                    tensor(attn, "zero_rows", [3, 2, S], BF16))
            V = tensor(attn, "V", [P, T, D])
            phase_setup(k, bufs)
            phase_linear_attention(k)
            with ExitStack() as mixture:
                w_gu = [tensor(mixture, f"w_gu_{n}", [P, E, 2 * P], F32R) for n in ("high", "low")]
                w_down = [tensor(mixture, f"w_down_{n}", [P, E, D], F32R) for n in ("high", "low")]
                with ExitStack() as whole:
                    gu, down = tensor(whole, "w_gu", [P, E, 2 * P]), tensor(whole, "w_down", [P, E, D])
                    pieces = [tuple(w[:, e:e + E // 2, :] for w in (gu, *w_gu)) + (s_w0, 32) for e in (0, E // 2)]
                    pieces += [(down[:], w_down[0][:], w_down[1][:], s_w0, 32)]
                    phase_gating(k, 0, "L0_ffn_gate_wT", (ALU.max, 1e-12),
                                 [(gu[:], ins["L0_ffn_gu"], s_w0), (down[:], ins["L0_ffn_down"], s_w0)], pieces)
                phase_experts0(k, w_gu, w_down)
            phase_qkv(k, V, q_dram, k_dram)
            C = k.HT[:].rearrange("p (t d) -> p t d", d=D)
            phase_attention(k, V, C, q_dram, k_dram, bufs)
        w1 = [k.sb(f"w1_{n}", [P, E, F1], F32R) for n in ("high", "low")]
        w2 = [k.sb(f"w2_{n}", [P, E, FC, D], F32R) for n in ("high", "low")]
        b2 = [k.sb(f"b2_{n}", [2 * E, D], F32R) for n in ("high", "low")]
        b1 = k.sb("b1", [P, E, FC])
        with ExitStack() as whole:
            up, down, bias = tensor(whole, "w1", [P, E, F1]), tensor(whole, "w2", [P, E, FC, D]), tensor(whole, "b2", [2 * E, D])
            b2_src = ins["L1_ffn_b2"]
            loads = [(up[:], ins["L1_ffn_W1"].rearrange("e d f -> d e f"), s_w1[0]), (b1[:], ins["L1_ffn_b1"], s_w1[0]),
                     (down[:], ins["L1_ffn_W2"].rearrange("e (c f) d -> f e c d", f=P), s_w1[1]),
                     (bias[0:E, :], b2_src, s_w1[1]), (bias[E:2 * E, :], b2_src, s_w1[1])]
            pieces = [tuple(w[:, e:e + 2, :] for w in (up, *w1)) + (s_w1[0], 32) for e in range(0, E, 2)]
            pieces += [tuple(w[:, e:e + 2] for w in (down, *w2)) + (s_w1[1], 48) for e in range(0, E, 2)]
            pieces += [(bias[:], b2[0][:], b2[1][:], s_w1[1], 48)]
            phase_project(k, C, loads)
            phase_gating(k, 1, "L1_ffn_Wg", (ALU.add, 1e-9), [], pieces)
        phase_experts1(k, w1, b1, w2, b2)


def kernel(**inputs):
    import numpy as np
    import concourse.bacc as bacc
    from concourse.bass_utils import run_bass_kernel_spmd

    a = {n: np.asarray(v) for n, v in inputs.items()}
    consts = np.concatenate([np.eye(P), np.kron(np.eye(H), np.ones((DH, DH))), np.tile(np.arange(E, 0, -1), (P, 1)),
                             np.tile(np.eye(E).reshape(1, -1), (P, 1))], axis=1).astype(np.float32)
    same = ["L0_attn_x", "L0_attn_Wq", "L0_attn_Wk", "L0_attn_Wv", "L0_attn_Wo", "L0_attn_bq", "L0_attn_bk", "L0_attn_bv", "L0_attn_bo",
            "L0_attn_m", "L0_ffn_similarity_matrix", "L0_wmod", "L1_attn_q_b", "L1_attn_k_b", "L1_attn_v_b", "L1_attn_out_b",
            "L1_ffn_Wg", "L1_ffn_W1", "L1_ffn_W2", "L1_ffn_b2", "L1_wmod"]
    laid = {n: a[n] for n in same} | {"consts": consts}
    laid |= {f"L1_attn_{n}_wT": a[f"L1_attn_{n}_w"].T for n in ("q", "k", "v", "out")}
    laid |= {f"L{i}_cT": a[f"L{i}_c"].T for i in range(2)}
    laid["L0_ffn_gate_wT"] = a["L0_ffn_gate_weight"].T
    laid["L0_ffn_gu"] = a["L0_ffn_gate_up_proj"].transpose(2, 0, 1)
    laid["L0_ffn_down"] = a["L0_ffn_down_proj"].transpose(2, 0, 1)
    laid["L1_ffn_b1"] = a["L1_ffn_b1"].reshape(E, FC, P).transpose(2, 0, 1)

    nc = bacc.Bacc("TRN2", target_bir_lowering=False, num_devices=1)
    arrays, aps = {}, {}
    for n, v in laid.items():
        arrays[f"in_{n}"] = np.ascontiguousarray(v)
        aps[n] = nc.dram_tensor(f"in_{n}", arrays[f"in_{n}"].shape, F32, kind="ExternalInput").ap()
    out = nc.dram_tensor("out", [B, S, D], F32, kind="ExternalOutput").ap()
    build(nc, aps, out)
    r = run_bass_kernel_spmd(nc, [arrays], core_ids=[0])
    return r.results[0]["out"]
```

```python
import math
from contextlib import ExitStack

import concourse.bass as bass
from concourse import mybir

ALU = mybir.AluOpType
ACT = mybir.ActivationFunctionType
AX_X = mybir.AxisListType.X
F32 = mybir.dt.float32
BF16 = mybir.dt.bfloat16
F32R = mybir.dt.float32r
U32 = mybir.dt.uint32

P = 128
B, S, D = 4, 1024, 128
H, DH = 16, 8
E = 8
F1 = 512
FC = F1 // P
N = B * S
T = N // P
GT = 4
GN = GT * P
G = T // GT
BG = S // GN
LN_EPS = 1e-5
SIM_MIN = 0.7
NEG = 3.0e38
QUADS = H // 4
TERMS = 6
SLOT = TERMS * DH
PART_TERMS = (((0, 1, 2), (4, 5), (3,)), ((2, 3, 4), (1, 5), (0,)))
SROWS = SLOT + 3
KT = S // P
HQ = GN // 2
HALVES = B * QUADS * 2
CYCLE = QUADS * 2
PART_SLOTS = 3
STORES = 2 * 3 * 16
TOPS = GT * 4 * 2
ds = bass.ds


class Chain:

    def __init__(self, eng, sem, base=0):
        self.eng, self.sem, self.base, self.n = eng, sem, base, 0

    def add(self, ins):
        ins.then_inc(self.sem, 1)
        self.n += 1

    def wait(self):
        self.eng.wait_ge(self.sem, self.base + self.n)

    def link(self, ins):
        self.add(ins)
        self.wait()


def wait_pos(eng, sem, value):
    if not (isinstance(value, int) and value <= 0):
        eng.wait_ge(sem, value)


class Kernel:

    def __init__(self, nc, ctx, ins, out):
        self.nc, self.ctx, self.ins, self.out = nc, ctx, ins, out
        self.X = self.sb("X", [P, T, D])
        self.HT = self.sb("HT", [P, N])
        self.MV = self.sb("MV", [P, T, 2])
        self.bstats = self.sb("bstats", [P, GT, 6])
        self.std = self.sb("std", [P, T])
        self.rstd = self.sb("rstd", [P, T])
        self.nmr = self.sb("nmr", [P, T])
        self.xn = self.sb("xn", [P, 2, GN])
        self.hT = self.sb("hT", [P, 2, GN])
        self.mv4 = self.sb("mv4", [P, GT, 2])
        self.kvmask = self.sb("kvmask", [P, P])
        self.mark = self.sb("mark", [P, 1])
        self.spare = self.sb("spare", [1, 1])
        self.gated = self.sb("gated", [P, 2, GT, D])
        self.ident = self.sb("ident", [P, P])
        self.identb = self.sb("identb", [P, P], BF16)
        self.ones = self.sb("ones", [P, P])
        self.rank = self.sb("rank", [P, E])
        self.eye8 = self.sb("eye8", [P, E, E])
        self.pick = self.sb("pick", [2 * E, E, P], F32R)
        self.WT = self.sb("WT", [2 * E, N], F32R)
        self.modv = self.sb("modv", [P, 2, 4, B])
        self.gate_row = self.sb("gate_row", [P, 2, B, 2, D])
        self.wts = self.sb("wts", [P, T, E])

    def sb(self, name, shape, dt=F32):
        return self.ctx.enter_context(self.nc.sbuf_tensor(name, shape, dt))

    def sem(self, name):
        return self.ctx.enter_context(self.nc.semaphore(name))

    def sems(self, tag, names):
        return [self.sem(f"{tag}_{n}") for n in names.split()]

    def stats(self, chain, tile0, loop=False):
        nc = self.nc
        if loop:
            nc.vector.memset(self.mark[:], 0.0)
        for t in range(GT):
            chain.add(nc.vector.bn_stats(self.bstats[:, t, :], self.X[:, tile0 + t, :] if not loop else
                                         self.X[:, ds(tile0 + t, 1), :].rearrange("p o d -> p (o d)")))
        chain.wait()
        if loop:
            nc.vector.memset(self.mark[:], 0.0)
        for t in range(GT):
            chain.add(nc.vector.bn_aggr(self.mv4[:, t, :] if loop else self.MV[:, tile0 + t, :], self.bstats[:, t, :]))
        if loop:
            chain.wait()
            chain.link(nc.vector.tensor_scalar(self.MV[:, ds(tile0, GT), :], self.mv4[:], 1.0, None, ALU.mult))

    def norm_dve(self, dve, chain, s_var, s_std):
        nc = self.nc
        nc.vector.tensor_scalar(self.std[:], self.MV[:, :, 1], LN_EPS, None, ALU.add).then_inc(s_var, 1)
        dve.wait_ge(s_std, 1)
        chain.link(nc.vector.reciprocal(self.rstd[:], self.std[:]))
        chain.link(nc.vector.scalar_tensor_tensor(out=self.nmr[:], in0=self.MV[:, :, 0], scalar=-1.0, in1=self.rstd[:],
                                                  op0=ALU.mult, op1=ALU.mult))

    def load_table(self, func):
        self.nc.scalar.activation(self.spare[:], self.spare[:], func)

    def norm_act(self, act, s_var, s_std):
        self.load_table(ACT.Sqrt)
        act.wait_ge(s_var, 1)
        self.nc.scalar.activation(self.std[:], self.std[:], ACT.Sqrt).then_inc(s_std, 1)

    def normalise(self, tile, t, slot):
        return self.nc.vector.tensor_scalar(self.xn[:, slot, t * P:(t + 1) * P], self.X[:, tile, :], self.rstd[:, tile:tile + 1],
                                            self.nmr[:, tile:tile + 1], ALU.mult, ALU.add)

    def normalise_pool(self, tile, t, slot):
        return self.nc.gpsimd.tensor_scalar(self.xn[:, slot, t * P:(t + 1) * P], self.X[:, tile, :], self.rstd[:, tile:tile + 1],
                                            self.nmr[:, tile:tile + 1], ALU.mult, ALU.add)

    def normalise_act(self, tile, t, slot):
        return self.nc.scalar.activation(self.xn[:, slot, t * P:(t + 1) * P], self.X[:, tile, :], ACT.Identity,
                                         scale=self.rstd[:, tile:tile + 1], bias=self.nmr[:, tile:tile + 1])

    def transpose_group(self, dst, slot):
        for t in range(GT):
            last = self.nc.tensor.transpose(dst[:, t * P:(t + 1) * P], self.xn[:, slot, t * P:(t + 1) * P], self.ident[:])
        return last

    def modulate(self, dst, src, layer, which, b):
        return self.nc.scalar.activation(dst, src, ACT.Identity, scale=self.modv[:, layer, 2 * which + 1, ds(b, 1)],
                                         bias=self.modv[:, layer, 2 * which, ds(b, 1)])

    def gate(self, y, layer, which, b, slot=0):
        g = self.gate_row[:, layer, ds(b, 1), which, :].broadcast_to([P, GT, D])
        return self.nc.vector.tensor_tensor(self.gated[:, slot], y, g, ALU.mult)

    def add_gated(self, tile0, slot=0, eng=None):
        x = self.X[:, ds(tile0, GT), :]
        return (eng or self.nc.vector).tensor_tensor(x, x, self.gated[:, slot], ALU.add)


def psum(nc, stack, name, n, cols=512):
    return [stack.enter_context(nc.psum_tensor(f"{name}{i}", [P, cols], F32)) for i in range(n)]


def row_of(ap, n):
    return bass.AP(ap.tensor, 0, [[0, P], [1, n]])


def phase_setup(k):
    nc, ins = k.nc, k.ins
    s_load, s_chain, s_silu, s_spread, s_sig, s_mod = k.sems("set", "load chain silu spread sig mod")
    s_x, s_spare = k.sems("set_x", "0 1"), k.sem("set_spare")
    with ExitStack() as ph:
        def tmp(name, shape):
            return ph.enter_context(nc.sbuf_tensor(name, shape, F32))
        wmod = [tmp(f"wmod{i}", [P, 6 * D]) for i in range(2)]
        cT, cs, cspread = tmp("cT", [P, 2, B]), tmp("cs", [P, 2, B]), tmp("cspread", [P, 2 * B, P])
        headmask, m_col, m_sig = tmp("headmask", [P, P]), tmp("m_col", [P, 1]), tmp("m_sig", [P, 2])
        p_col = psum(nc, ph, "p_col", 1)[0]
        p_row = psum(nc, ph, "p_row", 4)
        consts = ins["consts"]
        loads = [(cT[:, 0, :], ins["L0_cT"]), (cT[:, 1, :], ins["L1_cT"]),
                 (wmod[0][:], ins["L0_wmod"]), (wmod[1][:], ins["L1_wmod"]),
                 (k.ident[:], consts[:, 0:P]), (headmask[:], consts[:, P:2 * P]), (k.rank[:], consts[:, 2 * P:2 * P + E]),
                 (k.eye8[:], consts[:, 2 * P + E:2 * P + E + E * E].rearrange("p (i j) -> p i j", i=E)),
                 (m_col[:], bass.AP(ins["L0_attn_m"].tensor, 0, [[1, H], [0, DH], [1, 1]]))]
        xv = ins["L0_attn_x"].rearrange("b (t p) d -> p (b t) d", p=P)
        halves = [slice(i * T // 2, (i + 1) * T // 2) for i in range(2)]
        with nc.Block() as block:
            @block.sync
            def _(sp):
                for dst, src in loads:
                    sp.dma_start(dst, src).then_inc(s_load, 16)
                for half, s in zip(halves, s_x):
                    sp.dma_start(k.X[:, half, :], xv[:, half, :]).then_inc(s, 16)

            @block.scalar
            def _(act):
                act.wait_ge(s_spare, 1)
                k.load_table(ACT.Silu)
                act.wait_ge(s_load, 16 * len(loads))
                nc.scalar.activation(cs[:], cT[:], ACT.Silu).then_inc(s_silu, 1)
                nc.scalar.activation(m_sig[:, 0:1], m_col[:], ACT.Sigmoid).then_inc(s_sig, 1)
                act.wait_ge(s_sig, 1)
                nc.scalar.activation(m_sig[:, 1:2], m_sig[:, 0:1], ACT.Exp, scale=-math.log(S)).then_inc(s_sig, 1)
                act.wait_ge(s_mod, 1)
                for i in range(4):
                    nc.scalar.activation(gate_rows(k, i), p_row[i][:, :], ACT.Copy)

            @block.tensor
            def _(pe):
                pe.wait_ge(s_silu, 1)
                for layer in range(2):
                    for i, j in enumerate((0, 1, 3, 4)):
                        at = (layer * 4 + i) * B
                        nc.tensor.matmul(p_col[:, at:at + B], wmod[layer][:, j * D:(j + 1) * D], cs[:, layer, :], start=True, stop=True)
                pe.wait_ge(s_spread, 1)
                for layer in range(2):
                    for b in range(B):
                        for i, j in enumerate((2, 5)):
                            at = (b % 2) * 2 * D + i * D
                            last = nc.tensor.matmul(p_row[layer * 2 + b // 2][:, at:at + D], cspread[:, layer * B + b, :],
                                                    wmod[layer][:, j * D:(j + 1) * D], start=True, stop=True)
                last.then_inc(s_mod, 1)

            @block.vector
            def _(dve):
                chain = Chain(dve, s_chain)
                nc.vector.memset(k.spare[:], 0.0).then_inc(s_spare, 1)
                chain.add(nc.vector.memset(k.ones[:], 1.0))
                dve.wait_ge(s_load, 16 * len(loads))
                chain.add(nc.vector.tensor_copy(k.identb[:], k.ident[:]))
                dve.wait_ge(s_silu, 1)
                nc.vector.tensor_copy(cspread[:], cs[:].rearrange("p l b -> p (l b)").unsqueeze(2).broadcast_to([P, 2 * B, P])).then_inc(s_spread, 1)
                for g in range(G):
                    if g % (G // 2) == 0:
                        dve.wait_ge(s_x[g // (G // 2)], 16)
                    chain.wait()
                    k.stats(chain, g * GT)
                dve.wait_ge(s_sig, 2)
                chain.add(nc.vector.tensor_scalar(k.kvmask[:], headmask[:], m_sig[:, 1:2], None, ALU.mult))
                dve.wait_ge(s_mod, 1)
                chain.link(nc.vector.tensor_copy(k.modv[:].rearrange("p l k b -> p (l k b)"), p_col[:, 0:2 * 4 * B]))
                for layer in range(2):
                    for i in (1, 3):
                        chain.add(nc.vector.tensor_scalar(k.modv[:, layer, i, :], k.modv[:, layer, i, :], 1.0, None, ALU.add))


def gate_rows(k, i):
    return k.gate_row[:, i // 2, (i % 2) * 2:(i % 2) * 2 + 2, :, :].rearrange("p b k d -> p (b k d)")


def bound_gates(k, chain, sign, size, i):
    nc, row = k.nc, gate_rows(k, i)
    chain.add(nc.vector.tensor_scalar(sign[:], row, 0.0, 2.0, ALU.is_ge, ALU.mult))
    chain.link(nc.vector.scalar_tensor_tensor(out=size[:], in0=row, scalar=-1.0, in1=row, op0=ALU.mult, op1=ALU.max))
    chain.link(nc.vector.tensor_scalar(size[:], size[:], 0.25, None, ALU.max))
    chain.link(nc.vector.scalar_tensor_tensor(out=row, in0=sign[:], scalar=-1.0, in1=size[:], op0=ALU.add, op1=ALU.mult))


def phase_linear_attention(k, bufs):
    nc, ins = k.nc, k.ins
    s_w, s_var, s_std, s_chain, s_xn, s_xT, s_hT, s_qkv, s_biased, s_sq, s_sum, s_root, s_unit = k.sems(
        "la", "w var std chain xn xT hT qkv biased sq sum root unit")
    s_kv, s_kvT, s_g, s_gm, s_qT, s_qTs, s_o, s_oT, s_back, s_gated, s_x = k.sems(
        "la2", "kv kvT g gm qT qTs o oT back gated x")
    s_zero = k.sem("la_zero")
    Q, K, Vs, zero_rows = bufs
    RING = 3
    with ExitStack() as ph:
        def tmp(name, shape):
            return ph.enter_context(nc.sbuf_tensor(name, shape, F32))
        w_qkv, b_qkv, w_o, b_o = tmp("w_qkv", [P, 3 * D]), tmp("b_qkv", [P, 3 * D]), tmp("w_o", [P, D]), tmp("b_o", [P, 1])
        qkv = tmp("qkv", [P, RING, GT, 3 * D])
        sq, norm, inv = tmp("sq", [P, 2, GT, 2 * D]), tmp("norm", [P, 2, GT * 2 * H]), tmp("inv", [P, GT * 2 * H])
        qT, kvT, kvo = tmp("qT", [P, GT, GN]), tmp("kvT", [P, P]), tmp("kvo", [P, P])
        oT, sign, size = tmp("oT", [P, GN]), tmp("sign", [P, GN]), tmp("size", [P, GN])
        p_x = psum(nc, ph, "p_x", 1)[0]
        p_qkv = psum(nc, ph, "p_qkv", 3)
        p_kv, p_kvo, p_qT, p_o = (psum(nc, ph, n, 1)[0] for n in ("p_kv", "p_kvo", "p_qT", "p_o"))
        loads = [(w_qkv[:, i * D:(i + 1) * D], ins[f"L0_attn_W{n}"]) for i, n in enumerate("qkv")]
        loads += [(b_qkv[:, i * D:(i + 1) * D], row_of(ins[f"L0_attn_b{n}"], D)) for i, n in enumerate("qkv")]
        loads += [(w_o[:], ins["L0_attn_Wo"]), (b_o[:], ins["L0_attn_bo"].unsqueeze(1))]
        with nc.Block() as block:
            @block.sync
            def _(sp):
                for dst, src in loads:
                    sp.dma_start(dst, src).then_inc(s_w, 16)

            @block.scalar
            def _(act):
                def norm_group(g):
                    wait_pos(act, s_xT, g - 1)
                    for t in range(GT):
                        last = k.normalise_act(g * GT + t, t, g % 2)
                    last.then_inc(s_xn, 1)

                def modulate(g):
                    act.wait_ge(s_xT, g + 1)
                    wait_pos(act, s_qkv, (g - 1) * GT)
                    k.modulate(k.hT[:, g % 2, :], p_x[:, :], 0, 0, g // BG).then_inc(s_hT, 1)

                def queries(g):
                    act.wait_ge(s_qT, g + 1)
                    wait_pos(act, s_o, g - GT + 1)
                    nc.scalar.activation(qT[:, g % GT, :], p_qT[:, :], ACT.Copy).then_inc(s_qTs, 1)

                k.norm_act(act, s_var, s_std)
                act.wait_ge(s_chain, 2)
                norm_group(0)
                modulate(0)
                norm_group(1)
                for i in range(G + 4):
                    if 1 <= i <= G:
                        g = i - 1
                        act.wait_ge(s_biased, (g + 1) * GT)
                        wait_pos(act, s_sum, g - 1)
                        nc.scalar.activation(sq[:, g % 2], qkv[:, g % RING, :, 0:2 * D], ACT.Square).then_inc(s_sq, 1)
                    if i >= 4:
                        g = i - 4
                        act.wait_ge(s_o, g + 1)
                        wait_pos(act, s_back, g)
                        nc.scalar.activation(oT[:], p_o[:, :], ACT.Identity, bias=b_o[:]).then_inc(s_oT, 1)
                    if 1 <= i <= G:
                        act.wait_ge(s_sum, i)
                        nc.scalar.activation(norm[:, (i - 1) % 2, :], norm[:, (i - 1) % 2, :], ACT.Sqrt).then_inc(s_root, 1)
                    if i + 1 < G:
                        modulate(i + 1)
                    if i + 2 < G:
                        norm_group(i + 2)
                    if 2 <= i < G + 2:
                        queries(i - 2)

            @block.tensor
            def _(pe):
                def turn(g):
                    pe.wait_ge(s_xn, g + 1)
                    wait_pos(pe, s_hT, g)
                    k.transpose_group(p_x, g % 2).then_inc(s_xT, 1)

                def project(g, tiles):
                    pe.wait_ge(s_hT, g + 1)
                    for t in tiles:
                        n = g * GT + t
                        wait_pos(pe, s_biased, n - 2)
                        nc.tensor.matmul(p_qkv[n % 3][:, 0:3 * D], k.hT[:, g % 2, t * P:(t + 1) * P], w_qkv[:],
                                         start=True, stop=True).then_inc(s_qkv, 1)

                def keys_values(g):
                    pe.wait_ge(s_unit, g + 1)
                    if g % BG == 0:
                        wait_pos(pe, s_kvT, g // BG)
                    for t in range(GT):
                        last = nc.tensor.matmul(p_kv[:, 0:P], qkv[:, g % RING, t, 2 * D:3 * D], qkv[:, g % RING, t, D:2 * D],
                                                start=(g % BG == 0 and t == 0), stop=(g % BG == BG - 1 and t == GT - 1))
                    last.then_inc(s_kv, 1)
                    wait_pos(pe, s_qTs, g)
                    for t in range(GT):
                        last = nc.tensor.transpose(p_qT[:, t * P:(t + 1) * P], qkv[:, g % RING, t, 0:D], k.ident[:])
                    last.then_inc(s_qT, 1)

                def fold_projection(b):
                    pe.wait_ge(s_kvT, b + 1)
                    wait_pos(pe, s_gm, b)
                    nc.tensor.matmul(p_kvo[:, 0:D], kvT[:], w_o[:], start=True, stop=True).then_inc(s_g, 1)

                def output(g):
                    pe.wait_ge(s_gm, g // BG + 1)
                    pe.wait_ge(s_qTs, g + 1)
                    wait_pos(pe, s_gated, g)
                    nc.tensor.matmul(p_o[:, :], kvo[:], qT[:, g % GT, :], start=True, stop=True).then_inc(s_o, 1)

                def back(g):
                    pe.wait_ge(s_oT, g + 1)
                    for t in range(GT):
                        last = nc.tensor.transpose(p_o[:, t * D:(t + 1) * D], oT[:, t * P:(t + 1) * P], k.ident[:])
                    last.then_inc(s_back, 1)

                turn(0)
                pe.wait_ge(s_w, 16 * len(loads))
                for i in range(G + 4):
                    if i + 1 < G:
                        turn(i + 1)
                    if i >= 4:
                        back(i - 4)
                    if i < G:
                        project(i, range(GT - 1))
                    if 3 <= i < G + 3 and i % BG == 1:
                        fold_projection((i - 3) // BG)
                    if 3 <= i < G + 3:
                        output(i - 3)
                    if i < G:
                        project(i, (GT - 1,))
                    if 1 <= i <= G:
                        keys_values(i - 1)

            @block.gpsimd
            def _(pool):
                chain = Chain(pool, s_zero)
                chain.link(nc.gpsimd.memset(K[:].bitcast(U32), 0))
                chain.link(nc.gpsimd.memset(Q[:].bitcast(U32), 0))
                chain.link(nc.gpsimd.memset(zero_rows[:].bitcast(U32), 0))
                chain.link(nc.gpsimd.memset(Vs[:], 1.0))
                for par in range(2):
                    chain.link(nc.gpsimd.memset(K[64 * par + 32:64 * par + 64, :, :, par, :], -1.0))
                for g in range(G):
                    pool.wait_ge(s_gated, g + 1)
                    k.add_gated(g * GT, g % 2, nc.gpsimd).then_inc(s_x, 1)

            @block.vector
            def _(dve):
                chain = Chain(dve, s_chain)
                k.norm_dve(dve, chain, s_var, s_std)
                dve.wait_ge(s_w, 16 * len(loads))
                for i in range(G + 5):
                    if 1 <= i <= 4:
                        bound_gates(k, chain, sign, size, i - 1)
                    if i >= 5:
                        dve.wait_ge(s_x, i - 4)
                        k.stats(chain, (i - 5) * GT)
                        chain.wait()
                    if 1 <= i <= G:
                        dve.wait_ge(s_sq, i)
                        nc.vector.tensor_reduce(norm[:, (i - 1) % 2, :], sq[:, (i - 1) % 2].rearrange("p t (h d) -> p (t h) d", d=DH),
                                                AX_X, ALU.add).then_inc(s_sum, 1)
                    fold = 3 <= i < G + 3 and i % BG == 1
                    if fold:
                        b = (i - 3) // BG
                        dve.wait_ge(s_kv, (b + 1) * BG)
                        wait_pos(dve, s_g, b)
                        nc.vector.tensor_tensor(kvT[:], p_kv[:, 0:P], k.kvmask[:], ALU.mult).then_inc(s_kvT, 1)
                    if 4 <= i < G + 4:
                        g = i - 4
                        dve.wait_ge(s_back, g + 1)
                        wait_pos(dve, s_x, g - 1)
                        chain.wait()
                        k.gate(p_o[:, :].rearrange("p (t d) -> p t d", t=GT), 0, 0, g // BG, g % 2).then_inc(s_gated, 1)
                    if fold:
                        dve.wait_ge(s_g, b + 1)
                        wait_pos(dve, s_o, b * BG)
                        nc.vector.tensor_copy(kvo[:], p_kvo[:, 0:D]).then_inc(s_gm, 1)
                    if 1 <= i <= G:
                        dve.wait_ge(s_root, i)
                        chain.link(nc.vector.tensor_scalar(inv[:], norm[:, (i - 1) % 2, :], 1e-12, None, ALU.max))
                        chain.link(nc.vector.reciprocal(inv[:], inv[:]))
                        qk = qkv[:, (i - 1) % RING, :, 0:2 * D].rearrange("p t (h d) -> p t h d", d=DH)
                        iv = inv[:].rearrange("p (t h) -> p t h", t=GT).unsqueeze(3).broadcast_to([P, GT, 2 * H, DH])
                        nc.vector.tensor_tensor(qk, qk, iv, ALU.mult).then_inc(s_unit, 1)
                    if i < G:
                        wait_pos(dve, s_qT, i - RING + 1)
                        for t in range(GT):
                            n = i * GT + t
                            dve.wait_ge(s_qkv, n + 1)
                            nc.vector.tensor_tensor(qkv[:, i % RING, t, :], p_qkv[n % 3][:, 0:3 * D], b_qkv[:], ALU.add).then_inc(s_biased, 1)


def top_two(k, dve, chain, logits, act_sems, scr, guard):
    nc = k.nc
    s_shift, s_exp = act_sems
    p, first, second, cand, v1, v2, r = (scr[n] for n in ("p", "first", "second", "cand", "v1", "v2", "r"))

    def wide(v):
        return v[:].unsqueeze(2).broadcast_to([P, T, E])

    rank = k.rank[:].unsqueeze(1).broadcast_to([P, T, E])
    chain.link(nc.vector.tensor_reduce(v1[:], logits, AX_X, ALU.max))
    nc.vector.tensor_tensor(p[:], logits, wide(v1), ALU.subtract).then_inc(s_shift, 1)
    dve.wait_ge(s_exp, 1)
    chain.link(nc.vector.tensor_reduce(v1[:], p[:], AX_X, ALU.add))
    chain.link(nc.vector.reciprocal(v1[:], v1[:]))
    chain.link(nc.vector.tensor_tensor(p[:], p[:], wide(v1), ALU.mult))
    for v, mask in ((v1, first), (v2, second)):
        chain.link(nc.vector.tensor_reduce(v[:], p[:], AX_X, ALU.max))
        chain.link(nc.vector.tensor_tensor(cand[:], p[:], wide(v), ALU.is_equal))
        chain.link(nc.vector.tensor_tensor(cand[:], cand[:], rank, ALU.mult))
        chain.link(nc.vector.tensor_reduce(r[:], cand[:], AX_X, ALU.max))
        chain.link(nc.vector.tensor_tensor(mask[:], wide(r), rank, ALU.is_equal))
        if v is v1:
            chain.link(nc.vector.scalar_tensor_tensor(out=p[:], in0=mask[:], scalar=-4.0, in1=p[:], op0=ALU.mult, op1=ALU.add))
    chain.link(nc.vector.tensor_tensor(r[:], v1[:], v2[:], ALU.add))
    chain.link(nc.vector.tensor_scalar(r[:], r[:], guard[1], None, guard[0]))
    chain.link(nc.vector.reciprocal(r[:], r[:]))
    chain.link(nc.vector.tensor_tensor(v1[:], v1[:], r[:], ALU.mult))
    chain.link(nc.vector.tensor_tensor(v2[:], v2[:], r[:], ALU.mult))
    chain.link(nc.vector.tensor_tensor(cand[:], first[:], wide(v1), ALU.mult))
    chain.link(nc.vector.tensor_tensor(k.wts[:], second[:], wide(v2), ALU.mult))
    chain.link(nc.vector.tensor_tensor(k.wts[:], k.wts[:], cand[:], ALU.add))


def phase_gating(k, layer, w_name, guard, loads, splits):
    nc, ins = k.nc, k.ins
    tag = f"g{layer}"
    s_w, s_var, s_std, s_chain, s_xn, s_xT, s_hT, s_logit, s_shift, s_exp, s_prim = k.sems(
        tag, "w var std chain xn xT hT logit shift exp prim")
    s_high, s_low, s_parts, s_wT, s_wTs, s_lT, s_lTs = k.sems(tag + "b", "high low parts wT wTs lT lTs")
    with ExitStack() as ph:
        def tmp(name, shape):
            return ph.enter_context(nc.sbuf_tensor(f"{tag}_{name}", shape, F32))
        w_gate = tmp("w_gate", [P, E])
        scr = {n: tmp(n, [P, T, E]) for n in ("p", "first", "second", "cand")}
        scr |= {n: tmp(n, [P, T]) for n in ("v1", "v2", "r")}
        p_x = psum(nc, ph, f"{tag}_px", 2)
        p_l, p_lT = psum(nc, ph, f"{tag}_pl", 1)[0], psum(nc, ph, f"{tag}_plT", 2)
        logitT = tmp("logitT", [E, 2, GN])
        p_c = psum(nc, ph, f"{tag}_pc", 1)[0]
        p_w = psum(nc, ph, f"{tag}_pw", 2)
        parts = tmp("parts", [P, T, 2 * E])
        own = tmp("own", [2 * E, E])
        mine = [(w_gate[:], ins[w_name])]
        if layer == 0:
            sim = tmp("sim", [P, E, E])
            used, prim, best, move = tmp("used", [P, E]), tmp("prim", [P, E]), tmp("best", [P, E]), tmp("move", [P, E])
            eq, far = tmp("eq", [P, E, E]), tmp("far", [P, E])
            route = tmp("route", [P, E, E])
            chosen, column = tmp("chosen", [2 * E, E, E]), tmp("column", [2 * E, E])
            mine.append((sim[:], bass.AP(ins["L0_ffn_similarity_matrix"].tensor, 0, [[0, P], [E, E], [1, E]])))
        with nc.Block() as block:
            @block.sync
            def _(sp):
                for dst, src in mine:
                    sp.dma_start(dst, src).then_inc(s_w, 16)
                for dst, src, s in loads:
                    sp.dma_start(dst, src).then_inc(s, 16)

            @block.scalar
            def _(act):
                k.norm_act(act, s_var, s_std)
                for g in range(G):
                    act.wait_ge(s_xT, g + 1)
                    k.modulate(k.HT[:, g * GN:(g + 1) * GN], p_x[g % 2][:, :], layer, 1, g // BG).then_inc(s_hT, 1)
                    for whole, high, _, s, value in splits[g * len(splits) // G:(g + 1) * len(splits) // G]:
                        act.wait_ge(s, value)
                        nc.scalar.activation(high, whole, ACT.Copy).then_inc(s_high, 1)
                k.load_table(ACT.Exp)
                act.wait_ge(s_shift, 1)
                nc.scalar.activation(scr["p"][:], scr["p"][:], ACT.Exp).then_inc(s_exp, 1)
                for g in range(G):
                    act.wait_ge(s_wT, g + 1)
                    nc.scalar.activation(k.WT[:, g * GN:(g + 1) * GN], p_w[g % 2][0:2 * E, :], ACT.Copy).then_inc(s_wTs, 1)

            @block.gpsimd
            def _(pool):
                for i, (whole, high, low, _, _) in enumerate(splits):
                    pool.wait_ge(s_high, i + 1)
                    nc.gpsimd.tensor_tensor(low, whole, high, ALU.subtract).then_inc(s_low, 1)

            @block.tensor
            def _(pe):
                for i in range(G + 2):
                    if i < G:
                        pe.wait_ge(s_xn, i + 1)
                        wait_pos(pe, s_hT, i - 1)
                        k.transpose_group(p_x[i % 2], i % 2).then_inc(s_xT, 1)
                    if 1 <= i <= G:
                        g = i - 1
                        if g == 0:
                            pe.wait_ge(s_w, 16 * len(mine))
                        pe.wait_ge(s_hT, g + 1)
                        wait_pos(pe, s_lTs, g - 1)
                        nc.tensor.matmul(p_lT[g % 2][0:E, :], w_gate[:], k.HT[:, g * GN:(g + 1) * GN], start=True, stop=True).then_inc(s_lT, 1)
                    if i >= 2:
                        g = i - 2
                        pe.wait_ge(s_lTs, g + 1)
                        for t in range(GT):
                            at = (g * GT + t) * E
                            last = nc.tensor.transpose(p_l[:, at:at + E], logitT[:, g % 2, t * P:(t + 1) * P], k.ident[0:E, 0:E])
                        last.then_inc(s_logit, 1)
                pe.wait_ge(s_parts, 2)
                for g in range(G):
                    wait_pos(pe, s_wTs, g - 1)
                    for t in range(GT):
                        last = nc.tensor.transpose(p_w[g % 2][0:2 * E, t * P:(t + 1) * P], parts[:, g * GT + t, :], k.ident[:])
                    last.then_inc(s_wT, 1)
                    if layer == 0 and g == 0:
                        pe.wait_ge(s_prim, 1)
                        nc.tensor.matmul(p_c[:, 0:E], k.ones[:], used[:], start=True, stop=True).then_inc(s_prim, 1)

            @block.vector
            def _(dve):
                chain = Chain(dve, s_chain)
                k.norm_dve(dve, chain, s_var, s_std)
                for i in range(G + 2):
                    if i < G:
                        wait_pos(dve, s_xT, i - 1)
                        for t in range(GT):
                            last = k.normalise(i * GT + t, t, i % 2)
                        last.then_inc(s_xn, 1)
                    if i >= 2:
                        g = i - 2
                        dve.wait_ge(s_lT, g + 1)
                        wait_pos(dve, s_logit, g - 1)
                        nc.vector.tensor_copy(logitT[:, g % 2, :], p_lT[g % 2][0:E, :]).then_inc(s_lTs, 1)
                chain.link(nc.vector.tensor_tensor(own[:], k.ident[0:2 * E, 0:E], k.ident[0:2 * E, E:2 * E], ALU.add))
                if layer:
                    chain.link(nc.vector.tensor_copy(k.pick[:], own[:].unsqueeze(2).broadcast_to([2 * E, E, P])))
                dve.wait_ge(s_logit, G)
                top_two(k, dve, chain, p_l[:, 0:T * E].rearrange("p (t e) -> p t e", e=E), (s_shift, s_exp), scr, guard)

                high = parts[:, :, 0:E].bitcast(F32R)
                nc.vector.tensor_copy(high, k.wts[:]).then_inc(s_parts, 1)
                dve.wait_ge(s_parts, 1)
                nc.vector.tensor_tensor(parts[:, :, E:2 * E], k.wts[:], high, ALU.subtract).then_inc(s_parts, 1)
                if layer:
                    return
                nc.vector.tensor_reduce(used[:], scr["first"][:].rearrange("p t e -> p e t"), AX_X, ALU.max).then_inc(s_prim, 1)
                dve.wait_ge(s_prim, 2)
                chain.link(nc.vector.tensor_scalar(prim[:], p_c[:, 0:E], 0.5, None, ALU.is_gt))
                chain.link(nc.vector.tensor_scalar(far[:], prim[:], -1.0, NEG, ALU.add, ALU.mult))
                dve.wait_ge(s_w, 16 * len(mine))
                columns = prim[:].unsqueeze(1).broadcast_to([P, E, E])
                chain.link(nc.vector.tensor_tensor(sim[:], sim[:], columns, ALU.mult))
                chain.link(nc.vector.tensor_tensor(sim[:], sim[:], far[:].unsqueeze(1).broadcast_to([P, E, E]), ALU.add))
                chain.link(nc.vector.tensor_reduce(best[:], sim[:], AX_X, ALU.max))
                rank = k.rank[:].unsqueeze(1).broadcast_to([P, E, E])
                chain.link(nc.vector.tensor_tensor(eq[:], sim[:], best[:].unsqueeze(2).broadcast_to([P, E, E]), ALU.is_equal))
                chain.link(nc.vector.tensor_tensor(eq[:], eq[:], rank, ALU.mult))
                chain.link(nc.vector.tensor_reduce(far[:], eq[:], AX_X, ALU.max))
                chain.link(nc.vector.tensor_tensor(route[:], far[:].unsqueeze(2).broadcast_to([P, E, E]), rank, ALU.is_equal))
                chain.link(nc.vector.tensor_scalar(move[:], best[:], SIM_MIN, None, ALU.is_ge))
                chain.link(nc.vector.tensor_scalar(prim[:], prim[:], -1.0, 1.0, ALU.mult, ALU.add))
                chain.link(nc.vector.tensor_tensor(move[:], move[:], prim[:], ALU.mult))
                chain.link(nc.vector.tensor_tensor(route[:], route[:], k.eye8[:], ALU.subtract))
                chain.link(nc.vector.tensor_tensor(route[:], route[:], move[:].unsqueeze(2).broadcast_to([P, E, E]), ALU.mult))
                chain.link(nc.vector.tensor_tensor(route[:], route[:], k.eye8[:], ALU.add))
                chain.link(nc.vector.tensor_tensor(chosen[:], route[0:2 * E], own[:].unsqueeze(2).broadcast_to([2 * E, E, E]), ALU.mult))
                chain.link(nc.vector.tensor_reduce(column[:], chosen[:].rearrange("p i j -> p j i"), AX_X, ALU.add))
                chain.link(nc.vector.tensor_copy(k.pick[:], column[:].unsqueeze(2).broadcast_to([2 * E, E, P])))


def by_groups(eng, step):
    step(0, 0, False)
    with eng.Fori(0, B - 1) as base:
        for c in range(1, BG + 1):
            step(base, c, False)
    step(B - 1, 1, True)


def product3(nc, out, lhs, rhs, start=True, stop=True):
    (lh, ll), (rh, rl) = lhs, rhs
    nc.tensor.matmul(out, lh, rh, start=start, stop=False)
    nc.tensor.matmul(out, lh, rl, start=False, stop=False)
    return nc.tensor.matmul(out, ll, rh, start=False, stop=stop)


def split_input(k, dve, s_x, x, w_rows, g):
    h = k.HT[:, ds(g * GN, GN)]
    k.nc.vector.tensor_scalar(x[:, 0, :], h, 1.0, None, ALU.mult).then_inc(s_x, 1)
    dve.wait_ge(s_x, 2 * g + 1)
    k.nc.vector.tensor_tensor(x[:, 1, :], h, x[:, 0, :], ALU.subtract)
    k.nc.vector.tensor_scalar(w_rows, k.WT[:, ds(g * GN, GN)], 1.0, None, ALU.mult).then_inc(s_x, 1)


def phase_experts0(k, w_gu, w_down):
    nc = k.nc
    s_chain, s_x, s_gu, s_silu, s_t, s_mid, s_high, s_low, s_y, s_yT, s_turn, s_gated, s_res = k.sems(
        "x0", "chain x gu silu t mid high low y yT turn gated res")
    LAG = 3
    with ExitStack() as ph:
        def tmp(name, shape, dt=F32):
            return ph.enter_context(nc.sbuf_tensor(name, shape, dt))
        x = tmp("x0_parts", [P, 2, 2, GN], F32R)
        w_rows = tmp("w0_rows", [2 * E, 2, GN], F32R)
        gate_s, mid, yT = k.xn, k.hT, k.gated[:, 1].rearrange("p t d -> p (t d)")
        mid_parts = tmp("mid_parts", [P, 4, 2, GN], F32R)
        p_g, p_u, p_w = psum(nc, ph, "p_g", 2), psum(nc, ph, "p_u", 2), psum(nc, ph, "p_w0", 2)
        p_y, p_t = psum(nc, ph, "p_y0", 1)[0], psum(nc, ph, "p_t0", 1)[0]
        stat_steps = 2 * GT + 1

        def first(g):
            return isinstance(g, int) and g == 0

        with nc.Block() as block:
            @block.scalar
            def _(act):
                def high(n, e):
                    act.wait_ge(s_mid, n + 1)
                    nc.scalar.activation(mid_parts[:, e % 4, 0, :], mid[:, e % 2, :], ACT.Copy).then_inc(s_high, 1)

                def out_of_psum(g):
                    act.wait_ge(s_y, (g + 1) * E)
                    nc.scalar.activation(yT, p_y[:, :], ACT.Copy).then_inc(s_yT, 1)

                def step(base, c, last):
                    g = base * BG + c
                    for e in range(E):
                        n = g * E + e
                        act.wait_ge(s_gu, n + 1)
                        wait_pos(act, s_mid, n - 1)
                        nc.scalar.activation(gate_s[:, e % 2, :], p_g[e % 2][:, :], ACT.Silu).then_inc(s_silu, 1)
                        if e or not first(g):
                            high(n - 1, (e - 1) % E)
                        if e == LAG - 1 and not first(g):
                            out_of_psum(g - 1)

                k.load_table(ACT.Silu)
                by_groups(act, step)
                high(G * E - 1, E - 1)
                out_of_psum(G - 1)

            @block.tensor
            def _(pe):
                def project(g, c, e):
                    n = g * E + e
                    wait_pos(pe, s_silu, n - 1)
                    wait_pos(pe, s_mid, n - 1)
                    if e == 0:
                        pe.wait_ge(s_x, 2 * g + 2)
                    xs = (x[:, c % 2, 0, :], x[:, c % 2, 1, :])
                    nc.tensor.matmul(p_w[e % 2][:, :], k.pick[:, e, :], w_rows[:, c % 2, :], start=True, stop=True)
                    for p, at in ((p_g, 0), (p_u, P)):
                        ws = (w_gu[0][:, e, at:at + P], w_gu[1][:, e, at:at + P])
                        last = product3(nc, p[e % 2][:, :], ws, xs)
                    last.then_inc(s_gu, 1)

                def down(g, e):
                    n = g * E + e
                    pe.wait_ge(s_low, n + 1)
                    if e == 0:
                        wait_pos(pe, s_yT, g)
                    ws = (w_down[0][:, e, :], w_down[1][:, e, :])
                    last = product3(nc, p_y[:, :], ws, (mid_parts[:, e % 4, 0, :], mid_parts[:, e % 4, 1, :]), e == 0, e == E - 1)
                    last.then_inc(s_y, 1)

                def turn(g):
                    pe.wait_ge(s_yT, g + 1)
                    for t in range(GT):
                        last = nc.tensor.transpose(p_t[:, t * P:(t + 1) * P], yT[:, t * P:(t + 1) * P], k.ident[:])
                    last.then_inc(s_turn, 1)

                def step(base, c, last):
                    g = base * BG + c
                    for e in range(E):
                        project(g, c, e)
                        if e >= LAG:
                            down(g, e - LAG)
                        elif not first(g):
                            down(g - 1, E - LAG + e)
                        if e == LAG + 1 and not first(g):
                            turn(g - 1)

                by_groups(pe, step)
                for e in range(E - LAG, E):
                    down(G - 1, e)
                turn(G - 1)

            @block.gpsimd
            def _(pool):
                def low(n, e):
                    pool.wait_ge(s_high, n + 1)
                    nc.gpsimd.tensor_tensor(mid_parts[:, e % 4, 1, :], mid[:, e % 2, :], mid_parts[:, e % 4, 0, :],
                                            ALU.subtract).then_inc(s_low, 1)

                def add(g):
                    pool.wait_ge(s_gated, g + 1)
                    k.add_gated(g * GT, 0, nc.gpsimd).then_inc(s_res, 1)

                def step(base, c, last):
                    g = base * BG + c
                    for e in range(E):
                        if e or not first(g):
                            low(g * E + e - 1, (e - 1) % E)
                        if e == LAG + 3 and not first(g):
                            add(g - 1)

                by_groups(pool, step)
                low(G * E - 1, E - 1)
                add(G - 1)

            @block.vector
            def _(dve):
                def gate(g, b):
                    dve.wait_ge(s_turn, g + 1)
                    k.gate(p_t[:, :].rearrange("p (t d) -> p t d", t=GT), 0, 1, b).then_inc(s_gated, 1)

                def stats(g):
                    chain = Chain(dve, s_chain, g * stat_steps)
                    dve.wait_ge(s_res, g + 1)
                    k.stats(chain, g * GT, True)
                    assert chain.n == stat_steps

                def step(base, c, last):
                    g = base * BG + c
                    for e in range(E):
                        n = g * E + e
                        dve.wait_ge(s_silu, n + 1)
                        nc.vector.tensor_tensor(gate_s[:, e % 2, :], gate_s[:, e % 2, :], p_w[e % 2][:, :], ALU.mult).then_inc(s_t, 1)
                        dve.wait_ge(s_t, n + 1)
                        wait_pos(dve, s_low, n - 1)
                        nc.vector.tensor_tensor(mid[:, e % 2, :], gate_s[:, e % 2, :], p_u[e % 2][:, :], ALU.mult).then_inc(s_mid, 1)
                        if not first(g):
                            if e == LAG + 2:
                                gate(g - 1, base + (c - 1) // BG)
                            if e == LAG + 4:
                                stats(g - 1)
                        if e == 5 and not last:
                            split_input(k, dve, s_x, x[:, (c + 1) % 2], w_rows[:, (c + 1) % 2, :], g + 1)

                split_input(k, dve, s_x, x[:, 0], w_rows[:, 0, :], 0)
                by_groups(dve, step)
                gate(G - 1, B - 1)
                stats(G - 1)
                dve.wait_ge(s_chain, G * stat_steps)


def store_batch(sp, part, dram, s_store, b):
    for i in range(2):
        for n, terms in enumerate(PART_TERMS[i]):
            step = terms[1] - terms[0] if len(terms) > 1 else 1
            dst = dram[i][terms[0]:terms[-1] + 1:step, :, b * S:(b + 1) * S].rearrange("t p s -> p t s")
            src = part[:, b % PART_SLOTS, i, n, :].unsqueeze(1).broadcast_to([P, len(terms), S])
            sp.dma_start(dst, src).then_inc(s_store[b % PART_SLOTS], 16)


def fill_slot(eng, bufs, dram, sem, token0, c):
    Q, K, _, zero_rows = bufs
    q = c % CYCLE // 2
    for par in range(2):
        rows = slice(64 * par, 64 * par + SLOT)
        for pair in range(2):
            h = 4 * q + 2 * pair + par
            eng.dma_start(Q[rows, q, pair, :], dram[0][:, h * DH:(h + 1) * DH, ds(token0, S)]).then_inc(sem, 16)
            eng.dma_start(K[rows, q, pair, par, :], dram[1][:, h * DH:(h + 1) * DH, ds(token0, S)]).then_inc(sem, 16)
        eng.dma_start(Q[64 * par + SLOT:64 * par + SROWS, q, :, :], zero_rows[:]).then_inc(sem, 16)


def phase_qkv(k, V, part, dram, bufs, s_split, s_store, s_begin):
    nc, ins = k.nc, k.ins
    s_w, s_var, s_std, s_chain, s_xn, s_xT, s_hT, s_proj, s_full, s_rest, s_v, s_vs = k.sems(
        "qkv", "w var std chain xn xT hT proj full rest v vs")
    with ExitStack() as ph:
        def tmp(name, shape, dt=F32):
            return ph.enter_context(nc.sbuf_tensor(name, shape, dt))
        w = {n: tmp(f"w_{n}", [P, D]) for n in "qkv"}
        bias = tmp("bias_qk", [P, 2])
        b_v = tmp("b_v", [P, D])
        full = tmp("full", [P, 2, 2, GN])
        p_x = psum(nc, ph, "q_px", 2)
        p_q, p_k, p_v = psum(nc, ph, "p_q", 2), psum(nc, ph, "p_k", 2), psum(nc, ph, "p_v", 2)
        loads = [(w[n][:], ins[f"L1_attn_{n}_wT"]) for n in "qkv"]
        loads += [(bias[:, i:i + 1], ins[f"L1_attn_{n}_b"].unsqueeze(1)) for i, n in enumerate("qk")]
        loads += [(b_v[:], row_of(ins["L1_attn_v_b"], D))]
        scale = 1.0 / math.sqrt(DH)

        def part_of(g, i, n):
            return part[:, g // BG % PART_SLOTS, i, n, (g % BG) * GN:(g % BG + 1) * GN]

        with nc.Block() as block:
            @block.sync
            def _(sp):
                for dst, src in loads:
                    sp.dma_start(dst, src).then_inc(s_w, 16)
                for b in range(B - 1):
                    sp.wait_ge(s_split, 2 * (b + 1) * BG)
                    store_batch(sp, part, dram, s_store, b)
                    if b == 0:
                        sp.wait_ge(s_store[0], STORES)
                        fill_slot(sp, bufs, dram, s_begin, 0, 0)

            @block.gpsimd
            def _(pool):
                pool.wait_ge(s_chain, 2)
                for g in range(G):
                    wait_pos(pool, s_xT, g - 1)
                    for t in range(GT):
                        last = k.normalise_pool(g * GT + t, t, g % 2)
                    last.then_inc(s_xn, 1)

            @block.scalar
            def _(act):
                def modulate(g):
                    act.wait_ge(s_xT, g + 1)
                    wait_pos(act, s_v, g - 1)
                    k.modulate(k.hT[:, g % 2, :], p_x[g % 2][:, :], 1, 0, g // BG).then_inc(s_hT, 1)

                k.norm_act(act, s_var, s_std)
                modulate(0)
                for g in range(G):
                    if g + 1 < G:
                        modulate(g + 1)
                    if g == 0:
                        act.wait_ge(s_chain, 3)
                    for i, (p, sc) in enumerate(((p_q, scale), (p_k, 1.0))):
                        act.wait_ge(s_proj, 2 * g + i + 1)
                        wait_pos(act, s_split, 2 * (g - 2) + i + 1)
                        if g % BG == 0:
                            wait_pos(act, s_store[g // BG % PART_SLOTS], STORES * (g // BG // PART_SLOTS))
                        nc.scalar.activation(full[:, g % 2, i, :], p[g % 2][:, :], ACT.Identity, scale=sc, bias=bias[:, i:i + 1])
                        nc.scalar.activation(part_of(g, i, 0), p[g % 2][:, :], ACT.Identity, scale=sc, bias=bias[:, i:i + 1]).then_inc(s_full, 1)

            @block.tensor
            def _(pe):
                def turn(g):
                    pe.wait_ge(s_xn, g + 1)
                    wait_pos(pe, s_hT, g - 1)
                    k.transpose_group(p_x[g % 2], g % 2).then_inc(s_xT, 1)

                turn(0)
                pe.wait_ge(s_w, 16 * len(loads))
                for g in range(G):
                    if g + 1 < G:
                        turn(g + 1)
                    pe.wait_ge(s_hT, g + 1)
                    wait_pos(pe, s_full, 2 * (g - 1))
                    for p, n in ((p_q, "q"), (p_k, "k")):
                        nc.tensor.matmul(p[g % 2][:, :], w[n][:], k.hT[:, g % 2, :], start=True, stop=True).then_inc(s_proj, 1)
                    wait_pos(pe, s_vs, g - 1)
                    for t in range(GT):
                        last = nc.tensor.matmul(p_v[g % 2][:, t * D:(t + 1) * D], k.hT[:, g % 2, t * P:(t + 1) * P], w["v"][:], start=True, stop=True)
                    last.then_inc(s_v, 1)

            @block.vector
            def _(dve):
                chain = Chain(dve, s_chain)
                k.norm_dve(dve, chain, s_var, s_std)
                dve.wait_ge(s_w, 16 * len(loads))
                chain.link(nc.vector.tensor_scalar(bias[:, 0:1], bias[:, 0:1], scale, None, ALU.mult))
                for g in range(G):
                    for i in range(2):
                        dve.wait_ge(s_full, 2 * g + i + 1)
                        x = full[:, g % 2, i, :]
                        nc.vector.tensor_tensor(x, x, part_of(g, i, 0), ALU.subtract).then_inc(s_rest, 1)
                    for i in range(2):
                        dve.wait_ge(s_rest, 2 * g + i + 1)
                        chain.add(nc.vector.tensor_copy(part_of(g, i, 1), full[:, g % 2, i, :]))
                    dve.wait_ge(s_v, g + 1)
                    nc.vector.tensor_tensor(V[:, g * GT:(g + 1) * GT, :], p_v[g % 2][:, :].rearrange("p (t d) -> p t d", t=GT),
                                            b_v[:].unsqueeze(1).broadcast_to([P, GT, D]), ALU.add).then_inc(s_vs, 1)
                    chain.wait()
                    for i in range(2):
                        nc.vector.tensor_tensor(part_of(g, i, 2), full[:, g % 2, i, :], part_of(g, i, 1), ALU.subtract).then_inc(s_split, 1)


def base_batch(base, c):
    return base + c // CYCLE


def run(eng, step):
    step(0, 0, False)
    with eng.Fori(0, B - 1) as base:
        for c in range(1, CYCLE + 1):
            step(base, c, False)
    for c in range(1, CYCLE):
        step(B - 1, c, True)


def phase_attention(k, V, C, part, dram, bufs, s_store, s_begin, s_slot):
    nc = k.nc
    s_top, s_max, s_mparts, s_mT, s_mrows, s_mdma, s_qk, s_exp, s_v, s_pv, s_o, s_oT, s_c, s_chain, s_recip = k.sems(
        "at", "top max mparts mT mrows mdma qk exp v pv o oT c chain recip")
    Q, K, Vs, zero_rows = bufs
    with ExitStack() as ph:
        def tmp(name, shape, dt=F32):
            return ph.enter_context(nc.sbuf_tensor(name, shape, dt))
        prob = tmp("prob", [P, 2, 4, GN])
        halfmax, top, rest = tmp("halfmax", [P, 2, TOPS]), tmp("top", [P, GT * 4]), tmp("rest", [P, GT * 4])
        mparts = tmp("mparts", [P, 2, GT, 12], BF16)
        mrows = tmp("mrows", [12, 2, GN], BF16)
        o_sb, recip = k.xn[:, 0, :], tmp("recip", [P, GT * 4])
        p_s = psum(nc, ph, "p_s", 2, 1024)
        p_m = psum(nc, ph, "p_m", 2)
        p_out = psum(nc, ph, "p_out", 1)[0]
        p_t = psum(nc, ph, "p_t", 1)[0]
        p_tb = p_t[:, :].bitcast(BF16)

        def top_banks(base, c):
            return 4 if isinstance(base, int) and base == 0 and c < 2 else 2

        def top_bank(base, c, n):
            i = n % top_banks(base, c)
            return p_m[i][:, :] if i < 2 else p_s[i - 2][:, 0:GN]

        def quad(c):
            return (c % CYCLE) // 2

        with nc.Block() as block:
            @block.sync
            def _(sp):
                def max_rows(base, c):
                    q, half = quad(c), c % 2
                    sp.wait_ge(s_mrows, base * CYCLE + c + 1)
                    for par in range(2):
                        for pair in range(2):
                            at = (par * 2 + pair) * 3
                            sp.dma_start(Q[64 * par + SLOT:64 * par + SROWS, q, pair, half * GN:(half + 1) * GN],
                                         mrows[at:at + 3, c % 2, :]).then_inc(s_mdma, 16)

                def step(base, c, last):
                    j = base * CYCLE + c
                    if c % 2 == 0 and (not last or c + 4 < CYCLE):
                        token0 = sp.snap(base_batch(base, c + 4) * S) if not isinstance(base, int) else base_batch(base, c + 4) * S
                        sp.wait_ge(s_qk, 2 * KT * j + 1)
                        fill_slot(sp, bufs, dram, s_slot[quad(c + 4)], token0, c + 4)
                    if not last or c + 1 < CYCLE:
                        max_rows(base, c + 1)

                fill_slot(sp, bufs, dram, s_slot[1], 0, 2)
                store_batch(sp, part, dram, s_store, B - 1)
                max_rows(0, 0)
                for slot in range(PART_SLOTS):
                    sp.wait_ge(s_store[slot], STORES * len(range(slot, B, PART_SLOTS)))
                run(sp, step)
                sp.wait_ge(s_mdma, 64 * HALVES)

            @block.gpsimd
            def _(pool):
                def values(base, c):
                    b, q = base_batch(base, c), quad(c)
                    for h in range(4):
                        at = (4 * q + h) * DH
                        last = nc.gpsimd.tensor_copy(Vs[:, q % 2, :, h, 0:DH], V[:, ds(b * KT, KT), at:at + DH])
                    last.then_inc(s_v, 1)

                def step(base, c, last):
                    j = base * CYCLE + c
                    if c % 2 == 0 and (not last or c + 2 < CYCLE):
                        wait_pos(pool, s_pv, KT * j)
                        values(base, c + 2)

                values(0, 0)
                run(pool, step)

            @block.tensor
            def _(pe):
                def tops(base, c, n):
                    x = TOPS * (base * CYCLE + c) + n
                    q, half = quad(c), c % 2
                    tile, h, kh = n // 8, n // 2 % 4, n % 2
                    pair, par = h // 2, h % 2
                    at = half * GN + tile * P
                    if n == 0 and half == 0:
                        b = base_batch(base, c)
                        if q:
                            pe.wait_ge(s_slot[q], 160 * (b + 1))
                        elif isinstance(b, int) and b == 0:
                            pe.wait_ge(s_begin, 160)
                        else:
                            pe.wait_ge(s_slot[q], 160 * b)
                    wait_pos(pe, s_max, x + 1 - top_banks(base, c))
                    nc.tensor.matmul(top_bank(base, c, n), Q[:, q, pair, at:at + P], K[:, q, pair, par, kh * GN:(kh + 1) * GN],
                                     start=True, stop=True).then_inc(s_top, 1)

                def scores(base, c, kt, pair):
                    u = (base * CYCLE + c) * KT + kt
                    q, half = quad(c), c % 2
                    wait_pos(pe, s_exp, 2 * u + pair - 1)
                    for par in range(2):
                        last = nc.tensor.matmul(p_s[pair][:, par * GN:(par + 1) * GN], K[:, q, pair, par, kt * P:(kt + 1) * P],
                                                Q[:, q, pair, half * GN:(half + 1) * GN], start=True, stop=True)
                    last.then_inc(s_qk, 1)

                def weigh(base, c, kt, part):
                    u = (base * CYCLE + c) * KT + kt
                    if part == 0:
                        pe.wait_ge(s_exp, 2 * u + 2)
                    if kt == 0 and part == 0:
                        if c % 2 == 0:
                            pe.wait_ge(s_v, base * QUADS + c // 2 + 1)
                        wait_pos(pe, s_o, base * CYCLE + c)
                    for h in range(4):
                        last = nc.tensor.matmul(p_out[32 * h:32 * h + 32, part * HQ:(part + 1) * HQ], Vs[:, quad(c) % 2, kt, h, :],
                                                prob[:, kt % 2, h, part * HQ:(part + 1) * HQ], start=(kt == 0 and part == 0),
                                                stop=(kt == KT - 1), skip_group_check=True)
                    if part:
                        last.then_inc(s_pv, 1)

                def turn_max(base, c):
                    j = base * CYCLE + c
                    pe.wait_ge(s_mparts, j + 1)
                    wait_pos(pe, s_c, j - 2)
                    for t in range(GT):
                        last = nc.tensor.transpose(p_tb[0:12, t * P:(t + 1) * P], mparts[:, c % 2, t, :], k.identb[:])
                    last.then_inc(s_mT, 1)

                def turn_out(base, c, turned):
                    j = base * CYCLE + c
                    pe.wait_ge(s_o, j + 1)
                    pe.wait_ge(s_mrows, turned)
                    wait_pos(pe, s_c, j)
                    for t in range(GT):
                        last = nc.tensor.transpose(p_t[:, t * P:(t + 1) * P], o_sb[:, t * P:(t + 1) * P], k.ident[:])
                    last.then_inc(s_oT, 1)

                def step(base, c, last):
                    ahead = not last or c + 2 < CYCLE
                    pe.wait_ge(s_mdma, 64 * (base * CYCLE + c + 1))
                    for kt in range(KT):
                        for i in range(4):
                            if i < 2:
                                scores(base, c, kt, i)
                            elif kt or c:
                                weigh(base, c if kt else c - 1, (kt - 1) % KT, i - 2)
                            if ahead:
                                tops(base, c + 2, 4 * kt + i)
                        if kt == 1 and (not last or c + 1 < CYCLE):
                            turn_max(base, c + 1)
                        if kt == 3 and c:
                            turn_out(base, c - 1, base * CYCLE + c + 2 if not last or c + 1 < CYCLE else HALVES)

                for c in range(2):
                    for n in range(TOPS):
                        tops(0, c, n)
                    if c == 0:
                        turn_max(0, 0)
                pe.wait_ge(s_max, 2 * TOPS)
                run(pe, step)
                weigh(B - 1, CYCLE - 1, KT - 1, 0)
                weigh(B - 1, CYCLE - 1, KT - 1, 1)
                turn_out(B - 1, CYCLE - 1, HALVES)

            @block.scalar
            def _(act):
                def rows_out(base, c):
                    j = base * CYCLE + c
                    act.wait_ge(s_mT, j + 1)
                    wait_pos(act, s_mdma, 64 * (j - 1))
                    nc.scalar.activation(mrows[:, c % 2, :], p_tb[0:12, 0:GN], ACT.Copy).then_inc(s_mrows, 1)

                def evacuate(base, c):
                    j = base * CYCLE + c
                    act.wait_ge(s_pv, KT * (j + 1))
                    wait_pos(act, s_oT, j)
                    nc.scalar.activation(o_sb, p_out[:, :], ACT.Copy).then_inc(s_o, 1)

                def step(base, c, last):
                    for kt in range(KT):
                        u = (base * CYCLE + c) * KT + kt
                        if kt == 1 and c:
                            evacuate(base, c - 1)
                        wait_pos(act, s_pv, u - 1)
                        for pair in range(2):
                            act.wait_ge(s_qk, 2 * u + pair + 1)
                            nc.scalar.activation(prob[:, kt % 2, 2 * pair:2 * pair + 2, :],
                                                 p_s[pair][:, :].rearrange("p (h n) -> p h n", h=2), ACT.Exp).then_inc(s_exp, 1)
                        if kt == 2 and (not last or c + 1 < CYCLE):
                            rows_out(base, c + 1)

                k.load_table(ACT.Exp)
                rows_out(0, 0)
                run(act, step)
                evacuate(B - 1, CYCLE - 1)

            @block.vector
            def _(dve):
                steps = 4
                def tops(base, c, n):
                    x = TOPS * (base * CYCLE + c) + n
                    dve.wait_ge(s_top, x + 1)
                    nc.vector.tensor_reduce(halfmax[:, c % 2, n:n + 1], top_bank(base, c, n), AX_X, ALU.max).then_inc(s_max, 1)

                def parts(base, c):
                    j = base * CYCLE + c
                    dve.wait_ge(s_max, TOPS * (j + 1))
                    wait_pos(dve, s_mT, j - 1)
                    chain = Chain(dve, s_chain, j * steps)
                    chain.link(nc.vector.tensor_reduce(top[:], halfmax[:, c % 2, :].rearrange("p (n k) -> p n k", k=2), AX_X, ALU.max))
                    view = mparts[:, c % 2, :, :].rearrange("p t (par pair part) -> p t pair par part", par=2, pair=2)

                    def heads(x):
                        return x[:].rearrange("p (t pair par) -> p t pair par", t=GT, pair=2)
                    chain.link(nc.vector.tensor_copy(view[:, :, :, :, 0], heads(top)))
                    chain.link(nc.vector.tensor_tensor(heads(rest), heads(top), view[:, :, :, :, 0], ALU.subtract))
                    chain.link(nc.vector.tensor_copy(view[:, :, :, :, 1], heads(rest)))
                    nc.vector.tensor_tensor(view[:, :, :, :, 2], heads(rest), view[:, :, :, :, 1], ALU.subtract).then_inc(s_mparts, 1)

                def normalise(base, c):
                    j = base * CYCLE + c
                    dve.wait_ge(s_oT, j + 1)
                    o = p_t[:, :].rearrange("p (t h r) -> p t h r", t=GT, h=4)
                    nc.vector.reciprocal(recip[:].rearrange("p (t h) -> p t h", t=GT), o[:, :, :, DH]).then_inc(s_recip, 1)
                    dve.wait_ge(s_recip, j + 1)
                    tile0 = base_batch(base, c) * KT + (c % 2) * GT
                    at = quad(c) * 4 * DH
                    dst = C[:, ds(tile0, GT), at:at + 4 * DH].rearrange("p t (h d) -> p t h d", h=4)
                    nc.vector.tensor_tensor(dst, o[:, :, :, 0:DH],
                                            recip[:].rearrange("p (t h) -> p t h", t=GT).unsqueeze(3).broadcast_to([P, GT, 4, DH]),
                                            ALU.mult).then_inc(s_c, 1)

                def step(base, c, last):
                    if not last or c + 1 < CYCLE:
                        parts(base, c + 1)
                    for kt in range(KT):
                        if not last or c + 2 < CYCLE:
                            for n in range(4):
                                tops(base, c + 2, 4 * kt + n)
                        if kt == 5 and c:
                            normalise(base, c - 1)

                for c in range(2):
                    for n in range(TOPS):
                        tops(0, c, n)
                    if c == 0:
                        parts(0, 0)
                run(dve, step)
                normalise(B - 1, CYCLE - 1)


def phase_project(k, C, loads):
    nc, ins = k.nc, k.ins
    s_w, s_chain, s_cT, s_cTs, s_o, s_oT, s_back, s_gated, s_x = k.sems("pr", "w chain cT cTs o oT back gated x")
    with ExitStack() as ph:
        def tmp(name, shape):
            return ph.enter_context(nc.sbuf_tensor(name, shape, F32))
        w_o, b_o, oT = tmp("w_o1", [P, D]), tmp("b_o1", [P, 1]), tmp("oT1", [P, 2, GN])
        p_c, p_o, p_b = psum(nc, ph, "p_c", 2), psum(nc, ph, "p_o1", 2), psum(nc, ph, "p_b1", 2)
        with nc.Block() as block:
            @block.sync
            def _(sp):
                sp.dma_start(w_o[:], ins["L1_attn_out_wT"]).then_inc(s_w, 16)
                sp.dma_start(b_o[:], ins["L1_attn_out_b"].unsqueeze(1)).then_inc(s_w, 16)
                for dst, src, s in loads:
                    sp.dma_start(dst, src).then_inc(s, 16)

            @block.scalar
            def _(act):
                for i in range(G + 1):
                    if i < G:
                        act.wait_ge(s_cT, i + 1)
                        wait_pos(act, s_o, i - 1)
                        nc.scalar.activation(k.hT[:, i % 2, :], p_c[i % 2][:, :], ACT.Copy).then_inc(s_cTs, 1)
                    if i:
                        g = i - 1
                        act.wait_ge(s_o, g + 1)
                        wait_pos(act, s_back, g - 1)
                        nc.scalar.activation(oT[:, g % 2, :], p_o[g % 2][:, :], ACT.Identity, bias=b_o[:]).then_inc(s_oT, 1)

            @block.tensor
            def _(pe):
                def turn(g):
                    wait_pos(pe, s_cTs, g - 1)
                    for t in range(GT):
                        last = nc.tensor.transpose(p_c[g % 2][:, t * P:(t + 1) * P], C[:, g * GT + t, :], k.ident[:])
                    last.then_inc(s_cT, 1)

                def project(g):
                    pe.wait_ge(s_cTs, g + 1)
                    wait_pos(pe, s_oT, g - 1)
                    nc.tensor.matmul(p_o[g % 2][:, :], w_o[:], k.hT[:, g % 2, :], start=True, stop=True).then_inc(s_o, 1)

                def back(g):
                    pe.wait_ge(s_oT, g + 1)
                    wait_pos(pe, s_gated, g - 1)
                    for t in range(GT):
                        last = nc.tensor.transpose(p_b[g % 2][:, t * P:(t + 1) * P], oT[:, g % 2, t * P:(t + 1) * P], k.ident[:])
                    last.then_inc(s_back, 1)

                turn(0)
                pe.wait_ge(s_w, 32)
                for i in range(G + 1):
                    if i + 1 < G:
                        turn(i + 1)
                    if i < G:
                        project(i)
                    if i:
                        back(i - 1)

            @block.gpsimd
            def _(pool):
                for g in range(G):
                    pool.wait_ge(s_gated, g + 1)
                    k.add_gated(g * GT, g % 2, nc.gpsimd).then_inc(s_x, 1)

            @block.vector
            def _(dve):
                chain = Chain(dve, s_chain)
                for i in range(G + 1):
                    if i < G:
                        dve.wait_ge(s_back, i + 1)
                        wait_pos(dve, s_x, i - 1)
                        k.gate(p_b[i % 2][:, :].rearrange("p (t d) -> p t d", t=GT), 1, 0, i // BG, i % 2).then_inc(s_gated, 1)
                    if i:
                        dve.wait_ge(s_x, i)
                        k.stats(chain, (i - 1) * GT)
                        chain.wait()


def phase_experts1(k, w1, b1, w2, b2):
    nc = k.nc
    s_x, s_w, s_ws, s_up, s_gelu, s_low, s_y, s_mul, s_b, s_acc, s_turn, s_gated, s_res, s_out = k.sems(
        "x1", "x w ws up gelu low y mul b acc turn gated res out")
    out_v = k.out.rearrange("b (t p) d -> p (b t) d", p=P)
    with ExitStack() as ph:
        def tmp(name, shape, dt=F32):
            return ph.enter_context(nc.sbuf_tensor(name, shape, dt))
        x = tmp("x1_parts", [P, 2, 2, GN], F32R)
        w_rows = tmp("w1_rows", [2 * E, 2, GN], F32R)
        hid = tmp("hid", [P, FC, GN])
        hid_parts = tmp("hid_parts", [P, 2, 2, FC, GN], F32R)
        w_rep = tmp("w_rep", [P, 4, GN])
        weighted, acc = k.xn, k.hT
        p_h, p_y = psum(nc, ph, "p_h", 4), psum(nc, ph, "p_y1", 2)
        p_w, p_t = psum(nc, ph, "p_w1", 1)[0], psum(nc, ph, "p_t1", 1)[0]

        def first(g):
            return isinstance(g, int) and g == 0

        with nc.Block() as block:
            @block.sync
            def _(sp):
                with sp.Fori(0, G) as g:
                    sp.wait_ge(s_res, g + 1)
                    sp.dma_start(out_v[:, ds(g * GT, GT), :], k.X[:, ds(g * GT, GT), :]).then_inc(s_out, 16)
                sp.wait_ge(s_out, 16 * G)

            @block.scalar
            def _(act):
                def step(base, c, last):
                    for e in range(E):
                        n = (base * BG + c) * E + e
                        act.wait_ge(s_w, n + 1)
                        wait_pos(act, s_mul, n - 3)
                        nc.scalar.activation(w_rep[:, e % 4, :], p_w[:, :], ACT.Copy).then_inc(s_ws, 1)
                        wait_pos(act, s_y, n - 1)
                        for f in range(FC):
                            act.wait_ge(s_up, n * FC + f + 1)
                            wait_pos(act, s_low, (n - 1) * FC + f + 1)
                            nc.scalar.activation(hid[:, f, :], p_h[f][:, :], ACT.Gelu, bias=b1[:, e, f:f + 1])
                            nc.scalar.activation(hid_parts[:, e % 2, 0, f, :], p_h[f][:, :], ACT.Gelu, bias=b1[:, e, f:f + 1]).then_inc(s_gelu, 1)

                k.load_table(ACT.Gelu)
                by_groups(act, step)

            @block.tensor
            def _(pe):
                def weight_row(g, c, e):
                    wait_pos(pe, s_ws, g * E + e)
                    nc.tensor.matmul(p_w[:, :], k.pick[:, e, :], w_rows[:, c % 2, :], start=True, stop=True).then_inc(s_w, 1)

                def up(g, c, e):
                    n = g * E + e
                    xs = (x[:, c % 2, 0, :], x[:, c % 2, 1, :])
                    for f in range(FC):
                        wait_pos(pe, s_gelu, (n - 1) * FC + f + 1)
                        cols = slice(f * P, (f + 1) * P)
                        product3(nc, p_h[f][:, :], (w1[0][:, e, cols], w1[1][:, e, cols]), xs).then_inc(s_up, 1)

                def second_biases(c):
                    nc.tensor.matmul(p_t[:, :], b2[0][:], w_rows[:, c % 2, :], start=True, stop=False)
                    nc.tensor.matmul(p_t[:, :], b2[1][0:E, :], w_rows[0:E, c % 2, :], start=False, stop=True).then_inc(s_b, 1)

                def down(n, e):
                    pe.wait_ge(s_low, (n + 1) * FC)
                    wait_pos(pe, s_mul, n - 1)
                    for f in range(FC):
                        hs = (hid_parts[:, e % 2, 0, f, :], hid_parts[:, e % 2, 1, f, :])
                        last = product3(nc, p_y[e % 2][:, :], (w2[0][:, e, f, :], w2[1][:, e, f, :]), hs, f == 0, f == FC - 1)
                    last.then_inc(s_y, 1)

                def turn(g, slot):
                    pe.wait_ge(s_acc, (g + 1) * E)
                    for t in range(GT):
                        last = nc.tensor.transpose(p_t[:, t * P:(t + 1) * P], acc[:, slot, t * P:(t + 1) * P], k.ident[:])
                    last.then_inc(s_turn, 1)

                def step(base, c, last):
                    g = base * BG + c
                    pe.wait_ge(s_x, 2 * g + 2)
                    for e in range(E):
                        weight_row(g, c, e)
                        up(g, c, e)
                        if e == 0:
                            second_biases(c)
                        if e or not first(g):
                            down(g * E + e - 1, (e - 1) % E)
                        if e == 3 and not first(g):
                            pe.wait_ge(s_acc, g * E + 1)
                            turn(g - 1, (c + 1) % 2)

                by_groups(pe, step)
                down(G * E - 1, E - 1)
                turn(G - 1, (G - 1) % 2)

            @block.vector
            def _(dve):
                def low(n, e, f):
                    dve.wait_ge(s_gelu, n * FC + f + 1)
                    nc.vector.tensor_tensor(hid_parts[:, e % 2, 1, f, :], hid[:, f, :], hid_parts[:, e % 2, 0, f, :],
                                            ALU.subtract).then_inc(s_low, 1)

                def weigh(n, e):
                    dve.wait_ge(s_ws, n + 1)
                    dve.wait_ge(s_y, n + 1)
                    wait_pos(dve, s_acc, n - 1)
                    nc.vector.tensor_tensor(weighted[:, e % 2, :], p_y[e % 2][:, :], w_rep[:, e % 4, :], ALU.mult).then_inc(s_mul, 1)

                def accumulate(g, e, acc_slot):
                    n = g * E + e
                    dve.wait_ge(s_mul, n + 1)
                    if e == 0:
                        dve.wait_ge(s_b, g + 1)
                    else:
                        dve.wait_ge(s_acc, n)
                    a = acc[:, acc_slot, :]
                    nc.vector.tensor_tensor(a, weighted[:, e % 2, :], p_t[:, :] if e == 0 else a, ALU.add).then_inc(s_acc, 1)

                def finish(g, b):
                    dve.wait_ge(s_turn, g + 1)
                    k.gate(p_t[:, :].rearrange("p (t d) -> p t d", t=GT), 1, 1, b).then_inc(s_gated, 1)
                    dve.wait_ge(s_gated, g + 1)
                    k.add_gated(g * GT).then_inc(s_res, 1)
                    dve.wait_ge(s_res, g + 1)

                def step(base, c, last):
                    g = base * BG + c
                    for e in range(E):
                        n = g * E + e
                        low(n, e, 0)
                        if e >= 2:
                            accumulate(g, e - 2, c % 2)
                        elif not first(g):
                            accumulate(g - 1, E - 2 + e, (c + 1) % 2)
                        for f in range(1, FC):
                            low(n, e, f)
                        if e or not first(g):
                            weigh(n - 1, (e - 1) % E)
                        if e == 4 and not first(g):
                            finish(g - 1, base + (c - 1) // BG)
                        if e == 5 and not last:
                            split_input(k, dve, s_x, x[:, (c + 1) % 2], w_rows[:, (c + 1) % 2, :], g + 1)

                split_input(k, dve, s_x, x[:, 0], w_rows[:, 0, :], 0)
                by_groups(dve, step)
                accumulate(G - 1, E - 2, (G - 1) % 2)
                weigh(G * E - 1, E - 1)
                accumulate(G - 1, E - 1, (G - 1) % 2)
                finish(G - 1, B - 1)


def build(nc, ins, out):
    with ExitStack() as ctx:
        k = Kernel(nc, ctx, ins, out)
        q_dram = nc.dram_tensor("q_parts", [TERMS, P, N], BF16).ap()
        k_dram = nc.dram_tensor("k_parts", [TERMS, P, N], BF16).ap()
        s_w0, s_w1 = k.sem("weights0"), k.sems("weights1", "up down")

        def tensor(stack, name, shape, dt=F32):
            return stack.enter_context(nc.sbuf_tensor(name, shape, dt))

        with ExitStack() as attn:
            bufs = (tensor(attn, "Q", [P, QUADS, 2, S], BF16),
                    tensor(attn, "K", [P, QUADS, 2, 2, S], BF16),
                    tensor(attn, "Vs", [P, 2, KT, 4, 32]),
                    tensor(attn, "zero_rows", [3, 2, S], BF16))
            V = tensor(attn, "V", [P, T, D])
            phase_setup(k)
            phase_linear_attention(k, bufs)
            with ExitStack() as mixture:
                w_gu = [tensor(mixture, f"w_gu_{n}", [P, E, 2 * P], F32R) for n in ("high", "low")]
                w_down = [tensor(mixture, f"w_down_{n}", [P, E, D], F32R) for n in ("high", "low")]
                with ExitStack() as whole:
                    gu, down = tensor(whole, "w_gu", [P, E, 2 * P]), tensor(whole, "w_down", [P, E, D])
                    pieces = [tuple(w[:, e:e + E // 2, :] for w in (gu, *w_gu)) + (s_w0, 32) for e in (0, E // 2)]
                    pieces += [(down[:], w_down[0][:], w_down[1][:], s_w0, 32)]
                    phase_gating(k, 0, "L0_ffn_gate_wT", (ALU.max, 1e-12),
                                 [(gu[:], ins["L0_ffn_gu"], s_w0), (down[:], ins["L0_ffn_down"], s_w0)], pieces)
                phase_experts0(k, w_gu, w_down)
            part = tensor(attn, "part", [P, PART_SLOTS, 2, 3, S], BF16)
            s_split, s_store, s_begin, s_slot = k.sem("split"), k.sems("store", "0 1 2"), k.sem("begin"), k.sems("slot", "0 1 2 3")
            phase_qkv(k, V, part, (q_dram, k_dram), bufs, s_split, s_store, s_begin)
            C = k.HT[:].rearrange("p (t d) -> p t d", d=D)
            phase_attention(k, V, C, part, (q_dram, k_dram), bufs, s_store, s_begin, s_slot)
        w1 = [k.sb(f"w1_{n}", [P, E, F1], F32R) for n in ("high", "low")]
        w2 = [k.sb(f"w2_{n}", [P, E, FC, D], F32R) for n in ("high", "low")]
        b2 = [k.sb(f"b2_{n}", [2 * E, D], F32R) for n in ("high", "low")]
        b1 = k.sb("b1", [P, E, FC])
        with ExitStack() as whole:
            up, down, bias = tensor(whole, "w1", [P, E, F1]), tensor(whole, "w2", [P, E, FC, D]), tensor(whole, "b2", [2 * E, D])
            b2_src = ins["L1_ffn_b2"]
            loads = [(up[:], ins["L1_ffn_W1"].rearrange("e d f -> d e f"), s_w1[0]), (b1[:], ins["L1_ffn_b1"], s_w1[0]),
                     (down[:], ins["L1_ffn_W2"].rearrange("e (c f) d -> f e c d", f=P), s_w1[1]),
                     (bias[0:E, :], b2_src, s_w1[1]), (bias[E:2 * E, :], b2_src, s_w1[1])]
            pieces = [tuple(w[:, e:e + 2, :] for w in (up, *w1)) + (s_w1[0], 32) for e in range(0, E, 2)]
            pieces += [tuple(w[:, e:e + 2] for w in (down, *w2)) + (s_w1[1], 48) for e in range(0, E, 2)]
            pieces += [(bias[:], b2[0][:], b2[1][:], s_w1[1], 48)]
            phase_project(k, C, loads)
            phase_gating(k, 1, "L1_ffn_Wg", (ALU.add, 1e-9), [], pieces)
        phase_experts1(k, w1, b1, w2, b2)


def kernel(**inputs):
    import numpy as np
    import concourse.bacc as bacc
    from concourse.bass_utils import run_bass_kernel_spmd

    a = {n: np.asarray(v) for n, v in inputs.items()}
    consts = np.concatenate([np.eye(P), np.kron(np.eye(H), np.ones((DH, DH))), np.tile(np.arange(E, 0, -1), (P, 1)),
                             np.tile(np.eye(E).reshape(1, -1), (P, 1))], axis=1).astype(np.float32)
    same = ["L0_attn_x", "L0_attn_Wq", "L0_attn_Wk", "L0_attn_Wv", "L0_attn_Wo", "L0_attn_bq", "L0_attn_bk", "L0_attn_bv", "L0_attn_bo",
            "L0_attn_m", "L0_ffn_similarity_matrix", "L0_wmod", "L1_attn_q_b", "L1_attn_k_b", "L1_attn_v_b", "L1_attn_out_b",
            "L1_ffn_Wg", "L1_ffn_W1", "L1_ffn_W2", "L1_ffn_b2", "L1_wmod"]
    laid = {n: a[n] for n in same} | {"consts": consts}
    laid |= {f"L1_attn_{n}_wT": a[f"L1_attn_{n}_w"].T for n in ("q", "k", "v", "out")}
    laid |= {f"L{i}_cT": a[f"L{i}_c"].T for i in range(2)}
    laid["L0_ffn_gate_wT"] = a["L0_ffn_gate_weight"].T
    laid["L0_ffn_gu"] = a["L0_ffn_gate_up_proj"].transpose(2, 0, 1)
    laid["L0_ffn_down"] = a["L0_ffn_down_proj"].transpose(2, 0, 1)
    laid["L1_ffn_b1"] = a["L1_ffn_b1"].reshape(E, FC, P).transpose(2, 0, 1)

    nc = bacc.Bacc("TRN2", target_bir_lowering=False, num_devices=1)
    arrays, aps = {}, {}
    for n, v in laid.items():
        arrays[f"in_{n}"] = np.ascontiguousarray(v)
        aps[n] = nc.dram_tensor(f"in_{n}", arrays[f"in_{n}"].shape, F32, kind="ExternalInput").ap()
    out = nc.dram_tensor("out", [B, S, D], F32, kind="ExternalOutput").ap()
    build(nc, aps, out)
    r = run_bass_kernel_spmd(nc, [arrays], core_ids=[0])
    return r.results[0]["out"]
```
